# Optimizing a Trainium2 kernel written in Bass

```python
import numpy as np
import jax
import jax.numpy as jnp

def _softmax(x, axis=-1):
    return jax.nn.softmax(x, axis=axis)

def _gelu(x):
    return jax.nn.gelu(x, approximate=True)

def _silu(x):
    return jax.nn.silu(x)

def _sigmoid(x):
    return jax.nn.sigmoid(x)

def _layernorm(x, axis=-1, eps=1e-05):
    m = jnp.mean(x, axis=axis, keepdims=True)
    v = jnp.var(x, axis=axis, keepdims=True)
    return (x - m) / jnp.sqrt(v + eps)

def _scatter_add(tgt, idx, src, axis=0):
    return tgt.at[idx].add(src)

def _segment_sum(src, seg, n):
    return jax.ops.segment_sum(src, seg, n)
kernel_name = 'mk_gnn_resnorm_d4_gnn_r64_6bea2e'

def setup_inputs(seed: int=0):
    np.random.seed(seed)
    _w = jnp.asarray

    def _rec_inputs():
        import jax
        import jax.numpy as jnp
        _gk = jax.random.key(seed)
        x = -8.776e-05 + 1 * jax.random.normal(jax.random.fold_in(_gk, 1), (625, 128), jnp.float32)
        _s = jax.random.randint(jax.random.fold_in(_gk, 2), (10000,), 0, 625, jnp.int32)
        _d = jax.random.randint(jax.random.fold_in(_gk, 3), (10000,), 0, 625, jnp.int32)
        _loop = jnp.arange(625, dtype=jnp.int32)
        src = jnp.concatenate([_s, _d, _loop])
        dst = jnp.concatenate([_d, _s, _loop])
        _o = jnp.argsort(dst, stable=True)
        src = src[_o]
        dst = dst[_o]
        return (x, src, dst)
    x, src, dst = _rec_inputs()

    def _L0_gnn_setup():
        import jax, jax.numpy as jnp
        import numpy as np
        N, E, F_IN, F_HID, F_OUT = (625, 10000, 128, 128, 128)

        def _sage_pool_layer(x, src, dst, Wp, bp, Ws, Wn, b):
            h_pool = jax.nn.relu(x @ Wp.T + bp)
            msg = jnp.take(h_pool, src, axis=0)
            agg = jax.ops.segment_max(msg, dst, num_segments=N)
            deg = jax.ops.segment_sum(jnp.ones((src.shape[0],), x.dtype), dst, num_segments=N)
            h_neigh = jnp.where(deg[:, None] > 0, agg, jnp.zeros_like(agg))
            return x @ Ws.T + h_neigh @ Wn.T + b
        key = jax.random.key(seed)
        ks = jax.random.split(key, 16)
        p = lambda k, shape: jax.random.normal(k, shape, jnp.float32) * 0.05
        inputs = jax.random.normal(ks[0], (N, F_IN), jnp.float32)
        src = jax.random.randint(ks[1], (E,), 0, N)
        dst = jax.random.randint(ks[2], (E,), 0, N)
        return {'inputs': inputs, 'src': src, 'dst': dst, 'Wp1': p(ks[3], (F_IN, F_IN)), 'bp1': p(ks[4], (F_IN,)), 'Ws1': p(ks[5], (F_HID, F_IN)), 'Wn1': p(ks[6], (F_HID, F_IN)), 'b1': p(ks[7], (F_HID,)), 'Wp2': p(ks[8], (F_HID, F_HID)), 'bp2': p(ks[9], (F_HID,)), 'Ws2': p(ks[10], (F_OUT, F_HID)), 'Wn2': p(ks[11], (F_OUT, F_HID)), 'b2': p(ks[12], (F_OUT,))}
    _L0_gnn_all = _L0_gnn_setup()
    _L0_gnn_in = {k: v for k, v in _L0_gnn_all.items() if k in ('Wp1', 'bp1', 'Ws1', 'Wn1', 'b1', 'Wp2', 'bp2', 'Ws2', 'Wn2', 'b2')}
    del _L0_gnn_all

    def _L1_gnn_setup():
        import jax, jax.numpy as jnp
        import numpy as np
        N_NODES = 10000
        key = jax.random.key(seed)
        k1, k2 = jax.random.split(key)
        x = jax.random.normal(k1, (N_NODES, 128), dtype=jnp.float32)
        edge_index = jax.random.randint(k2, (2, 10000), 0, N_NODES, dtype=jnp.int64)
        return {'x': x, 'edge_index': edge_index}
    _L1_gnn_all = _L1_gnn_setup()
    _L1_gnn_in = {k: v for k, v in _L1_gnn_all.items() if k in ()}
    del _L1_gnn_all

    def _L2_gnn_setup():
        import jax, jax.numpy as jnp
        import numpy as np
        NEG_SLOPE = 0.2
        N_NODES, IN_DIM, HID, HEADS, OUT = (50000, 128, 64, 4, 128)
        N_EDGES = 12500

        def gat_conv(x, src, dst, num_nodes, W, a_src, a_dst, bias, concat):
            H, C = a_src.shape
            xp = (x @ W).reshape(num_nodes, H, C)
            s = jnp.einsum('nhc,hc->nh', xp, a_src)
            d = jnp.einsum('nhc,hc->nh', xp, a_dst)
            e = s[src] + d[dst]
            e = jnp.where(e > 0, e, NEG_SLOPE * e)
            m = jax.ops.segment_max(e, dst, num_segments=num_nodes)
            p = jnp.exp(e - m[dst])
            z = jax.ops.segment_sum(p, dst, num_segments=num_nodes)
            alpha = p / (z[dst] + 1e-16)
            out = jax.ops.segment_sum(xp[src] * alpha[:, :, None], dst, num_segments=num_nodes)
            out = out.reshape(num_nodes, H * C) if concat else out.mean(axis=1)
            return out + bias
        key = jax.random.key(seed)
        ks = jax.random.split(key, 16)
        HC = HEADS * HID
        inp = {'x': jax.random.normal(ks[0], (N_NODES, IN_DIM), dtype=jnp.float32), 'edge_index': jax.random.randint(ks[1], (2, N_EDGES), 0, N_NODES, dtype=jnp.int32), 'W0': jax.random.normal(ks[2], (IN_DIM, HC), dtype=jnp.float32) * 0.08, 'a_src0': jax.random.normal(ks[3], (HEADS, HID), dtype=jnp.float32) * 0.1, 'a_dst0': jax.random.normal(ks[4], (HEADS, HID), dtype=jnp.float32) * 0.1, 'b0': jnp.zeros((HC,), dtype=jnp.float32), 'W1': jax.random.normal(ks[5], (HC, HC), dtype=jnp.float32) * 0.06, 'a_src1': jax.random.normal(ks[6], (HEADS, HID), dtype=jnp.float32) * 0.1, 'a_dst1': jax.random.normal(ks[7], (HEADS, HID), dtype=jnp.float32) * 0.1, 'b1': jnp.zeros((HC,), dtype=jnp.float32), 'W2': jax.random.normal(ks[8], (HC, OUT), dtype=jnp.float32) * 0.06, 'a_src2': jax.random.normal(ks[9], (1, OUT), dtype=jnp.float32) * 0.1, 'a_dst2': jax.random.normal(ks[10], (1, OUT), dtype=jnp.float32) * 0.1, 'b2': jnp.zeros((OUT,), dtype=jnp.float32)}
        return inp
    _L2_gnn_all = _L2_gnn_setup()
    _L2_gnn_in = {k: v for k, v in _L2_gnn_all.items() if k in ('W0', 'a_src0', 'a_dst0', 'b0', 'W1', 'a_src1', 'a_dst1', 'b1', 'W2', 'a_src2', 'a_dst2', 'b2')}
    del _L2_gnn_all

    def _L3_gnn_setup():
        import jax, jax.numpy as jnp
        import numpy as np
        TOPK = 2
        key = jax.random.key(seed)
        ks = jax.random.split(key, 18)
        N, E = (20000, 5000)
        IN, H, OUT, L = (128, 256, 128, 3)
        NW, NS = (4, 4)
        NE = NW + NS

        def w(k, shape, fan):
            return jax.random.normal(k, shape, dtype=jnp.float32) / np.float32(np.sqrt(fan))
        inp = {'x': jax.random.normal(ks[0], (N, IN), dtype=jnp.float32), 'edge_index': jax.random.randint(ks[1], (2, E), 0, N, dtype=jnp.int64), 'W_in': w(ks[2], (IN, H), IN), 'b_in': jnp.zeros((H,), jnp.float32), 'router_W': w(ks[3], (L, 2 * H, NE), 2 * H), 'router_b': jnp.zeros((L, NE), jnp.float32), 'weak_W': w(ks[4], (L, NW, H, H), H), 'weak_b': jnp.zeros((L, NW, H), jnp.float32), 'strong_W1': w(ks[5], (L, NS, H, 2 * H), H), 'strong_b1': jnp.zeros((L, NS, 2 * H), jnp.float32), 'strong_W2': w(ks[6], (L, NS, 2 * H, H), 2 * H), 'strong_b2': jnp.zeros((L, NS, H), jnp.float32), 'conf_W': w(ks[7], (L, H, 1), H), 'conf_b': jnp.zeros((L, 1), jnp.float32), 'W_out': w(ks[8], (H, OUT), H), 'b_out': jnp.zeros((OUT,), jnp.float32)}
        return inp
    _L3_gnn_all = _L3_gnn_setup()
    _L3_gnn_in = {k: v for k, v in _L3_gnn_all.items() if k in ('W_in', 'b_in', 'router_W', 'router_b', 'weak_W', 'weak_b', 'strong_W1', 'strong_b1', 'strong_W2', 'strong_b2', 'conf_W', 'conf_b', 'W_out', 'b_out')}
    del _L3_gnn_all
    return {'x': x, 'src': src, 'dst': dst, 'L0_gnn_Wp1': _L0_gnn_in['Wp1'], 'L0_gnn_bp1': _L0_gnn_in['bp1'], 'L0_gnn_Ws1': _L0_gnn_in['Ws1'], 'L0_gnn_Wn1': _L0_gnn_in['Wn1'], 'L0_gnn_b1': _L0_gnn_in['b1'], 'L0_gnn_Wp2': _L0_gnn_in['Wp2'], 'L0_gnn_bp2': _L0_gnn_in['bp2'], 'L0_gnn_Ws2': _L0_gnn_in['Ws2'], 'L0_gnn_Wn2': _L0_gnn_in['Wn2'], 'L0_gnn_b2': _L0_gnn_in['b2'], 'L2_gnn_W0': _L2_gnn_in['W0'], 'L2_gnn_a_src0': _L2_gnn_in['a_src0'], 'L2_gnn_a_dst0': _L2_gnn_in['a_dst0'], 'L2_gnn_b0': _L2_gnn_in['b0'], 'L2_gnn_W1': _L2_gnn_in['W1'], 'L2_gnn_a_src1': _L2_gnn_in['a_src1'], 'L2_gnn_a_dst1': _L2_gnn_in['a_dst1'], 'L2_gnn_b1': _L2_gnn_in['b1'], 'L2_gnn_W2': _L2_gnn_in['W2'], 'L2_gnn_a_src2': _L2_gnn_in['a_src2'], 'L2_gnn_a_dst2': _L2_gnn_in['a_dst2'], 'L2_gnn_b2': _L2_gnn_in['b2'], 'L3_gnn_W_in': _L3_gnn_in['W_in'], 'L3_gnn_b_in': _L3_gnn_in['b_in'], 'L3_gnn_router_W': _L3_gnn_in['router_W'], 'L3_gnn_router_b': _L3_gnn_in['router_b'], 'L3_gnn_weak_W': _L3_gnn_in['weak_W'], 'L3_gnn_weak_b': _L3_gnn_in['weak_b'], 'L3_gnn_strong_W1': _L3_gnn_in['strong_W1'], 'L3_gnn_strong_b1': _L3_gnn_in['strong_b1'], 'L3_gnn_strong_W2': _L3_gnn_in['strong_W2'], 'L3_gnn_strong_b2': _L3_gnn_in['strong_b2'], 'L3_gnn_conf_W': _L3_gnn_in['conf_W'], 'L3_gnn_conf_b': _L3_gnn_in['conf_b'], 'L3_gnn_W_out': _L3_gnn_in['W_out'], 'L3_gnn_b_out': _L3_gnn_in['b_out']}

def reference(x, src, dst, L0_gnn_Wp1, L0_gnn_bp1, L0_gnn_Ws1, L0_gnn_Wn1, L0_gnn_b1, L0_gnn_Wp2, L0_gnn_bp2, L0_gnn_Ws2, L0_gnn_Wn2, L0_gnn_b2, L2_gnn_W0, L2_gnn_a_src0, L2_gnn_a_dst0, L2_gnn_b0, L2_gnn_W1, L2_gnn_a_src1, L2_gnn_a_dst1, L2_gnn_b1, L2_gnn_W2, L2_gnn_a_src2, L2_gnn_a_dst2, L2_gnn_b2, L3_gnn_W_in, L3_gnn_b_in, L3_gnn_router_W, L3_gnn_router_b, L3_gnn_weak_W, L3_gnn_weak_b, L3_gnn_strong_W1, L3_gnn_strong_b1, L3_gnn_strong_W2, L3_gnn_strong_b2, L3_gnn_conf_W, L3_gnn_conf_b, L3_gnn_W_out, L3_gnn_b_out):
    import jax
    import jax.numpy as jnp

    def _L0_gnn_ref(inputs, src, dst, Wp1, bp1, Ws1, Wn1, b1, Wp2, bp2, Ws2, Wn2, b2):
        import jax, jax.numpy as jnp
        import numpy as np
        N, E, F_IN, F_HID, F_OUT = (625, 10000, 128, 128, 128)

        def _sage_pool_layer(x, src, dst, Wp, bp, Ws, Wn, b):
            h_pool = jax.nn.relu(x @ Wp.T + bp)
            msg = jnp.take(h_pool, src, axis=0)
            agg = jax.ops.segment_max(msg, dst, num_segments=N)
            deg = jax.ops.segment_sum(jnp.ones((src.shape[0],), x.dtype), dst, num_segments=N)
            h_neigh = jnp.where(deg[:, None] > 0, agg, jnp.zeros_like(agg))
            return x @ Ws.T + h_neigh @ Wn.T + b
        h = _sage_pool_layer(inputs, src, dst, Wp1, bp1, Ws1, Wn1, b1)
        h = jax.nn.relu(h)
        h = _sage_pool_layer(h, src, dst, Wp2, bp2, Ws2, Wn2, b2)
        return h

    def _L1_gnn_ref(x, edge_index):
        import jax, jax.numpy as jnp
        import numpy as np
        N_NODES = 10000
        row, col = (edge_index[0], edge_index[1])
        msgs = x[col]
        h = jax.ops.segment_sum(msgs, row, num_segments=x.shape[0])
        return h

    def _L2_gnn_ref(x, edge_index, W0, a_src0, a_dst0, b0, W1, a_src1, a_dst1, b1, W2, a_src2, a_dst2, b2):
        import jax, jax.numpy as jnp
        import numpy as np
        NEG_SLOPE = 0.2
        N_NODES, IN_DIM, HID, HEADS, OUT = (50000, 128, 64, 4, 128)
        N_EDGES = 12500

        def gat_conv(x, src, dst, num_nodes, W, a_src, a_dst, bias, concat):
            H, C = a_src.shape
            xp = (x @ W).reshape(num_nodes, H, C)
            s = jnp.einsum('nhc,hc->nh', xp, a_src)
            d = jnp.einsum('nhc,hc->nh', xp, a_dst)
            e = s[src] + d[dst]
            e = jnp.where(e > 0, e, NEG_SLOPE * e)
            m = jax.ops.segment_max(e, dst, num_segments=num_nodes)
            p = jnp.exp(e - m[dst])
            z = jax.ops.segment_sum(p, dst, num_segments=num_nodes)
            alpha = p / (z[dst] + 1e-16)
            out = jax.ops.segment_sum(xp[src] * alpha[:, :, None], dst, num_segments=num_nodes)
            out = out.reshape(num_nodes, H * C) if concat else out.mean(axis=1)
            return out + bias
        N = x.shape[0]
        loops = jnp.arange(N, dtype=edge_index.dtype)
        src = jnp.concatenate([edge_index[0], loops])
        dst = jnp.concatenate([edge_index[1], loops])
        h = gat_conv(x, src, dst, N, W0, a_src0, a_dst0, b0, True)
        h = jax.nn.elu(h)
        h = gat_conv(h, src, dst, N, W1, a_src1, a_dst1, b1, True)
        h = jax.nn.elu(h)
        h = gat_conv(h, src, dst, N, W2, a_src2, a_dst2, b2, False)
        return h

    def _L3_gnn_ref(x, edge_index, W_in, b_in, router_W, router_b, weak_W, weak_b, strong_W1, strong_b1, strong_W2, strong_b2, conf_W, conf_b, W_out, b_out):
        import jax, jax.numpy as jnp
        import numpy as np
        TOPK = 2
        N = x.shape[0]
        L = router_W.shape[0]
        src = edge_index[0]
        dst = edge_index[1]
        deg = jax.ops.segment_sum(jnp.ones(src.shape, x.dtype), dst, num_segments=N)
        deg = jnp.clip(deg, 1.0)[:, None]
        h = x @ W_in + b_in
        rows = jnp.arange(N)[:, None]
        for l in range(L):
            agg = jax.ops.segment_sum(h[src], dst, num_segments=N) / deg
            logits = jnp.concatenate([h, agg], axis=-1) @ router_W[l] + router_b[l]
            vals, idx = jax.lax.top_k(logits, TOPK)
            gates = jax.nn.softmax(vals, axis=-1)
            gate_dense = jnp.zeros_like(logits).at[rows, idx].set(gates)
            weak = jax.nn.relu(jnp.einsum('nh,ehf->nef', agg, weak_W[l]) + weak_b[l])
            sh = jax.nn.relu(jnp.einsum('nh,ehf->nef', agg, strong_W1[l]) + strong_b1[l])
            strong = jnp.einsum('nef,efh->neh', sh, strong_W2[l]) + strong_b2[l]
            experts = jnp.concatenate([weak, strong], axis=1)
            moe = jnp.einsum('ne,neh->nh', gate_dense, experts)
            conf = jax.nn.sigmoid(h @ conf_W[l] + conf_b[l])
            h = h + conf * moe
        return h @ W_out + b_out
    edge_index = jnp.stack([src, dst])
    x = _layernorm(x + _L0_gnn_ref(x, src, dst, L0_gnn_Wp1, L0_gnn_bp1, L0_gnn_Ws1, L0_gnn_Wn1, L0_gnn_b1, L0_gnn_Wp2, L0_gnn_bp2, L0_gnn_Ws2, L0_gnn_Wn2, L0_gnn_b2), axis=-1)
    x = _layernorm(x + _L1_gnn_ref(x, edge_index), axis=-1)
    x = _layernorm(x + _L2_gnn_ref(x, edge_index, L2_gnn_W0, L2_gnn_a_src0, L2_gnn_a_dst0, L2_gnn_b0, L2_gnn_W1, L2_gnn_a_src1, L2_gnn_a_dst1, L2_gnn_b1, L2_gnn_W2, L2_gnn_a_src2, L2_gnn_a_dst2, L2_gnn_b2), axis=-1)
    x = _layernorm(x + _L3_gnn_ref(x, edge_index, L3_gnn_W_in, L3_gnn_b_in, L3_gnn_router_W, L3_gnn_router_b, L3_gnn_weak_W, L3_gnn_weak_b, L3_gnn_strong_W1, L3_gnn_strong_b1, L3_gnn_strong_W2, L3_gnn_strong_b2, L3_gnn_conf_W, L3_gnn_conf_b, L3_gnn_W_out, L3_gnn_b_out), axis=-1)
    return x

_drawn_inputs = setup_inputs


def setup_inputs(seed=0):
    import zlib

    import numpy as np

    out = dict(_drawn_inputs(seed))
    spreads = {'L2_gnn_b0': (0.0, 0.1),
     'L2_gnn_b1': (0.0, 0.1),
     'L2_gnn_b2': (0.0, 0.1),
     'L3_gnn_b_in': (0.0, 0.1),
     'L3_gnn_router_b': (0.0, 0.1),
     'L3_gnn_weak_b': (0.0, 0.527),
     'L3_gnn_strong_b1': (0.0, 0.1),
     'L3_gnn_strong_b2': (0.0, 0.1),
     'L3_gnn_conf_b': (0.0, 0.8),
     'L3_gnn_b_out': (0.0, 0.1)}
    factors = {'L2_gnn_a_src0': 3.022,
     'L2_gnn_a_dst0': 12.706,
     'L2_gnn_a_src1': 35.324,
     'L2_gnn_a_dst1': 64.0,
     'L2_gnn_a_src2': 64.0,
     'L2_gnn_a_dst2': 64.0}
    for name, (base, spread) in spreads.items():
        noise = np.random.default_rng([zlib.crc32(name.encode()), seed]).standard_normal(out[name].shape)
        drawn = base * np.exp(spread * noise) if base else spread * noise
        out[name] = jnp.asarray(drawn.astype(out[name].dtype))
    for name, factor in factors.items():
        out[name] = (out[name] * factor).astype(out[name].dtype)
    return out
```

```python
from contextlib import ExitStack

import concourse.bass as bass
from concourse import mybir

N = 625
P = 125
T = N // P
E = 20625
CHUNKS = E // P
D = 128
FULL = 128
WIDE = 4 * P
EDGE = 512 - WIDE
HEADS = 4
HID = 256
LAYERS = 3
NEXP = 8
NW = 4
NS = 4
FF = 512
NEG_SLOPE = 0.2
BIG = 1.0e30
EPS = 1e-5

ALU = mybir.AluOpType
ACT = mybir.ActivationFunctionType
AX = mybir.AxisListType
F32 = mybir.dt.float32
BF16 = mybir.dt.bfloat16
F16 = mybir.dt.float16
I32 = mybir.dt.int32
ds = bass.ds

ROWS = ((0, WIDE), (WIDE, N))


class Chain:

    def __init__(self, eng, sem):
        self.eng, self.sem, self.done, self.loop = eng, sem, 0, 0

    def link(self, ins):
        self.done += 1
        ins.then_inc(self.sem, 1)
        self.eng.wait_ge(self.sem, self.loop + self.done)

    def enter(self, i, per_turn):
        self.start, self.per_turn = self.done, per_turn
        self.loop = i * per_turn

    def leave(self, turns):
        assert self.done - self.start == self.per_turn, self.done - self.start
        self.loop = 0
        self.done = self.start + turns * self.per_turn


class Program:
    pass


def build(nc, a, out):
    g = Program()
    g.a, g.out = a, out
    with ExitStack() as ctx:
        def sb(name, shape, dt=F32):
            return ctx.enter_context(nc.sbuf_tensor(name, shape, dt))

        def sem(name):
            return ctx.enter_context(nc.semaphore(name))

        g.psum = ctx.enter_context(nc.psum_tensor("psum", [FULL, 8 * 512], F32))

        def wide(b):
            return g.psum[:, b * 512 + EDGE:b * 512 + EDGE + N]

        def bank(b):
            return g.psum[:, b * 512:(b + 1) * 512]

        g.ident = sb("ident", [FULL, FULL])
        g.ident_bf = sb("ident_bf", [FULL, FULL], BF16)
        g.ones = sb("ones", [FULL, FULL])
        g.count = sb("count", [P, T, N])
        g.count_t = sb("count_t", [P, T, N])
        g.has_edge_t = sb("has_edge_t", [P, T, N], BF16)
        g.count_loop = sb("count_loop", [P, T, N])
        g.no_edge_t = sb("no_edge_t", [P, T, N], BF16)
        g.recip_deg = sb("recip_deg", [P, T])
        g.xa = sb("xa", [P, T, D])
        g.xb = sb("xb", [P, T, D])
        g.res = sb("res", [P, T, D])
        g.x_t = sb("x_t", [FULL, 2, N])
        g.ln_stats = sb("ln_stats", [P, T, 6])
        g.ln_mv = sb("ln_mv", [P, T, 2])
        g.ln_var = sb("ln_var", [P, T])
        g.ln_std = sb("ln_std", [P, T])
        g.ln_rstd = sb("ln_rstd", [P, T])

        g.w_sage = sb("w_sage", [FULL, 6, D])
        g.b_sage = sb("b_sage", [FULL, 3])
        g.b_sage2 = sb("b_sage2", [1, D])
        g.w_gat0 = sb("w_gat0", [FULL, 1, HID])
        g.w_gat1 = sb("w_gat1", [FULL, 2, HID])
        g.w_gat2 = sb("w_gat2", [FULL, 2, D])
        g.att = [sb(f"att{i}", [P, 2, HID if i < 2 else D]) for i in range(3)]
        g.b_gat = [sb(f"b_gat{i}", [P, HID if i < 2 else D]) for i in range(3)]
        g.w_in = sb("w_in", [FULL, HID])
        g.b_in = sb("b_in", [1, HID])
        g.w_router = sb("w_router", [FULL, LAYERS, 4, NEXP + 1])
        g.b_router = sb("b_router", [1, LAYERS, NEXP + 1])
        g.w_weak = sb("w_weak", [FULL, 2, NW, HID])
        g.b_weak = sb("b_weak", [P, LAYERS, NW * HID])
        g.w_strong1 = sb("w_strong1", [FULL, NS, 2, FF])
        g.b_strong1 = sb("b_strong1", [FULL, LAYERS, NS, 4])
        g.w_strong2 = sb("w_strong2", [FULL, NS, 4, HID])
        g.b_strong2 = sb("b_strong2", [NEXP, LAYERS, HID])
        g.w_out = sb("w_out", [FULL, 2, D])
        g.b_out = sb("b_out", [1, D])

        g.edges_loaded = sem("edges_loaded")
        g.x_loaded = sem("x_loaded")
        g.sage_loaded = sem("sage_loaded")
        g.gat_loaded = sem("gat_loaded")
        g.moe_loaded = sem("moe_loaded")
        g.weak_loaded = sem("weak_loaded")
        g.strong_loaded = [sem(f"strong{e}_loaded") for e in range(NS)]
        g.consts_ready = sem("consts_ready")
        g.dve_chain = sem("dve_chain")
        g.ln_var_ready = sem("ln_var_ready")
        g.ln_std_ready = sem("ln_std_ready")

        def layernorm_vector(chain, r, y, k):
            for t in range(T):
                last = nc.vector.bn_stats(g.ln_stats[:, t, :], r[:, t, :])
            chain.link(last)
            for t in range(T):
                last = nc.vector.bn_aggr(g.ln_mv[:, t, :], g.ln_stats[:, t, :])
            chain.link(last)
            nc.vector.tensor_scalar(g.ln_var[:, :], g.ln_mv[:, :, 1], EPS, None, ALU.add).then_inc(g.ln_var_ready, 1)
            nc.vector.wait_ge(g.ln_std_ready, k)
            chain.link(nc.vector.reciprocal(g.ln_rstd[:, :], g.ln_std[:, :]))
            for t in range(T):
                last = nc.vector.tensor_scalar(y[:, t, :], r[:, t, :], g.ln_mv[:, t, 0:1], g.ln_rstd[:, t:t + 1],
                                               ALU.subtract, ALU.mult)
            return last

        def layernorm_scalar(k):
            nc.scalar.wait_ge(g.ln_var_ready, k)
            nc.scalar.activation(g.ln_std[:, :], g.ln_var[:, :], ACT.Sqrt).then_inc(g.ln_std_ready, 1)

        g.wide, g.bank = wide, bank
        g.layernorm_vector, g.layernorm_scalar = layernorm_vector, layernorm_scalar
        adjacency(nc, g)
        sage(nc, g)
        propagate(nc, g)
        gat(nc, g)
        moe(nc, g)


def adjacency(nc, g):
    a = g.a
    TURN = 5
    TURNS = CHUNKS // TURN
    assert TURNS * TURN == CHUNKS
    with ExitStack() as ctx:
        def sb(name, shape, dt=F32):
            return ctx.enter_context(nc.sbuf_tensor(name, shape, dt))

        def sem(name):
            return ctx.enter_context(nc.semaphore(name))

        ends_i = sb("ends_i", [P, 2, CHUNKS], I32)
        ends = sb("ends", [P, 2, CHUNKS])
        node_i = sb("node_i", [P, N], I32)
        node = sb("node", [P, N], F16)
        onehot = sb("onehot", [P, TURN, 2, N], BF16)
        nodes_ready = sem("nodes_ready")
        onehot_ready = sem("onehot_ready")
        onehot_used = sem("onehot_used")
        counts_ready = sem("counts_ready")
        counts_copied_v = sem("counts_copied_v")
        counts_copied_s = sem("counts_copied_s")
        turned = sem("turned")
        turned_copied_v = sem("turned_copied_v")
        turned_copied_s = sem("turned_copied_s")
        ident_zero = sem("ident_zero")
        pool_chain = sem("pool_chain")
        psum = g.psum

        def row_main(t):
            return psum[0:P, t * 512 + EDGE:(t + 1) * 512]

        def row_rest(t):
            b, k = (5, t) if t < 4 else (6, 0)
            return psum[0:P, b * 512 + EDGE + P * k:b * 512 + EDGE + P * (k + 1)]

        with nc.Block() as block:
            @block.sync
            def _(sp):
                for i, name in enumerate(("src", "dst")):
                    sp.dma_start(ends_i[:, i, :], a[name].rearrange("(p c) -> p c", c=CHUNKS)).then_inc(g.edges_loaded, 16)
                sp.dma_start(g.xa[:, :, :], a["x"].rearrange("(t p) f -> p t f", p=P)).then_inc(g.x_loaded, 16)
                for i, name in enumerate(("Wp1", "Ws1", "Wn1", "Wp2", "Ws2", "Wn2")):
                    sp.dma_start(g.w_sage[:, i, :], a["L0_gnn_" + name]).then_inc(g.sage_loaded, 16)
                for i, name in enumerate(("bp1", "b1", "bp2")):
                    sp.dma_start(g.b_sage[:, i:i + 1], a["L0_gnn_" + name].rearrange("(p o) -> p o", o=1)).then_inc(g.sage_loaded, 16)
                sp.dma_start(g.b_sage2[:, :], a["L0_gnn_b2"].rearrange("(o f) -> o f", o=1)).then_inc(g.sage_loaded, 16)
                for i, w in enumerate((g.w_gat0, g.w_gat1, g.w_gat2)):
                    sp.dma_start(w[:, :, :], a[f"L2_gnn_W{i}"].rearrange("(k p) f -> p k f", p=FULL)).then_inc(g.gat_loaded, 16)
                    for j, side in enumerate(("src", "dst")):
                        vec = a[f"L2_gnn_a_{side}{i}"].rearrange("h c -> (h c)")
                        sp.dma_start(g.att[i][:, j, :], vec.partition_broadcast(P)).then_inc(g.gat_loaded, 16)
                    sp.dma_start(g.b_gat[i][:, :], a[f"L2_gnn_b{i}"].partition_broadcast(P)).then_inc(g.gat_loaded, 16)

            @block.gpsimd
            def _(pool):
                pool.iota(node_i[:, :], pattern=[[1, N]], base=0, channel_multiplier=0).then_inc(nodes_ready, 1)
                pool.memset(g.ident[:, :], 0.0).then_inc(ident_zero, 1)
                pool.memset(g.ones[:, :], 1.0).then_inc(g.consts_ready, 1)
                pool.wait_ge(ident_zero, 1)
                pool.affine_select(out=g.ident[:, :], in_=g.ident[:, :], compare_op=ALU.not_equal, fill=1.0,
                                   base=0, pattern=[[-1, FULL]], channel_multiplier=1).then_inc(g.consts_ready, 1)
                pool.wait_ge(g.consts_ready, 2)
                pool.tensor_copy(g.ident_bf[:, :], g.ident[:, :]).then_inc(g.consts_ready, 1)
                pool.memset(g.w_router[:, :, :, :], 0.0).then_inc(g.consts_ready, 1)
                pool.memset(g.b_strong2[:, :, :], 0.0).then_inc(g.consts_ready, 1)
                pool.wait_ge(g.consts_ready, 5)
                with nc.allow_non_contiguous_dma(reason="small weights, once"):
                    for l in range(LAYERS):
                        pool.dma_start(g.w_router[:, l, :, 0:NEXP], a["L3_gnn_router_W"][l].rearrange("(k p) e -> p k e", p=FULL)).then_inc(g.moe_loaded, 16)
                        pool.dma_start(g.w_router[:, l, 0:2, NEXP:NEXP + 1], a["L3_gnn_conf_W"][l].rearrange("(k p) e -> p k e", p=FULL)).then_inc(g.moe_loaded, 16)
                        pool.dma_start(g.b_strong1[:, l, :, :], a["L3_gnn_strong_b1"][l].rearrange("e (k p) -> p e k", p=FULL)).then_inc(g.moe_loaded, 16)
                    pool.dma_start(g.b_router[:, :, 0:NEXP], a["L3_gnn_router_b"].rearrange("(o l) e -> o l e", o=1)).then_inc(g.moe_loaded, 16)
                    pool.dma_start(g.b_router[:, :, NEXP:NEXP + 1], a["L3_gnn_conf_b"].rearrange("(o l) e -> o l e", o=1)).then_inc(g.moe_loaded, 16)
                    pool.dma_start(g.b_strong2[NW:NEXP, :, :], a["L3_gnn_strong_b2"].rearrange("l e f -> e l f")).then_inc(g.moe_loaded, 16)
                    pool.dma_start(g.b_weak[:, :, :], a["L3_gnn_weak_b"].rearrange("l e f -> l (e f)").partition_broadcast(P)).then_inc(g.moe_loaded, 16)
                    pool.dma_start(g.w_in[:, :], a["L3_gnn_W_in"]).then_inc(g.moe_loaded, 16)
                    pool.dma_start(g.b_in[:, :], a["L3_gnn_b_in"].rearrange("(o f) -> o f", o=1)).then_inc(g.moe_loaded, 16)
                    pool.dma_start(g.w_out[:, :, :], a["L3_gnn_W_out"].rearrange("(k p) f -> p k f", p=FULL)).then_inc(g.moe_loaded, 16)
                    pool.dma_start(g.b_out[:, :], a["L3_gnn_b_out"].rearrange("(o f) -> o f", o=1)).then_inc(g.moe_loaded, 16)
                pool.wait_ge(counts_copied_v, 4)
                pool.wait_ge(counts_copied_s, 3)
                pool.tensor_copy(g.count_loop[:, :, :], g.count[:, :, :]).then_inc(pool_chain, 1)
                pool.wait_ge(pool_chain, 1)
                for t in range(T):
                    block_t = g.count_loop[:, t, t * P:(t + 1) * P]
                    last = pool.tensor_tensor(block_t, block_t, g.ident[0:P, 0:P], ALU.add)
                last.then_inc(pool_chain, 1)

            @block.scalar
            def _(act):
                act.wait_ge(counts_ready, 1)
                for t in range(3):
                    nc.scalar.copy(g.count[:, t, 0:WIDE], row_main(t)).then_inc(counts_copied_s, 1)
                act.wait_ge(turned, 1)
                for t in range(3):
                    nc.scalar.copy(g.count_t[:, t, 0:WIDE], row_main(t)).then_inc(turned_copied_s, 1)

            @block.tensor
            def _(pe):
                def chunk(k, ready, start, stop):
                    pe.wait_ge(onehot_ready, ready)
                    for s in range(T):
                        lhs = onehot[:, k, 0, s * P:(s + 1) * P]
                        nc.tensor.matmul(row_main(s), lhs, onehot[:, k, 1, 0:WIDE], start=start, stop=stop,
                                         skip_group_check=True)
                        last = nc.tensor.matmul(row_rest(s), lhs, onehot[:, k, 1, WIDE:N],
                                                start=start and s in (0, 4), stop=stop, skip_group_check=True)
                    return last

                for k in range(TURN):
                    chunk(k, k + 1, k == 0, False).then_inc(onehot_used, 1)
                with pe.Fori(1, TURNS - 1) as i:
                    for k in range(TURN):
                        chunk(k, i * TURN + k + 1, False, False).then_inc(onehot_used, 1)
                for k in range(TURN):
                    last = chunk(k, CHUNKS - TURN + k + 1, False, k == TURN - 1)
                last.then_inc(counts_ready, 1)
                pe.wait_ge(counts_copied_v, 4)
                pe.wait_ge(counts_copied_s, 3)
                pe.wait_ge(g.consts_ready, 2)
                for d in range(T):
                    for s in range(T):
                        to = row_main(d)[:, s * P:(s + 1) * P] if s < 4 else row_rest(d)
                        last = nc.tensor.transpose(to, g.count[:, s, d * P:(d + 1) * P], g.ident[0:P, 0:P])
                last.then_inc(turned, 1)

            @block.vector
            def _(dve):
                chain = Chain(dve, g.dve_chain)
                dve.wait_ge(nodes_ready, 1)
                nc.vector.tensor_copy(node[:, :], node_i[:, :])
                dve.wait_ge(g.edges_loaded, 32)
                chain.link(nc.vector.tensor_copy(ends[:, :, :], ends_i[:, :, :]))

                def chunk(k, c):
                    for side in range(2):
                        last = nc.vector.tensor_scalar(onehot[:, k, side, :], node[:, :], ends[:, side, ds(c, 1)],
                                                       None, ALU.is_equal)
                    last.then_inc(onehot_ready, 1)

                for k in range(TURN):
                    chunk(k, k)
                with dve.Fori(1, TURNS) as i:
                    for k in range(TURN):
                        dve.wait_ge(onehot_used, (i - 1) * TURN + k + 1)
                        chunk(k, i * TURN + k)
                dve.wait_ge(counts_ready, 1)
                rests = psum[0:P, 5 * 512 + EDGE:6 * 512].rearrange("p (t n) -> p t n", n=P)

                def copy_rows(to, copied):
                    for t in (3, 4):
                        nc.vector.tensor_copy(to[:, t, 0:WIDE], row_main(t)).then_inc(copied, 1)
                    nc.vector.tensor_copy(to[:, 0:4, WIDE:N], rests).then_inc(copied, 1)
                    nc.vector.tensor_copy(to[:, 4, WIDE:N], row_rest(4)).then_inc(copied, 1)

                copy_rows(g.count, counts_copied_v)
                dve.wait_ge(turned, 1)
                copy_rows(g.count_t, turned_copied_v)
                dve.wait_ge(turned_copied_v, 4)
                dve.wait_ge(turned_copied_s, 3)
                nc.vector.tensor_scalar(g.has_edge_t[:, :, :], g.count_t[:, :, :], 1.0, None, ALU.min)
                nc.vector.tensor_scalar(g.no_edge_t[:, :, :], g.count_t[:, :, :], 0.0, -BIG, ALU.is_le, ALU.mult)
                chain.link(nc.vector.tensor_reduce(g.recip_deg[:, :], g.count_t[:, :, :], AX.X, ALU.add))
                chain.link(nc.vector.tensor_scalar(g.recip_deg[:, :], g.recip_deg[:, :], 1.0, None, ALU.max))
                nc.vector.reciprocal(g.recip_deg[:, :], g.recip_deg[:, :])
                for t in range(T):
                    block_t = g.no_edge_t[:, t, t * P:(t + 1) * P]
                    last = nc.vector.scalar_tensor_tensor(block_t, g.ident[0:P, 0:P], 0.0, block_t, ALU.is_equal, ALU.mult)
                chain.link(last)
                g.dve_links = chain.done


def sage(nc, g):
    FIRST = 1
    BODY = 4
    TURNS = (P - FIRST) // BODY
    RING = 4
    with ExitStack() as ctx:
        def sb(name, shape, dt=F32):
            return ctx.enter_context(nc.sbuf_tensor(name, shape, dt))

        def sem(name):
            return ctx.enter_context(nc.semaphore(name))

        pool_t = sb("pool_t", [FULL, N])
        masked = sb("masked", [FULL, RING, N], BF16)
        staged = sb("staged", [FULL, T, BODY])
        agg_t = sb("agg_t", [FULL, T, P])
        turned = sem("sage_turned")
        x_t_ready = sem("sage_x_t_ready")
        pooled = sem("pooled")
        pool_ready = sem("pool_ready")
        row_ready = sem("row_ready")
        row_used = sem("row_used")
        row_seen = sem("row_seen")
        agg_ready = sem("agg_ready")
        summed = sem("sage_summed")
        psum = g.psum

        def row(k):
            return g.wide(2 * (k % RING))

        with nc.Block() as block:
            @block.sync
            def _(sp):
                w1 = g.a["L3_gnn_strong_W1"][0].rearrange("e (k p) f -> p e k f", p=FULL)
                w2 = g.a["L3_gnn_strong_W2"][0].rearrange("e (k p) f -> p e k f", p=FULL)
                for k in range(2):
                    sp.dma_start(g.w_weak[:, k, :, :], g.a["L3_gnn_weak_W"][0, :, k * FULL:(k + 1) * FULL, :].rearrange("e p f -> p e f")).then_inc(g.weak_loaded, 16)
                for e in range(NS):
                    sp.dma_start(g.w_strong1[:, e, :, :], w1[:, e, :, :]).then_inc(g.strong_loaded[e], 16)
                    sp.dma_start(g.w_strong2[:, e, :, :], w2[:, e, :, :]).then_inc(g.strong_loaded[e], 16)

            @block.tensor
            def _(pe):
                pe.wait_ge(g.x_loaded, 16)
                for t in range(T):
                    last = nc.tensor.transpose(g.wide(0)[:, t * P:(t + 1) * P], g.xa[:, t, :], g.ident[0:P, 0:P])
                last.then_inc(turned, 1)
                pe.wait_ge(g.sage_loaded, 16 * 10)
                for layer in range(2):
                    wp, ws, wn = (g.w_sage[:, 3 * layer + i, :] for i in range(3))
                    base = layer * N
                    pe.wait_ge(x_t_ready, layer + 1)
                    for lo, hi in ROWS:
                        last = nc.tensor.matmul(g.wide(2)[:, lo:hi], wp, g.x_t[:, 0, lo:hi], start=True, stop=True)
                    last.then_inc(pooled, 1)
                    pe.wait_ge(pool_ready, layer + 1)

                    def spread(k, p, t):
                        lhs = g.ident_bf[0:P, ds(p, 1)].broadcast_to([P, FULL])
                        for lo, hi in ROWS:
                            last = nc.tensor.matmul(row(k)[:, lo:hi], lhs, g.has_edge_t[:, t, lo:hi], start=True, stop=True)
                        last.then_inc(row_ready, 1)

                    for t in range(T):
                        if base + t - RING + 1 > 0:
                            pe.wait_ge(row_used, base + t - RING + 1)
                        spread(base + t, 0, t)
                    with pe.Fori(0, TURNS) as i:
                        for j in range(BODY):
                            for t in range(T):
                                k = base + T * FIRST + j * T + t
                                pe.wait_ge(row_used, i * (BODY * T) + (k - RING + 1))
                                spread(k, i * BODY + (FIRST + j), t)
                    pe.wait_ge(agg_ready, layer + 1)
                    if layer == 0:
                        for lo, hi in ROWS:
                            nc.tensor.matmul(g.wide(0)[:, lo:hi], ws, g.x_t[:, 0, lo:hi], start=True, stop=False)
                            last = nc.tensor.matmul(g.wide(0)[:, lo:hi], wn, agg_t[:, :, :].rearrange("f t p -> f (t p)")[:, lo:hi],
                                                    start=False, stop=True)
                        last.then_inc(summed, 1)
                    else:
                        for t in range(T):
                            to = g.bank(t)[0:P, 0:D]
                            nc.tensor.matmul(to, g.x_t[:, 0, t * P:(t + 1) * P], ws, start=True, stop=False)
                            nc.tensor.matmul(to, agg_t[:, t, :], wn, start=False, stop=False)
                            last = nc.tensor.matmul(to, g.ones[0:1, 0:P], g.b_sage2[:, :], start=False, stop=True)
                        last.then_inc(summed, 1)

            @block.scalar
            def _(act):
                act.wait_ge(turned, 1)
                nc.scalar.copy(g.x_t[:, 0, :], g.wide(0)).then_inc(x_t_ready, 1)
                act.wait_ge(g.sage_loaded, 16 * 10)
                for layer in range(2):
                    act.wait_ge(pooled, layer + 1)
                    nc.scalar.activation(pool_t[:, :], g.wide(2), ACT.Relu, bias=g.b_sage[:, 2 * layer:2 * layer + 1]).then_inc(pool_ready, 1)
                    if layer == 0:
                        act.wait_ge(summed, 1)
                        nc.scalar.activation(g.x_t[:, 0, :], g.wide(0), ACT.Relu, bias=g.b_sage[:, 1:2]).then_inc(x_t_ready, 1)
                g.layernorm_scalar(1)

            @block.vector
            def _(dve):
                chain = Chain(dve, g.dve_chain)
                chain.done = g.dve_links
                for layer in range(2):
                    base = layer * N
                    dve.wait_ge(pool_ready, layer + 1)

                    def top(k, ready, to):
                        if ready is not None:
                            dve.wait_ge(row_ready, ready)
                            dve.sem_inc(row_seen, 1)
                        nc.vector.tensor_tensor_reduce(out=masked[:, k % RING, :], in0=row(k), in1=pool_t[:, :], scale=1.0, scalar=0.0,
                                                       op0=ALU.mult, op1=ALU.max, accum_out=to).then_inc(row_used, 1)

                    for t in range(T):
                        top(base + t, base + t + 1, staged[:, t, 0:1])
                    dve.wait_ge(row_used, base + T)
                    chain.link(nc.vector.tensor_copy(agg_t[:, :, 0:1], staged[:, :, 0:1]))
                    with dve.Fori(0, TURNS) as i:
                        chain.enter(i, 1)
                        for j in range(BODY):
                            for t in range(T):
                                k = base + T * FIRST + j * T + t
                                top(k, i * (BODY * T) + (k + 2) if (j * T + t) % 2 == 0 else None, staged[:, t, j:j + 1])
                        dve.wait_ge(row_used, i * (BODY * T) + (base + T * FIRST + BODY * T))
                        chain.link(nc.vector.tensor_copy(agg_t[:, :, ds(i * BODY + FIRST, BODY)], staged[:, :, :]))
                    chain.leave(TURNS)
                    nc.vector.engine_nop().then_inc(agg_ready, 1)
                dve.wait_ge(summed, 2)
                sums = psum[0:P, 0:T * 512].rearrange("p (t f) -> p t f", f=512)[:, :, 0:D]
                chain.link(nc.vector.tensor_tensor(g.res[:, :, :], sums, g.xa[:, :, :], ALU.add))
                chain.link(g.layernorm_vector(chain, g.res, g.xa, 1))
                g.dve_links = chain.done


def propagate(nc, g):
    with ExitStack() as ctx:
        def sb(name, shape, dt=F32):
            return ctx.enter_context(nc.sbuf_tensor(name, shape, dt))

        def sem(name):
            return ctx.enter_context(nc.semaphore(name))

        diag = sb("deg_diag", [P, T, P])
        diag_ready = sem("deg_diag_ready")
        spread = sem("deg_spread")
        summed = sem("prop_summed")
        psum = g.psum
        with nc.Block() as block:
            @block.gpsimd
            def _(pool):
                pool.tensor_tensor(diag[:, :, :], g.ident[0:P, 0:P].unsqueeze(1).broadcast_to([P, T, P]),
                                   g.recip_deg[:, :].unsqueeze(2).broadcast_to([P, T, P]), ALU.mult).then_inc(diag_ready, 1)

            @block.tensor
            def _(pe):
                for s in range(T):
                    for d in range(T):
                        last = nc.tensor.matmul(g.bank(s)[0:P, 0:D], g.count_t[:, d, s * P:(s + 1) * P], g.xa[:, d, :],
                                                start=d == 0, stop=d == T - 1)
                last.then_inc(summed, 1)
                pe.wait_ge(diag_ready, 1)
                for t in range(T):
                    last = nc.tensor.matmul(g.wide(5)[0:P, t * P:(t + 1) * P], g.ones[0:P, 0:P], diag[:, t, :], start=True, stop=True)
                last.then_inc(spread, 1)

            @block.scalar
            def _(act):
                g.layernorm_scalar(2)

            @block.vector
            def _(dve):
                chain = Chain(dve, g.dve_chain)
                chain.done = g.dve_links
                dve.wait_ge(summed, 1)
                sums = psum[0:P, 0:T * 512].rearrange("p (t f) -> p t f", f=512)[:, :, 0:D]
                chain.link(nc.vector.tensor_tensor(g.res[:, :, :], sums, g.xa[:, :, :], ALU.add))
                chain.link(g.layernorm_vector(chain, g.res, g.xb, 2))
                dve.wait_ge(spread, 1)
                for t in range(T):
                    last = nc.vector.tensor_tensor(g.count[:, t, :], g.count[:, t, :], g.wide(5)[0:P, :], ALU.mult)
                chain.link(last)
                g.dve_links = chain.done


def gat(nc, g):
    SHAPES = ((1, HEADS, HID // HEADS), (2, HEADS, HID // HEADS), (2, 1, D))
    SMAX, ATT, OUT = 0, (2, 4), 6
    with ExitStack() as ctx:
        def sb(name, shape, dt=F32):
            return ctx.enter_context(nc.sbuf_tensor(name, shape, dt))

        def sem(name):
            return ctx.enter_context(nc.semaphore(name))

        feats = [sb("feats4", [P, T, HEADS, HID // HEADS + 1]), sb("feats1", [P, T, 1, D + 1])]
        prod = sb("prod", [P, T, HID])
        src_score = sb("src_score", [P, T, HEADS])
        src_low = sb("src_low", [P, T, HEADS])
        dst_score = sb("dst_score", [P, T, HEADS])
        top = sb("top", [P, T])
        high_row = sb("high_row", [P, T])
        low_row = sb("low_row", [P, T])
        masked = sb("gat_masked", [P, T, N], BF16)
        diag_src = sb("diag_src", [P, T, P])
        diag_high = sb("diag_high", [P, T, P])
        diag_low = sb("diag_low", [P, T, P])
        score = sb("score", [P, T, N])
        prob = sb("prob", [P, T, N])
        recip = sb("recip", [P, T])
        heads_out = sb("heads_out", [P, T, HID])
        elu_e = sb("elu_e", [P, T, HID])
        ones_ready = sem("gat_ones_ready")
        turned = sem("gat_turned")
        x_t_ready_s = sem("gat_x_t_ready_s")
        x_t_ready_v = sem("gat_x_t_ready_v")
        feats_done = sem("feats_done")
        feats_ready = sem("feats_ready")
        src_score_ready = sem("src_score_ready")
        diag_src_ready = sem("diag_src_ready")
        src_spread = sem("src_spread")
        top_done = sem("top_done")
        spread_seen = sem("spread_seen")
        row_cols_ready = sem("row_cols_ready")
        diag_rows_ready = sem("diag_rows_ready")
        rows_spread = sem("rows_spread")
        low_ready = sem("low_ready")
        score_ready = sem("score_ready")
        exp_ready = sem("exp_ready")
        prob_ready = sem("prob_ready")
        heads_summed = sem("heads_summed")
        heads_copied = sem("heads_copied")
        min_ready = sem("min_ready")
        elu_exp_ready = sem("elu_exp_ready")
        elu_ready = sem("elu_ready")
        psum = g.psum

        def ident_rows():
            return g.ident[0:P, 0:P].unsqueeze(1).broadcast_to([P, T, P])

        with nc.Block() as block:
            @block.gpsimd
            def _(pool):
                pool.memset(feats[0][:, :, :, HID // HEADS:], 1.0).then_inc(ones_ready, 1)
                pool.memset(feats[1][:, :, :, D:], 1.0).then_inc(ones_ready, 1)
                base = 0
                for layer, (KT, H, C) in enumerate(SHAPES):
                    pool.wait_ge(src_score_ready, layer + 1)

                    def source_diagonal(h, n):
                        pool.wait_ge(src_spread, n)
                        pool.tensor_tensor(diag_src[:, :, :], ident_rows(),
                                           src_score[:, :, ds(h, 1)].broadcast_to([P, T, P]), ALU.mult).then_inc(diag_src_ready, 1)

                    def row_diagonals(n):
                        pool.wait_ge(row_cols_ready, n + 1)
                        pool.wait_ge(rows_spread, n)
                        for diag, col in ((diag_high, high_row), (diag_low, low_row)):
                            last = pool.tensor_tensor(diag[:, :, :], ident_rows(),
                                                      col[:, :].unsqueeze(2).broadcast_to([P, T, P]), ALU.mult)
                        last.then_inc(diag_rows_ready, 1)

                    source_diagonal(0, base)
                    row_diagonals(base)
                    if H > 1:
                        with pool.Fori(1, H) as h:
                            source_diagonal(h, h + base)
                            row_diagonals(h + base)
                    base += H

            @block.tensor
            def _(pe):
                pe.wait_ge(g.gat_loaded, 16 * 12)
                for t in range(T):
                    last = nc.tensor.transpose(g.wide(0)[:, t * P:(t + 1) * P], g.xb[:, t, :], g.ident[0:P, 0:P])
                last.then_inc(turned, 1)
                base = 0
                for layer, (KT, H, C) in enumerate(SHAPES):
                    w = (g.w_gat0, g.w_gat1, g.w_gat2)[layer]
                    x1 = feats[0 if H > 1 else 1]
                    pe.wait_ge(x_t_ready_s, layer + 1)
                    if layer:
                        pe.wait_ge(x_t_ready_v, layer)
                    for t in range(T):
                        for k in range(KT):
                            last = nc.tensor.matmul(g.bank(t)[0:P, 0:H * C], g.x_t[:, k, t * P:(t + 1) * P], w[:, k, :],
                                                    start=k == 0, stop=k == KT - 1)
                    last.then_inc(feats_done, 1)
                    pe.wait_ge(feats_ready, T * (layer + 1))

                    def spread_source(n):
                        pe.wait_ge(diag_src_ready, n + 1)
                        pe.wait_ge(top_done, n)
                        for t in range(T):
                            last = nc.tensor.matmul(g.wide(SMAX)[0:P, t * P:(t + 1) * P], g.ones[0:P, 0:P], diag_src[:, t, :],
                                                    start=True, stop=True)
                        last.then_inc(src_spread, 1)

                    def spread_rows(n):
                        pe.wait_ge(diag_rows_ready, n + 1)
                        pe.wait_ge(score_ready, n * T)
                        pe.wait_ge(low_ready, n * T)
                        for b, diag in ((ATT[1], diag_low), (ATT[0], diag_high)):
                            for t in range(T):
                                last = nc.tensor.matmul(g.wide(b)[0:P, t * P:(t + 1) * P], g.ones[0:P, 0:P], diag[:, t, :],
                                                        start=True, stop=True)
                        last.then_inc(rows_spread, 1)

                    def aggregate(h, n):
                        pe.wait_ge(heads_copied, n)
                        if H == 1:
                            pe.wait_ge(ones_ready, 2)
                        for s in range(T):
                            pe.wait_ge(prob_ready, n * T + (s + 1))
                            for d in range(T):
                                b, at = (OUT, d) if d < 3 else (OUT + 1, d - 3)
                                last = nc.tensor.matmul(g.bank(b)[0:P, at * (C + 1):(at + 1) * (C + 1)],
                                                        prob[:, s, d * P:(d + 1) * P],
                                                        x1[:, s, ds(h, 1), :].rearrange("p h c -> p (h c)"),
                                                        start=s == 0 and at == 0, stop=s == T - 1, skip_group_check=True)
                        last.then_inc(heads_summed, 1)

                    if layer == 0:
                        pe.wait_ge(ones_ready, 2)
                    spread_source(base)
                    spread_rows(base)
                    if H > 1:
                        with pe.Fori(0, H - 1) as h:
                            spread_source(h + (base + 1))
                            aggregate(h, h + base)
                            spread_rows(h + (base + 1))
                    aggregate(H - 1, base + H - 1)
                    base += H
                    if layer < 2:
                        pe.wait_ge(elu_ready, layer + 1)
                        for k in range(2):
                            for t in range(T):
                                last = nc.tensor.transpose(g.wide(2 * k)[:, t * P:(t + 1) * P],
                                                           heads_out[:, t, k * FULL:(k + 1) * FULL], g.ident[0:P, 0:P])
                        last.then_inc(turned, 1)

            @block.scalar
            def _(act):
                act.wait_ge(turned, 1)
                nc.scalar.copy(g.x_t[:, 0, :], g.wide(0)).then_inc(x_t_ready_s, 1)
                base = 0
                for layer, (KT, H, C) in enumerate(SHAPES):
                    x1 = feats[0 if H > 1 else 1]
                    act.wait_ge(feats_done, layer + 1)
                    for t in range(T):
                        nc.scalar.copy(x1[:, t, :, 0:C], g.bank(t)[0:P, 0:H * C].rearrange("p (h c) -> p h c", h=H)).then_inc(feats_ready, 1)

                    def head(h, n):
                        act.wait_ge(rows_spread, n + 1)
                        act.wait_ge(prob_ready, n * T)
                        for s in range(T + 1):
                            if s < T:
                                nc.scalar.activation(score[:, s, :], g.wide(ATT[1])[0:P, :], ACT.Identity,
                                                     bias=src_low[:, s, ds(h, 1)]).then_inc(low_ready, 1)
                            if s > 0:
                                act.wait_ge(score_ready, n * T + s)
                                nc.scalar.activation(score[:, s - 1, :], score[:, s - 1, :], ACT.Exp).then_inc(exp_ready, 1)

                    if H > 1:
                        with act.Fori(0, H) as h:
                            head(h, h + base)
                    else:
                        head(0, base)
                    base += H
                    if layer < 2:
                        act.wait_ge(min_ready, layer + 1)
                        nc.scalar.activation(elu_e[:, :, :], elu_e[:, :, :], ACT.Exp).then_inc(elu_exp_ready, 1)
                        act.wait_ge(turned, layer + 2)
                        nc.scalar.copy(g.x_t[:, 0, :], g.wide(0)).then_inc(x_t_ready_s, 1)
                g.layernorm_scalar(3)

            @block.vector
            def _(dve):
                chain = Chain(dve, g.dve_chain)
                chain.done = g.dve_links
                dve.wait_ge(g.gat_loaded, 16 * 12)
                base = 0
                for layer, (KT, H, C) in enumerate(SHAPES):
                    x1 = feats[0 if H > 1 else 1]
                    dve.wait_ge(feats_ready, T * (layer + 1))
                    for side, to in ((0, src_score), (1, dst_score)):
                        parts = prod[:, :, 0:H * C].rearrange("p t (h c) -> p t h c", h=H)
                        for h in range(H):
                            last = nc.vector.tensor_tensor(parts[:, :, h, :], x1[:, :, h, 0:C],
                                                           g.att[layer][:, side, h * C:(h + 1) * C].unsqueeze(1).broadcast_to([P, T, C]),
                                                           ALU.mult)
                        chain.link(last)
                        chain.link(nc.vector.tensor_reduce(to[:, :, 0:H], parts, AX.X, ALU.add))
                    nc.vector.tensor_scalar(src_low[:, :, 0:H], src_score[:, :, 0:H], NEG_SLOPE, None, ALU.mult).then_inc(src_score_ready, 1)

                    def maximum(h, n):
                        dve.wait_ge(src_spread, n + 1)
                        dve.sem_inc(spread_seen, 1)
                        for t in range(T):
                            last = nc.vector.tensor_tensor_reduce(out=masked[:, t, :], in0=g.wide(SMAX)[0:P, :], in1=g.no_edge_t[:, t, :],
                                                                  scale=1.0, scalar=-3.0e38, op0=ALU.add, op1=ALU.max,
                                                                  accum_out=top[:, t:t + 1])
                        last.then_inc(top_done, 1)
                        dve.wait_ge(top_done, n + 1)
                        dve.wait_ge(diag_rows_ready, n)
                        d_col = dst_score[:, :, ds(h, 1)].rearrange("p t o -> p (t o)")
                        chain.link(nc.vector.tensor_tensor(top[:, :], top[:, :], d_col, ALU.add))
                        chain.link(nc.vector.scalar_tensor_tensor(top[:, :], top[:, :], NEG_SLOPE, top[:, :], ALU.mult, ALU.max))
                        nc.vector.tensor_tensor(high_row[:, :], d_col, top[:, :], ALU.subtract)
                        nc.vector.scalar_tensor_tensor(low_row[:, :], d_col, NEG_SLOPE, top[:, :], ALU.mult, ALU.subtract).then_inc(row_cols_ready, 1)

                    def weigh(h, n):
                        dve.wait_ge(rows_spread, n + 1)
                        for s in range(T + 1):
                            if s < T:
                                dve.wait_ge(low_ready, n * T + (s + 1))
                                nc.vector.scalar_tensor_tensor(score[:, s, :], g.wide(ATT[0])[0:P, :], src_score[:, s, ds(h, 1)],
                                                               score[:, s, :], ALU.add, ALU.max).then_inc(score_ready, 1)
                            if s == 1:
                                dve.wait_ge(heads_summed, n)
                            if s > 0:
                                dve.wait_ge(exp_ready, n * T + s)
                                nc.vector.tensor_tensor(prob[:, s - 1, :], score[:, s - 1, :], g.count_loop[:, s - 1, :],
                                                        ALU.mult).then_inc(prob_ready, 1)

                    def normalise(h, n):
                        dve.wait_ge(heads_summed, n + 1)
                        sums = [g.bank(OUT)[0:P, 0:3 * (C + 1)].rearrange("p (t c) -> p t c", c=C + 1),
                                g.bank(OUT + 1)[0:P, 0:2 * (C + 1)].rearrange("p (t c) -> p t c", c=C + 1)]
                        for (lo, hi), s in zip(((0, 3), (3, 5)), sums):
                            last = nc.vector.tensor_scalar(recip[:, lo:hi], s[:, :, C], 1e-16, None, ALU.add)
                        chain.link(last)
                        chain.link(nc.vector.reciprocal(recip[:, :], recip[:, :]))
                        for (lo, hi), s in zip(((0, 3), (3, 5)), sums):
                            to = heads_out[:, lo:hi, ds(h * C, C)]
                            last = nc.vector.tensor_tensor(to, s[:, :, 0:C], recip[:, lo:hi].unsqueeze(2).broadcast_to([P, hi - lo, C]), ALU.mult)
                        last.then_inc(heads_copied, 1)

                    maximum(0, base)
                    if H > 1:
                        with dve.Fori(0, H - 1) as h:
                            chain.enter(h, 4)
                            maximum(h + 1, h + (base + 1))
                            weigh(h, h + base)
                            normalise(h, h + base)
                        chain.leave(H - 1)
                    weigh(H - 1, base + H - 1)
                    normalise(H - 1, base + H - 1)
                    base += H
                    dve.wait_ge(heads_copied, base)
                    HC = H * C
                    chain.link(nc.vector.tensor_tensor(heads_out[:, :, 0:HC], heads_out[:, :, 0:HC],
                                                       g.b_gat[layer][:, :].unsqueeze(1).broadcast_to([P, T, HC]), ALU.add))
                    if layer < 2:
                        nc.vector.tensor_scalar(elu_e[:, :, :], heads_out[:, :, :], 0.0, None, ALU.min).then_inc(min_ready, 1)
                        dve.wait_ge(elu_exp_ready, layer + 1)
                        nc.vector.scalar_tensor_tensor(heads_out[:, :, :], elu_e[:, :, :], -1.0, heads_out[:, :, :], ALU.add, ALU.max).then_inc(elu_ready, 1)
                        dve.wait_ge(turned, layer + 2)
                        nc.vector.tensor_copy(g.x_t[:, 1, :], g.wide(2)).then_inc(x_t_ready_v, 1)
                chain.link(nc.vector.tensor_tensor(g.res[:, :, :], heads_out[:, :, 0:D], g.xb[:, :, :], ALU.add))
                chain.link(g.layernorm_vector(chain, g.res, g.xa, 3))
                g.dve_links = chain.done


def moe(nc, g):
    a = g.a
    MOE_LOADS = 16 * (3 * LAYERS + 8)
    WEAK_BANK, STRONG_BANK = 4, 6
    with ExitStack() as ctx:
        def sb(name, shape, dt=F32):
            return ctx.enter_context(nc.sbuf_tensor(name, shape, dt))

        def sem(name):
            return ctx.enter_context(nc.semaphore(name))

        h = sb("h", [P, T, HID])
        agg_t = sb("moe_agg_t", [FULL, 2, N])
        hidden_t = sb("hidden_t", [FULL, 4, N])
        tri = sb("tri", [P, NEXP, NEXP])
        logits = sb("logits", [P, T, NEXP + 1])
        beats = sb("beats", [P, T, NEXP, NEXP])
        ties = sb("ties", [P, T, NEXP, NEXP])
        rank = sb("rank", [P, T, NEXP])
        best = sb("best", [P, T])
        gate = sb("gate", [P, T, NEXP])
        shifted = sb("shifted", [P, T, NEXP])
        conf = sb("conf", [P, T])
        total = sb("total", [P, T])
        gate_t = sb("gate_t", [NEXP, N])
        weak_sum = sb("weak_sum", [P, 2, 2 * HID])
        moe_sum = sb("moe_sum", [P, T, HID])
        y = sb("y", [P, T, D])
        tri_ready = sem("tri_ready")
        x3_turned = sem("x3_turned")
        x3_t_ready = sem("x3_t_ready")
        h_done = sem("h_done")
        h_ready = sem("h_ready")
        turned = sem("moe_turned")
        h_t_ready_s = sem("h_t_ready_s")
        h_t_ready_v = sem("h_t_ready_v")
        agg_done = sem("agg_done")
        agg_ready_s = sem("agg_ready_s")
        agg_ready_v = sem("agg_ready_v")
        logits_done = sem("logits_done")
        shifted_ready = sem("shifted_ready")
        exps_ready = sem("exps_ready")
        gate_ready = sem("gate_ready")
        gate_turned = sem("gate_turned")
        gate_t_ready = sem("gate_t_ready")
        weak_done = sem("weak_done")
        weak_read = sem("weak_read")
        hidden_done = sem("hidden_done")
        hidden_ready = sem("hidden_ready")
        strong_done = sem("strong_done")
        strong_read = sem("strong_read")
        weak_pair = sem("weak_pair")
        bias_done = sem("bias_done")
        bias_bank_seen = sem("bias_bank_seen")
        bias_read = sem("bias_read")
        y_done = sem("y_done")
        y_ready = sem("y_ready")
        stored = sem("stored")
        psum = g.psum
        WPAIR = NW // 2

        with nc.Block() as block:
            @block.sync
            def _(sp):
                w1 = a["L3_gnn_strong_W1"].rearrange("l e (k p) f -> l e p k f", p=FULL)
                w2 = a["L3_gnn_strong_W2"].rearrange("l e (k p) f -> l e p k f", p=FULL)
                ww = a["L3_gnn_weak_W"].rearrange("l e (k p) f -> l k p e f", p=FULL)
                with sp.Fori(1, LAYERS) as l:
                    sp.wait_ge(weak_done, l * (T * WPAIR))
                    for k in range(2):
                        sp.dma_start(g.w_weak[:, k, :, :], ww[ds(l, 1), k].rearrange("l p e f -> p (l e) f")).then_inc(g.weak_loaded, 16)
                    for e in range(NS):
                        sp.wait_ge(strong_done, l * (NS * T) + (e + 1 - NS) * T)
                        sp.dma_start(g.w_strong1[:, e, :, :], w1[ds(l, 1), e].rearrange("l p k f -> p (l k) f")).then_inc(g.strong_loaded[e], 16)
                        sp.dma_start(g.w_strong2[:, e, :, :], w2[ds(l, 1), e].rearrange("l p k f -> p (l k) f")).then_inc(g.strong_loaded[e], 16)
                sp.wait_ge(y_ready, 1)
                sp.dma_start(g.out.rearrange("(t p) f -> p t f", p=P), y[:, :, :]).then_inc(stored, 16)
                sp.wait_ge(stored, 16)

            @block.gpsimd
            def _(pool):
                pool.memset(tri[:, :, :], 1.0).then_inc(tri_ready, 1)
                pool.wait_ge(tri_ready, 1)
                pool.affine_select(out=tri[:, :, :], in_=tri[:, :, :], compare_op=ALU.is_gt, fill=0.0, base=0,
                                   pattern=[[1, NEXP], [-1, NEXP]], channel_multiplier=0).then_inc(tri_ready, 1)

            @block.tensor
            def _(pe):
                pe.wait_ge(g.moe_loaded, MOE_LOADS)
                for t in range(T):
                    last = nc.tensor.transpose(g.wide(0)[:, t * P:(t + 1) * P], g.xa[:, t, :], g.ident[0:P, 0:P])
                last.then_inc(x3_turned, 1)
                pe.wait_ge(x3_t_ready, 1)
                for t in range(T):
                    to = g.bank(2 + t)[0:P, 0:HID]
                    nc.tensor.matmul(to, g.x_t[:, 0, t * P:(t + 1) * P], g.w_in[:, :], start=True, stop=False)
                    last = nc.tensor.matmul(to, g.ones[0:1, 0:P], g.b_in[:, :], start=False, stop=True)
                last.then_inc(h_done, 1)

                def turn_h(n):
                    pe.wait_ge(h_ready, n + 1)
                    for k in range(2):
                        for t in range(T):
                            last = nc.tensor.transpose(g.wide(2 * k)[:, t * P:(t + 1) * P],
                                                       h[:, t, k * FULL:(k + 1) * FULL], g.ident[0:P, 0:P])
                    last.then_inc(turned, 1)

                with pe.Fori(0, LAYERS) as l:
                    turn_h(l)
                    for f in range(2):
                        for lo, hi in ROWS:
                            for s in range(T):
                                last = nc.tensor.matmul(g.wide(4 + 2 * f)[:, lo:hi], h[:, s, f * FULL:(f + 1) * FULL],
                                                        g.count[:, s, lo:hi], start=s == 0, stop=s == T - 1)
                    last.then_inc(agg_done, 1)
                    pe.wait_ge(h_t_ready_s, l + 1)
                    pe.wait_ge(h_t_ready_v, l + 1)
                    pe.wait_ge(agg_ready_s, l + 1)
                    pe.wait_ge(agg_ready_v, l + 1)
                    for t in range(T):
                        to = g.bank(STRONG_BANK)[0:P, t * 16:t * 16 + NEXP + 1]
                        for k in range(4):
                            lhs = (g.x_t if k < 2 else agg_t)[:, k % 2, t * P:(t + 1) * P]
                            nc.tensor.matmul(to, lhs, g.w_router[:, ds(l, 1), k, :].rearrange("p l e -> p (l e)"),
                                             start=k == 0, stop=False)
                        last = nc.tensor.matmul(to, g.ones[0:1, 0:P], g.b_router[:, ds(l, 1), :].rearrange("p l e -> p (l e)"),
                                                start=False, stop=True)
                    last.then_inc(logits_done, 1)
                    pe.wait_ge(g.weak_loaded, l * 32 + 32)
                    for t in range(T):
                        for q in range(WPAIR):
                            n = t * WPAIR + q
                            if n >= 2:
                                pe.wait_ge(weak_read, l * (T * WPAIR) + (n - 1))
                            for k in range(2):
                                last = nc.tensor.matmul(g.bank(WEAK_BANK + n % 2)[0:P, :], agg_t[:, k, t * P:(t + 1) * P],
                                                        g.w_weak[:, k, 2 * q:2 * q + 2, :].rearrange("p e f -> p (e f)"),
                                                        start=k == 0, stop=k == 1)
                            last.then_inc(weak_done, 1)
                    pe.wait_ge(gate_ready, l + 1)
                    for t in range(T):
                        last = nc.tensor.transpose(g.wide(STRONG_BANK)[0:NEXP, t * P:(t + 1) * P], gate[:, t, :], g.ident[0:P, 0:P])
                    last.then_inc(gate_turned, 1)
                    for e in range(NS):
                        pe.wait_ge(g.strong_loaded[e], l * 32 + 32)
                        for m in range(4):
                            n = e * 4 + m
                            if n >= 2:
                                pe.wait_ge(hidden_ready, l * (NS * 4) + (n - 1))
                            for lo, hi in ROWS:
                                for k in range(2):
                                    last = nc.tensor.matmul(g.wide(2 * (n % 2))[:, lo:hi], g.w_strong1[:, e, k, m * FULL:(m + 1) * FULL],
                                                            agg_t[:, k, lo:hi], start=k == 0, stop=k == 1)
                            last.then_inc(hidden_done, 1)
                        if e == 0:
                            pe.wait_ge(gate_t_ready, l + 1)
                        pe.wait_ge(hidden_ready, l * (NS * 4) + (e * 4 + 4))
                        for t in range(T):
                            n = e * T + t
                            if n >= 2:
                                pe.wait_ge(strong_read, l * (NS * T) + (n - 1))
                            for k in range(4):
                                last = nc.tensor.matmul(g.bank(STRONG_BANK + n % 2)[0:P, 0:HID], hidden_t[:, k, t * P:(t + 1) * P],
                                                        g.w_strong2[:, e, k, :], start=k == 0, stop=k == 3)
                            last.then_inc(strong_done, 1)
                    pe.wait_ge(weak_read, l * (T * WPAIR) + T * WPAIR)
                    pe.sem_inc(bias_bank_seen, 1)
                    for t in range(T):
                        if t >= 2:
                            pe.wait_ge(bias_read, l * T + (t - 1))
                            pe.sem_inc(bias_bank_seen, 1)
                        nc.tensor.matmul(g.bank(WEAK_BANK + t % 2)[0:P, 0:HID], gate_t[:, t * P:(t + 1) * P],
                                         g.b_strong2[:, ds(l, 1), :].rearrange("p l f -> p (l f)"), start=True, stop=True).then_inc(bias_done, 1)

                turn_h(LAYERS)
                pe.wait_ge(h_t_ready_s, LAYERS + 1)
                pe.wait_ge(h_t_ready_v, LAYERS + 1)
                for t in range(T):
                    to = g.bank(t)[0:P, 0:D]
                    for k in range(2):
                        nc.tensor.matmul(to, g.x_t[:, k, t * P:(t + 1) * P], g.w_out[:, k, :], start=k == 0, stop=False)
                    last = nc.tensor.matmul(to, g.ones[0:1, 0:P], g.b_out[:, :], start=False, stop=True)
                last.then_inc(y_done, 1)

            @block.scalar
            def _(act):
                act.wait_ge(g.moe_loaded, MOE_LOADS)
                act.wait_ge(x3_turned, 1)
                nc.scalar.copy(g.x_t[:, 0, :], g.wide(0)).then_inc(x3_t_ready, 1)
                with act.Fori(0, LAYERS) as l:
                    act.wait_ge(turned, l + 1)
                    nc.scalar.copy(g.x_t[:, 0, :], g.wide(0)).then_inc(h_t_ready_s, 1)
                    act.wait_ge(agg_done, l + 1)
                    nc.scalar.copy(agg_t[:, 0, :], g.wide(4)).then_inc(agg_ready_s, 1)
                    act.wait_ge(shifted_ready, l + 1)
                    nc.scalar.activation(shifted[:, :, :], shifted[:, :, :], ACT.Exp)
                    nc.scalar.activation(conf[:, :], conf[:, :], ACT.Exp, scale=-1.0).then_inc(exps_ready, 1)
                    for e in range(NS):
                        for m in range(4):
                            n = e * 4 + m
                            act.wait_ge(hidden_done, l * (NS * 4) + (n + 1))
                            if m == 0:
                                act.wait_ge(strong_done, l * (NS * T) + e * T)
                            nc.scalar.activation(hidden_t[:, m, :], g.wide(2 * (n % 2)), ACT.Relu,
                                                 bias=g.b_strong1[:, ds(l, 1), e, m]).then_inc(hidden_ready, 1)
                act.wait_ge(turned, LAYERS + 1)
                nc.scalar.copy(g.x_t[:, 0, :], g.wide(0)).then_inc(h_t_ready_s, 1)
                g.layernorm_scalar(4)

            @block.vector
            def _(dve):
                chain = Chain(dve, g.dve_chain)
                chain.done = g.dve_links
                dve.wait_ge(g.moe_loaded, MOE_LOADS)
                dve.wait_ge(h_done, 1)
                nc.vector.tensor_copy(h[:, :, :], psum[0:P, 2 * 512:7 * 512].rearrange("p (t f) -> p t f", f=512)[:, :, 0:HID]).then_inc(h_ready, 1)
                dve.wait_ge(tri_ready, 2)
                with dve.Fori(0, LAYERS) as l:
                    chain.enter(l, 31)
                    dve.wait_ge(turned, l + 1)
                    nc.vector.tensor_copy(g.x_t[:, 1, :], g.wide(2)).then_inc(h_t_ready_v, 1)
                    dve.wait_ge(agg_done, l + 1)
                    nc.vector.tensor_copy(agg_t[:, 1, :], g.wide(6)).then_inc(agg_ready_v, 1)
                    dve.wait_ge(logits_done, l + 1)
                    chain.link(nc.vector.tensor_copy(logits[:, :, :], g.bank(STRONG_BANK)[0:P, 0:T * 16].rearrange("p (t e) -> p t e", e=16)[:, :, 0:NEXP + 1]))
                    lg = logits[:, :, 0:NEXP]
                    nc.vector.tensor_copy(conf[:, :], logits[:, :, NEXP])
                    chain.link(nc.vector.tensor_reduce(best[:, :], lg, AX.X, ALU.max))
                    nc.vector.tensor_tensor(shifted[:, :, :], lg, best[:, :].unsqueeze(2).broadcast_to([P, T, NEXP]), ALU.subtract).then_inc(shifted_ready, 1)
                    for t in range(T):
                        other = logits[:, t, 0:NEXP].unsqueeze(1).broadcast_to([P, NEXP, NEXP])
                        mine = logits[:, t, 0:NEXP].unsqueeze(2).broadcast_to([P, NEXP, NEXP])
                        nc.vector.tensor_tensor(beats[:, t, :, :], other, mine, ALU.is_gt)
                        last = nc.vector.tensor_tensor(ties[:, t, :, :], other, mine, ALU.is_equal)
                    chain.link(last)
                    for t in range(T):
                        last = nc.vector.tensor_tensor(ties[:, t, :, :], ties[:, t, :, :], tri[:, :, :], ALU.mult)
                    chain.link(last)
                    chain.link(nc.vector.tensor_tensor(beats[:, :, :, :], beats[:, :, :, :], ties[:, :, :, :], ALU.add))
                    chain.link(nc.vector.tensor_reduce(rank[:, :, :], beats[:, :, :, :], AX.X, ALU.add))
                    dve.wait_ge(exps_ready, l + 1)
                    chain.link(nc.vector.scalar_tensor_tensor(gate[:, :, :], rank[:, :, :], 2.0, shifted[:, :, :], ALU.is_lt, ALU.mult))
                    chain.link(nc.vector.tensor_reduce(total[:, :], gate[:, :, :], AX.X, ALU.add))
                    chain.link(nc.vector.reciprocal(total[:, :], total[:, :]))
                    nc.vector.tensor_tensor(gate[:, :, :], gate[:, :, :], total[:, :].unsqueeze(2).broadcast_to([P, T, NEXP]), ALU.mult).then_inc(gate_ready, 1)
                    chain.link(nc.vector.tensor_scalar(conf[:, :], conf[:, :], 1.0, None, ALU.add))
                    chain.link(nc.vector.reciprocal(conf[:, :], conf[:, :]))
                    for t in range(T):
                        for q in range(WPAIR):
                            n = t * WPAIR + q
                            dve.wait_ge(weak_done, l * (T * WPAIR) + (n + 1))
                            nc.vector.tensor_tensor(weak_sum[:, q, :], g.bank(WEAK_BANK + n % 2)[0:P, :],
                                                    g.b_weak[:, ds(l, 1), 2 * q * HID:(2 * q + 2) * HID].rearrange("p l f -> p (l f)"),
                                                    ALU.add).then_inc(weak_read, 1)
                            dve.wait_ge(weak_read, l * (T * WPAIR) + (n + 1))
                            for j in range(2):
                                e = 2 * q + j
                                part = weak_sum[:, q, j * HID:(j + 1) * HID]
                                to = moe_sum[:, t, :] if e == 0 else part
                                last = nc.vector.tensor_scalar(to, part, 0.0, gate[:, t, e:e + 1], ALU.max, ALU.mult)
                            chain.link(last)
                            for j in range(2):
                                if 2 * q + j:
                                    add = nc.vector.tensor_tensor(moe_sum[:, t, :], moe_sum[:, t, :], weak_sum[:, q, j * HID:(j + 1) * HID], ALU.add)
                                    if j == 1:
                                        chain.link(add)
                                    else:
                                        add.then_inc(weak_pair, 1)
                                        dve.wait_ge(weak_pair, l * T + (t + 1))
                    dve.wait_ge(gate_turned, l + 1)
                    nc.vector.tensor_copy(gate_t[:, :], g.wide(STRONG_BANK)[0:NEXP, :]).then_inc(gate_t_ready, 1)
                    for e in range(NS):
                        for t in range(T):
                            n = e * T + t
                            dve.wait_ge(strong_done, l * (NS * T) + (n + 1))
                            if e:
                                dve.wait_ge(strong_read, l * (NS * T) + (n - T + 1))
                            nc.vector.scalar_tensor_tensor(moe_sum[:, t, :], g.bank(STRONG_BANK + n % 2)[0:P, 0:HID], gate[:, t, NW + e:NW + e + 1],
                                                           moe_sum[:, t, :], ALU.mult, ALU.add).then_inc(strong_read, 1)
                    for t in range(T):
                        dve.wait_ge(bias_done, l * T + (t + 1))
                        dve.wait_ge(strong_read, l * (NS * T) + NS * T)
                        nc.vector.tensor_tensor(moe_sum[:, t, :], g.bank(WEAK_BANK + t % 2)[0:P, 0:HID], moe_sum[:, t, :], ALU.add).then_inc(bias_read, 1)
                    dve.wait_ge(bias_read, l * T + T)
                    for t in range(T):
                        last = nc.vector.scalar_tensor_tensor(h[:, t, :], moe_sum[:, t, :], conf[:, t:t + 1], h[:, t, :], ALU.mult, ALU.add)
                    last.then_inc(h_ready, 1)
                chain.leave(LAYERS)
                dve.wait_ge(turned, LAYERS + 1)
                nc.vector.tensor_copy(g.x_t[:, 1, :], g.wide(2)).then_inc(h_t_ready_v, 1)
                dve.wait_ge(y_done, 1)
                sums = psum[0:P, 0:T * 512].rearrange("p (t f) -> p t f", f=512)[:, :, 0:D]
                chain.link(nc.vector.tensor_tensor(g.res[:, :, :], sums, g.xa[:, :, :], ALU.add))
                g.layernorm_vector(chain, g.res, y, 4).then_inc(y_ready, 1)


_WEIGHTS_TURNED = ("L0_gnn_Wp1", "L0_gnn_Ws1", "L0_gnn_Wn1", "L0_gnn_Wp2", "L0_gnn_Ws2", "L0_gnn_Wn2")


def kernel(**inputs):
    import numpy as _np
    import concourse.bacc as _bacc
    from concourse import mybir as _mybir
    from concourse.bass_utils import run_bass_kernel_spmd as _run

    nc = _bacc.Bacc("TRN2", target_bir_lowering=False, num_devices=1)
    arrays, aps = {}, {}
    for name, value in inputs.items():
        v = _np.asarray(value)
        v = _np.ascontiguousarray(v.T if name in _WEIGHTS_TURNED else v)
        arrays[f"in_{name}"] = v
        aps[name] = nc.dram_tensor(f"in_{name}", v.shape, _mybir.dt.from_np(v.dtype), kind="ExternalInput").ap()
    out = nc.dram_tensor("out_x", (N, D), F32, kind="ExternalOutput").ap()
    build(nc, aps, out)
    r = _run(nc, [arrays], core_ids=[0])
    return r.results[0]["out_x"]
```

```python
from contextlib import ExitStack

import concourse.bass as bass
from concourse import mybir

N = 625
P = 125
T = N // P
E = 20625
CHUNKS = E // P
D = 128
FULL = 128
WIDE = 4 * P
EDGE = 512 - WIDE
HEADS = 4
HID = 256
GAT_SHAPES = ((1, HEADS, HID // HEADS), (2, HEADS, HID // HEADS), (2, 1, D))
LAYERS = 3
NEXP = 8
NW = 4
NS = 4
FF = 512
NEG_SLOPE = 0.2
BIG = 1.0e30
EPS = 1e-5

ALU = mybir.AluOpType
ACT = mybir.ActivationFunctionType
AX = mybir.AxisListType
F32 = mybir.dt.float32
BF16 = mybir.dt.bfloat16
F16 = mybir.dt.float16
I32 = mybir.dt.int32
ds = bass.ds

ROWS = ((0, WIDE), (WIDE, N))


class Chain:

    def __init__(self, eng, sem):
        self.eng, self.sem, self.done, self.loop = eng, sem, 0, 0

    def link(self, ins):
        self.done += 1
        ins.then_inc(self.sem, 1)
        self.eng.wait_ge(self.sem, self.loop + self.done)

    def enter(self, i, per_turn):
        self.start, self.per_turn = self.done, per_turn
        self.loop = i * per_turn

    def leave(self, turns):
        assert self.done - self.start == self.per_turn, self.done - self.start
        self.loop = 0
        self.done = self.start + turns * self.per_turn


class Program:
    pass


def build(nc, a, out):
    g = Program()
    g.a, g.out = a, out
    with ExitStack() as ctx:
        def sb(name, shape, dt=F32):
            return ctx.enter_context(nc.sbuf_tensor(name, shape, dt))

        def sem(name):
            return ctx.enter_context(nc.semaphore(name))

        g.psum = ctx.enter_context(nc.psum_tensor("psum", [FULL, 8 * 512], F32))

        def wide(b):
            return g.psum[:, b * 512 + EDGE:b * 512 + EDGE + N]

        def bank(b):
            return g.psum[:, b * 512:(b + 1) * 512]

        g.ident = sb("ident", [FULL, FULL])
        g.log_count_ready = sem("log_count_ready")
        g.ident_bf = sb("ident_bf", [FULL, FULL], BF16)
        g.ones = sb("ones", [FULL, FULL])
        g.count = sb("count", [P, T, N])
        g.count_t = sb("count_t", [P, T, N])
        g.has_edge_t = sb("has_edge_t", [P, T, N], BF16)
        g.log_count = sb("log_count", [P, T, N])
        g.no_edge_t = sb("no_edge_t", [P, T, N], BF16)
        g.degree = sb("degree", [P, T])
        g.recip_deg = sb("recip_deg", [P, T])
        g.some_edge = sb("some_edge", [P, T])
        g.run_end = sb("run_end", [P, T], I32)
        g.is_sorted = sb("is_sorted", [1, 1], I32)
        g.node_col = sb("node_col", [P, T])
        g.xa = sb("xa", [P, T, D])
        g.xb = sb("xb", [P, T, D])
        g.res = sb("res", [P, T, D])
        g.x_t = sb("x_t", [FULL, 2, N])
        g.ln_stats = sb("ln_stats", [P, T, 6])
        g.ln_mv = sb("ln_mv", [P, T, 2])
        g.ln_var = sb("ln_var", [P, T])
        g.ln_std = sb("ln_std", [P, T])
        g.ln_rstd = sb("ln_rstd", [P, T])

        g.w_sage = sb("w_sage", [FULL, 6, D])
        g.b_sage = sb("b_sage", [FULL, 3])
        g.b_sage2 = sb("b_sage2", [1, D])
        g.b_pool = sb("b_pool", [1, 2, D])
        g.w_gat = [sb(f"w_gat{i}", [FULL, kt, h * c + 2 * h]) for i, (kt, h, c) in enumerate(GAT_SHAPES)]
        g.att = [sb(f"att{i}", [FULL, 2, h * c]) for i, (kt, h, c) in enumerate(GAT_SHAPES)]
        g.b_gat = [sb(f"b_gat{i}", [P, HID if i < 2 else D]) for i in range(3)]
        g.w_in = sb("w_in", [FULL, HID])
        g.b_in = sb("b_in", [1, HID])
        g.w_router = sb("w_router", [FULL, LAYERS, 4, NEXP + 1])
        g.b_router = sb("b_router", [1, LAYERS, NEXP + 1])
        g.b_strong1 = sb("b_strong1", [FULL, LAYERS, NS, 4])
        g.b_strong2 = sb("b_strong2", [NEXP, LAYERS, HID])
        g.w_out = sb("w_out", [FULL, 2, D])
        g.b_out = sb("b_out", [1, D])

        g.edges_loaded = sem("edges_loaded")
        g.x_loaded = sem("x_loaded")
        g.sage_loaded = sem("sage_loaded")
        g.edges_spread = sem("edges_spread")
        g.gat_loaded = sem("gat_loaded")
        g.moe_loaded = sem("moe_loaded")
        g.weak_loaded = sem("weak_loaded")
        g.b_weak_loaded = sem("b_weak_loaded")
        g.strong_loaded = [sem(f"strong{e}_loaded") for e in range(NS)]
        g.consts_ready = sem("consts_ready")
        g.dve_chain = sem("dve_chain")
        g.ln_var_ready = sem("ln_var_ready")
        g.ln_std_ready = sem("ln_std_ready")

        def layernorm_vector(chain, r, y, k):
            for t in range(T):
                last = nc.vector.bn_stats(g.ln_stats[:, t, :], r[:, t, :])
            chain.link(last)
            for t in range(T):
                last = nc.vector.bn_aggr(g.ln_mv[:, t, :], g.ln_stats[:, t, :])
            chain.link(last)
            nc.vector.tensor_scalar(g.ln_var[:, :], g.ln_mv[:, :, 1], EPS, None, ALU.add).then_inc(g.ln_var_ready, 1)
            nc.vector.wait_ge(g.ln_std_ready, k)
            chain.link(nc.vector.reciprocal(g.ln_rstd[:, :], g.ln_std[:, :]))
            for t in range(T):
                last = nc.vector.tensor_scalar(y[:, t, :], r[:, t, :], g.ln_mv[:, t, 0:1], g.ln_rstd[:, t:t + 1],
                                               ALU.subtract, ALU.mult)
            return last

        def layernorm_scalar(k):
            nc.scalar.wait_ge(g.ln_var_ready, k)
            nc.scalar.activation(g.ln_std[:, :], g.ln_var[:, :], ACT.Sqrt).then_inc(g.ln_std_ready, 1)

        g.wide, g.bank = wide, bank
        g.layernorm_vector, g.layernorm_scalar = layernorm_vector, layernorm_scalar
        g.src_row = nc.dram_tensor("src_row", (E,), F16, kind="Internal").ap()
        g.keep_row = nc.dram_tensor("keep_row", (E + 1,), BF16, kind="Internal").ap()
        g.max_rows = nc.dram_tensor("max_rows", (E, D), F32, kind="Internal").ap()
        with ExitStack() as edges:
            g.src_all = edges.enter_context(nc.sbuf_tensor("src_all", [P, E], F16))
            g.keep_all = edges.enter_context(nc.sbuf_tensor("keep_all", [FULL, E], BF16))
            adjacency(nc, g)
            sage(nc, g)
        with ExitStack() as experts:
            def ex(name, shape):
                return experts.enter_context(nc.sbuf_tensor(name, shape, F32))

            g.w_weak = ex("w_weak", [FULL, 2, NW, HID])
            g.b_weak = ex("b_weak", [P, LAYERS, NW * HID])
            g.w_strong1 = ex("w_strong1", [FULL, NS, 2, FF])
            g.w_strong2 = ex("w_strong2", [FULL, NS, 4, HID])
            propagate(nc, g)
            gat(nc, g)
            moe(nc, g)


def adjacency(nc, g):
    a = g.a
    TURN = 5
    TURNS = CHUNKS // TURN
    assert TURNS * TURN == CHUNKS
    with ExitStack() as ctx:
        def sb(name, shape, dt=F32):
            return ctx.enter_context(nc.sbuf_tensor(name, shape, dt))

        def sem(name):
            return ctx.enter_context(nc.semaphore(name))

        ends_i = sb("ends_i", [P, 2, CHUNKS], I32)
        ends = sb("ends", [P, 2, CHUNKS])
        next_i = sb("next_i", [P, CHUNKS], I32)
        next_f = sb("next_f", [P, CHUNKS])
        src16 = sb("src16", [P, CHUNKS], F16)
        keep = sb("keep", [P, CHUNKS], BF16)
        zero16 = sb("zero16", [1, 2], BF16)
        falls = sb("falls", [P, CHUNKS])
        any_fall = sb("any_fall", [P, 1])
        tri = sb("adj_tri", [P, P])
        node_col_i = sb("node_col_i", [P, T], I32)
        before = sb("before", [P, T + 1])
        last_place = sb("last_place", [P, T])
        node_i = sb("node_i", [P, N], I32)
        node = sb("node", [P, N], F16)
        onehot = sb("onehot", [P, TURN, 2, N], BF16)
        att_prod = sb("att_prod", [FULL, 2, HID])
        nodes_ready = sem("nodes_ready")
        onehot_ready = sem("onehot_ready")
        onehot_used = sem("onehot_used")
        counts_ready = sem("counts_ready")
        counts_copied_v = sem("counts_copied_v")
        counts_copied_s = sem("counts_copied_s")
        turned = sem("turned")
        turned_copied_v = sem("turned_copied_v")
        turned_copied_s = sem("turned_copied_s")
        ident_zero = sem("ident_zero")
        next_zero = sem("next_zero")
        next_loaded = sem("next_loaded")
        edge_rows_ready = sem("edge_rows_ready")
        rows_written = sem("rows_written")
        tri_ready = sem("adj_tri_ready")
        degree_ready = sem("degree_ready")
        ends_done = sem("ends_done")
        fall_ready = sem("fall_ready")
        pool_chain = sem("pool_chain")
        psum = g.psum

        def row_main(t):
            return psum[0:P, t * 512 + EDGE:(t + 1) * 512]

        def row_rest(t):
            b, k = (5, t) if t < 4 else (6, 0)
            return psum[0:P, b * 512 + EDGE + P * k:b * 512 + EDGE + P * (k + 1)]

        with nc.Block() as block:
            @block.sync
            def _(sp):
                for i, name in enumerate(("src", "dst")):
                    sp.dma_start(ends_i[:, i, :], a[name].rearrange("(p c) -> p c", c=CHUNKS)).then_inc(g.edges_loaded, 16)
                sp.wait_ge(next_zero, 1)
                sp.dma_start(next_i[0:P - 1, :], a["dst"][1:E - CHUNKS + 1].rearrange("(p c) -> p c", c=CHUNKS)).then_inc(next_loaded, 16)
                sp.dma_start(next_i[P - 1:P, 0:CHUNKS - 1], a["dst"][E - CHUNKS + 1:E].rearrange("(o c) -> o c", o=1)).then_inc(next_loaded, 16)
                sp.dma_start(g.xa[:, :, :], a["x"].rearrange("(t p) f -> p t f", p=P)).then_inc(g.x_loaded, 16)
                for i, name in enumerate(("Wp1", "Ws1", "Wn1", "Wp2", "Ws2", "Wn2")):
                    sp.dma_start(g.w_sage[:, i, :], a["L0_gnn_" + name]).then_inc(g.sage_loaded, 16)
                for i, name in enumerate(("bp1", "b1", "bp2")):
                    sp.dma_start(g.b_sage[:, i:i + 1], a["L0_gnn_" + name].rearrange("(p o) -> p o", o=1)).then_inc(g.sage_loaded, 16)
                for i, name in enumerate(("bp1", "bp2")):
                    sp.dma_start(g.b_pool[:, i, :], a["L0_gnn_" + name].rearrange("(o f) -> o f", o=1)).then_inc(g.sage_loaded, 16)
                sp.dma_start(g.b_sage2[:, :], a["L0_gnn_b2"].rearrange("(o f) -> o f", o=1)).then_inc(g.sage_loaded, 16)
                for i, (kt, h, c) in enumerate(GAT_SHAPES):
                    sp.dma_start(g.w_gat[i][:, :, 0:h * c], a[f"L2_gnn_W{i}"].rearrange("(k p) f -> p k f", p=FULL)).then_inc(g.gat_loaded, 16)
                    for j, side in enumerate(("src", "dst")):
                        vec = a[f"L2_gnn_a_{side}{i}"].rearrange("h c -> (h c)")
                        sp.dma_start(g.att[i][:, j, :], vec.partition_broadcast(FULL)).then_inc(g.gat_loaded, 16)
                    sp.dma_start(g.b_gat[i][:, :], a[f"L2_gnn_b{i}"].partition_broadcast(P)).then_inc(g.gat_loaded, 16)

            @block.gpsimd
            def _(pool):
                pool.iota(node_i[:, :], pattern=[[1, N]], base=0, channel_multiplier=0).then_inc(nodes_ready, 1)
                pool.iota(node_col_i[:, :], pattern=[[P, T]], base=0, channel_multiplier=1).then_inc(nodes_ready, 1)
                pool.memset(tri[:, :], 1.0).then_inc(tri_ready, 1)
                pool.wait_ge(tri_ready, 1)
                pool.affine_select(out=tri[:, :], in_=tri[:, :], compare_op=ALU.is_ge, fill=0.0, base=0,
                                   pattern=[[1, P]], channel_multiplier=-1).then_inc(tri_ready, 1)
                pool.memset(g.ident[:, :], 0.0).then_inc(ident_zero, 1)
                pool.memset(g.ones[:, :], 1.0).then_inc(g.consts_ready, 1)
                pool.wait_ge(ident_zero, 1)
                pool.affine_select(out=g.ident[:, :], in_=g.ident[:, :], compare_op=ALU.not_equal, fill=1.0,
                                   base=0, pattern=[[-1, FULL]], channel_multiplier=1).then_inc(g.consts_ready, 1)
                pool.wait_ge(g.consts_ready, 2)
                pool.tensor_copy(g.ident_bf[:, :], g.ident[:, :]).then_inc(g.consts_ready, 1)
                pool.memset(g.w_router[:, :, :, :], 0.0).then_inc(g.consts_ready, 1)
                pool.memset(g.b_strong2[:, :, :], 0.0).then_inc(g.consts_ready, 1)
                pool.wait_ge(g.consts_ready, 5)
                with nc.allow_non_contiguous_dma(reason="small weights, once"):
                    for l in range(LAYERS):
                        pool.dma_start(g.w_router[:, l, :, 0:NEXP], a["L3_gnn_router_W"][l].rearrange("(k p) e -> p k e", p=FULL)).then_inc(g.moe_loaded, 16)
                        pool.dma_start(g.w_router[:, l, 0:2, NEXP:NEXP + 1], a["L3_gnn_conf_W"][l].rearrange("(k p) e -> p k e", p=FULL)).then_inc(g.moe_loaded, 16)
                        pool.dma_start(g.b_strong1[:, l, :, :], a["L3_gnn_strong_b1"][l].rearrange("e (k p) -> p e k", p=FULL)).then_inc(g.moe_loaded, 16)
                    pool.dma_start(g.b_router[:, :, 0:NEXP], a["L3_gnn_router_b"].rearrange("(o l) e -> o l e", o=1)).then_inc(g.moe_loaded, 16)
                    pool.dma_start(g.b_router[:, :, NEXP:NEXP + 1], a["L3_gnn_conf_b"].rearrange("(o l) e -> o l e", o=1)).then_inc(g.moe_loaded, 16)
                    pool.dma_start(g.b_strong2[NW:NEXP, :, :], a["L3_gnn_strong_b2"].rearrange("l e f -> e l f")).then_inc(g.moe_loaded, 16)
                    pool.dma_start(g.w_in[:, :], a["L3_gnn_W_in"]).then_inc(g.moe_loaded, 16)
                    pool.dma_start(g.b_in[:, :], a["L3_gnn_b_in"].rearrange("(o f) -> o f", o=1)).then_inc(g.moe_loaded, 16)
                    pool.dma_start(g.w_out[:, :, :], a["L3_gnn_W_out"].rearrange("(k p) f -> p k f", p=FULL)).then_inc(g.moe_loaded, 16)
                    pool.dma_start(g.b_out[:, :], a["L3_gnn_b_out"].rearrange("(o f) -> o f", o=1)).then_inc(g.moe_loaded, 16)
                pool.wait_ge(counts_copied_v, 4)
                pool.wait_ge(counts_copied_s, 3)
                pool.tensor_copy(g.log_count[:, :, :], g.count[:, :, :]).then_inc(pool_chain, 1)
                pool.wait_ge(pool_chain, 1)
                for t in range(T):
                    block_t = g.log_count[:, t, t * P:(t + 1) * P]
                    last = pool.tensor_tensor(block_t, block_t, g.ident[0:P, 0:P], ALU.add)
                last.then_inc(pool_chain, 1)

            @block.scalar
            def _(act):
                act.wait_ge(edge_rows_ready, 2)
                act.dma_start(g.src_row.rearrange("(p c) -> p c", c=CHUNKS), src16[:, :]).then_inc(rows_written, 16)
                act.dma_start(g.keep_row[1:E + 1].rearrange("(p c) -> p c", c=CHUNKS), keep[:, :]).then_inc(rows_written, 16)
                act.dma_start(g.keep_row[0:1].rearrange("(o c) -> o c", o=1), zero16[:, 0:1]).then_inc(rows_written, 16)
                act.wait_ge(rows_written, 48)
                act.dma_start(g.src_all[:, :], g.src_row.partition_broadcast(P)).then_inc(g.edges_spread, 16)
                act.dma_start(g.keep_all[:, :], g.keep_row[0:E].partition_broadcast(FULL)).then_inc(g.edges_spread, 16)
                act.wait_ge(counts_ready, 1)
                for t in range(3):
                    nc.scalar.copy(g.count[:, t, 0:WIDE], row_main(t)).then_inc(counts_copied_s, 1)
                act.wait_ge(turned, 1)
                for t in range(3):
                    nc.scalar.copy(g.count_t[:, t, 0:WIDE], row_main(t)).then_inc(turned_copied_s, 1)

            @block.tensor
            def _(pe):
                def chunk(k, ready, start, stop):
                    pe.wait_ge(onehot_ready, ready)
                    for s in range(T):
                        lhs = onehot[:, k, 0, s * P:(s + 1) * P]
                        nc.tensor.matmul(row_main(s), lhs, onehot[:, k, 1, 0:WIDE], start=start, stop=stop,
                                         skip_group_check=True)
                        last = nc.tensor.matmul(row_rest(s), lhs, onehot[:, k, 1, WIDE:N],
                                                start=start and s in (0, 4), stop=stop, skip_group_check=True)
                    return last

                for k in range(TURN):
                    chunk(k, k + 1, k == 0, False).then_inc(onehot_used, 1)
                with pe.Fori(1, TURNS - 1) as i:
                    for k in range(TURN):
                        chunk(k, i * TURN + k + 1, False, False).then_inc(onehot_used, 1)
                for k in range(TURN):
                    last = chunk(k, CHUNKS - TURN + k + 1, False, k == TURN - 1)
                last.then_inc(counts_ready, 1)
                pe.wait_ge(counts_copied_v, 4)
                pe.wait_ge(counts_copied_s, 3)
                pe.wait_ge(g.consts_ready, 2)
                for d in range(T):
                    for s in range(T):
                        to = row_main(d)[:, s * P:(s + 1) * P] if s < 4 else row_rest(d)
                        last = nc.tensor.transpose(to, g.count[:, s, d * P:(d + 1) * P], g.ident[0:P, 0:P])
                last.then_inc(turned, 1)
                pe.wait_ge(degree_ready, 1)
                pe.wait_ge(tri_ready, 2)
                nc.tensor.matmul(g.bank(7)[0:P, 0:T], tri[:, :], g.degree[:, :], start=True, stop=False)
                nc.tensor.matmul(g.bank(7)[0:P, 0:T], g.ones[0:P, 0:P], before[:, 0:T], start=False, stop=True)
                nc.tensor.matmul(g.bank(7)[0:P, 16:17], g.ones[0:P, 0:P], any_fall[:, :], start=True, stop=True).then_inc(ends_done, 1)

            @block.vector
            def _(dve):
                chain = Chain(dve, g.dve_chain)
                nc.vector.memset(next_i[:, :], 1 << 20).then_inc(next_zero, 1)
                nc.vector.memset(zero16[:, :], 0.0)
                dve.wait_ge(nodes_ready, 2)
                nc.vector.tensor_copy(node[:, :], node_i[:, :])
                nc.vector.tensor_copy(g.node_col[:, :], node_col_i[:, :])
                dve.wait_ge(g.edges_loaded, 32)
                chain.link(nc.vector.tensor_copy(ends[:, :, :], ends_i[:, :, :]))
                nc.vector.tensor_copy(src16[:, :], ends[:, 0, :]).then_inc(edge_rows_ready, 1)
                dve.wait_ge(next_loaded, 32)
                chain.link(nc.vector.tensor_copy(next_f[:, :], next_i[:, :]))
                nc.vector.tensor_tensor(keep[:, :], next_f[:, :], ends[:, 1, :], ALU.is_equal).then_inc(edge_rows_ready, 1)
                chain.link(nc.vector.tensor_tensor(falls[:, :], next_f[:, :], ends[:, 1, :], ALU.is_lt))
                chain.link(nc.vector.tensor_reduce(any_fall[:, :], falls[:, :], AX.X, ALU.max))

                def chunk(k, c):
                    for side in range(2):
                        last = nc.vector.tensor_scalar(onehot[:, k, side, :], node[:, :], ends[:, side, ds(c, 1)],
                                                       None, ALU.is_equal)
                    last.then_inc(onehot_ready, 1)

                for k in range(TURN):
                    chunk(k, k)
                with dve.Fori(1, TURNS) as i:
                    for k in range(TURN):
                        dve.wait_ge(onehot_used, (i - 1) * TURN + k + 1)
                        chunk(k, i * TURN + k)
                dve.wait_ge(g.gat_loaded, 16 * 12)
                for i, (kt, h, c) in enumerate(GAT_SHAPES):
                    for side in range(2):
                        to = att_prod[:, 0:kt, 0:h * c]
                        chain.link(nc.vector.tensor_tensor(to, g.w_gat[i][:, :, 0:h * c],
                                                           g.att[i][:, side, :].unsqueeze(1).broadcast_to([FULL, kt, h * c]), ALU.mult))
                        at = h * c + side * h
                        chain.link(nc.vector.tensor_reduce(g.w_gat[i][:, :, at:at + h], to.rearrange("p k (h c) -> p k h c", h=h), AX.X, ALU.add))
                dve.wait_ge(counts_ready, 1)
                rests = psum[0:P, 5 * 512 + EDGE:6 * 512].rearrange("p (t n) -> p t n", n=P)

                def copy_rows(to, copied):
                    for t in (3, 4):
                        nc.vector.tensor_copy(to[:, t, 0:WIDE], row_main(t)).then_inc(copied, 1)
                    nc.vector.tensor_copy(to[:, 0:4, WIDE:N], rests).then_inc(copied, 1)
                    nc.vector.tensor_copy(to[:, 4, WIDE:N], row_rest(4)).then_inc(copied, 1)

                copy_rows(g.count, counts_copied_v)
                dve.wait_ge(turned, 1)
                copy_rows(g.count_t, turned_copied_v)
                dve.wait_ge(turned_copied_v, 4)
                dve.wait_ge(turned_copied_s, 3)
                nc.vector.tensor_scalar(g.has_edge_t[:, :, :], g.count_t[:, :, :], 1.0, None, ALU.min)
                nc.vector.tensor_scalar(g.no_edge_t[:, :, :], g.count_t[:, :, :], 0.0, -BIG, ALU.is_le, ALU.mult)
                nc.vector.memset(before[:, 0:1], 0.0)
                chain.link(nc.vector.tensor_reduce(g.degree[:, :], g.count_t[:, :, :], AX.X, ALU.add))
                for t in range(T):
                    chain.link(nc.vector.tensor_tensor(before[:, t + 1:t + 2], before[:, t:t + 1], g.degree[:, t:t + 1], ALU.add))
                nc.vector.tensor_scalar(g.some_edge[:, :], g.degree[:, :], 1.0, None, ALU.min).then_inc(degree_ready, 1)
                chain.link(nc.vector.tensor_scalar(g.recip_deg[:, :], g.degree[:, :], 1.0, None, ALU.max))
                nc.vector.reciprocal(g.recip_deg[:, :], g.recip_deg[:, :])
                for t in range(T):
                    block_t = g.no_edge_t[:, t, t * P:(t + 1) * P]
                    last = nc.vector.scalar_tensor_tensor(block_t, g.ident[0:P, 0:P], 0.0, block_t, ALU.is_equal, ALU.mult)
                chain.link(last)
                dve.wait_ge(ends_done, 1)
                chain.link(nc.vector.tensor_scalar(last_place[:, :], g.bank(7)[0:P, 0:T], -1.0, 0.0, ALU.add, ALU.max))
                nc.vector.tensor_copy(g.run_end[:, :], last_place[:, :])
                chain.link(nc.vector.tensor_scalar(g.is_sorted[:, :], g.bank(7)[0:1, 16:17], 0.0, None, ALU.is_le))
                g.dve_links = chain.done


def sage(nc, g):
    FIRST = 1
    BODY = 4
    TURNS = (P - FIRST) // BODY
    RING = 4
    GROUPS = E // N
    AHEAD = 3
    assert GROUPS * N == E and (GROUPS - AHEAD) % 2 == 0
    with ExitStack() as ctx:
        def sb(name, shape, dt=F32):
            return ctx.enter_context(nc.sbuf_tensor(name, shape, dt))

        def sem(name):
            return ctx.enter_context(nc.semaphore(name))

        far = sb("far", [P, T, N], BF16)
        agg_t = sb("agg_t", [FULL, T, P])
        staged = sb("staged", [FULL, T, BODY])
        pool_n = sb("pool_n", [P, T, D])
        parts = sb("parts", [P, 3, T, D], BF16)
        hot_all = sb("src_hot", [FULL, 2, T, N], BF16)
        src_hot = hot_all[0:P]
        masked = hot_all[:, 0, 0:RING, :]
        running = sb("running", [FULL, 2, N])
        pool_t = running[:, 0, :]
        rows = sb("rows", [P, 2, T, D])
        agg_n = sb("agg_n", [P, T, D])
        far_ready = sem("far_ready")
        count_floored = sem("count_floored")
        log_ready = sem("log_ready")
        turned = sem("sage_turned")
        x_t_ready = sem("sage_x_t_ready")
        agg_ready = sem("agg_ready")
        summed = sem("sage_summed")
        pooled = sem("pooled")
        pool_ready = sem("pool_ready")
        row_ready = sem("row_ready")
        row_used = sem("row_used")
        row_seen = sem("row_seen")
        any_chain = sem("any_chain")
        pooled_n = sem("pooled_n")
        pool_n_ready = sem("pool_n_ready")
        parts_chain = sem("parts_chain")
        parts_ready = sem("parts_ready")
        hot_ready = sem("hot_ready")
        messages_ready = sem("messages_ready")
        running_ready = sem("running_ready")
        running_turned = sem("running_turned")
        rows_copied = sem("rows_copied")
        rows_stored = [sem(f"rows{k}_stored") for k in range(2)]
        agg_fetched = sem("agg_fetched")
        agg_masked = sem("agg_masked")
        agg_turned = sem("agg_turned")
        psum = g.psum

        def row(k):
            return g.wide(2 * (k % RING))

        def messages(n):
            return g.wide(2 * (n % 2))

        def turned_rows(n):
            b = 4 + 2 * (n % 2)
            return psum[0:P, b * 512:b * 512 + T * D]

        def wait_past(eng, semaphore, value):
            if not isinstance(value, int) or value > 0:
                eng.wait_ge(semaphore, value)

        def over_groups(eng, step):
            for n in range(AHEAD):
                step(n, n, n // 2)
            with eng.Fori(0, (GROUPS - AHEAD) // 2) as i:
                for n in range(AHEAD, AHEAD + 2):
                    step(n, i * 2 + n, i + n // 2)

        def stores(layer, parity):
            return layer * ((GROUPS + 1 - parity) // 2)

        with nc.Block() as block:
            @block.tensor
            def _(pe):
                by_runs = pe.value_load(g.is_sorted[0:1, 0:1], min_val=0, max_val=1)

                def any_order(layer, wp):
                    base = layer * N
                    for lo, hi in ROWS:
                        last = nc.tensor.matmul(g.wide(2)[:, lo:hi], wp, g.x_t[:, 0, lo:hi], start=True, stop=True)
                    last.then_inc(pooled, 1)
                    pe.wait_ge(pool_ready, layer + 1)

                    def spread(k, p, t):
                        lhs = g.ident_bf[0:P, ds(p, 1)].broadcast_to([P, FULL])
                        for lo, hi in ROWS:
                            last = nc.tensor.matmul(row(k)[:, lo:hi], lhs, g.has_edge_t[:, t, lo:hi], start=True, stop=True)
                        last.then_inc(row_ready, 1)

                    for t in range(T):
                        wait_past(pe, row_used, base + t - RING + 1)
                        spread(base + t, 0, t)
                    with pe.Fori(0, TURNS) as i:
                        for j in range(BODY):
                            for t in range(T):
                                k = base + T * FIRST + j * T + t
                                pe.wait_ge(row_used, i * (BODY * T) + (k - RING + 1))
                                spread(k, i * BODY + (FIRST + j), t)

                def sorted_runs(layer, wp):
                    base = layer * GROUPS
                    for t in range(T):
                        to = g.bank(t)[0:P, 0:D]
                        nc.tensor.matmul(to, g.x_t[:, 0, t * P:(t + 1) * P], wp, start=True, stop=False)
                        last = nc.tensor.matmul(to, g.ones[0:1, 0:P], g.b_pool[:, layer, :], start=False, stop=True)
                    last.then_inc(pooled_n, 1)
                    pe.wait_ge(parts_ready, layer + 1)

                    def fetch(n, group):
                        pe.wait_ge(hot_ready, base + group + 1)
                        wait_past(pe, running_ready, base + group - 1)
                        for lo, hi in ROWS:
                            for k in range(3 * T):
                                part, s = k % 3, k // 3
                                last = nc.tensor.matmul(messages(n)[:, lo:hi], parts[:, part, s, :], src_hot[:, n % 2, s, lo:hi],
                                                        start=k == 0, stop=k == 3 * T - 1)
                        last.then_inc(messages_ready, 1)

                    def turn(n, group):
                        pe.wait_ge(running_ready, base + group + 1)
                        wait_past(pe, rows_copied, base + group - 1)
                        for j in range(T):
                            last = nc.tensor.transpose(turned_rows(n)[:, j * D:(j + 1) * D], running[:, n % 2, j * P:(j + 1) * P],
                                                       g.ident[:, :])
                        last.then_inc(running_turned, 1)

                    def step(n, group, pair):
                        fetch(n, group)
                        if isinstance(group, int) and group == 0:
                            return
                        turn(n + 1, group - 1)

                    over_groups(pe, step)
                    turn(GROUPS - 1, GROUPS - 1)
                    pe.wait_ge(agg_masked, layer + 1)
                    for t in range(T):
                        last = nc.tensor.transpose(g.wide(0)[:, t * P:(t + 1) * P], agg_n[:, t, :], g.ident[0:P, 0:P])
                    last.then_inc(agg_turned, 1)

                pe.wait_ge(g.x_loaded, 16)
                for t in range(T):
                    last = nc.tensor.transpose(g.wide(0)[:, t * P:(t + 1) * P], g.xa[:, t, :], g.ident[0:P, 0:P])
                last.then_inc(turned, 1)
                pe.wait_ge(g.sage_loaded, 16 * 12)
                for layer in range(2):
                    wp, ws, wn = (g.w_sage[:, 3 * layer + i, :] for i in range(3))
                    pe.wait_ge(x_t_ready, layer + 1)
                    with pe.If(by_runs != 0):
                        sorted_runs(layer, wp)
                    with pe.Else():
                        any_order(layer, wp)
                    pe.wait_ge(agg_ready, layer + 1)
                    if layer == 0:
                        for lo, hi in ROWS:
                            nc.tensor.matmul(g.wide(0)[:, lo:hi], ws, g.x_t[:, 0, lo:hi], start=True, stop=False)
                            last = nc.tensor.matmul(g.wide(0)[:, lo:hi], wn, agg_t[:, :, :].rearrange("f t p -> f (t p)")[:, lo:hi],
                                                    start=False, stop=True)
                        last.then_inc(summed, 1)
                    else:
                        for t in range(T):
                            to = g.bank(t)[0:P, 0:D]
                            nc.tensor.matmul(to, g.x_t[:, 0, t * P:(t + 1) * P], ws, start=True, stop=False)
                            nc.tensor.matmul(to, agg_t[:, t, :], wn, start=False, stop=False)
                            last = nc.tensor.matmul(to, g.ones[0:1, 0:P], g.b_sage2[:, :], start=False, stop=True)
                        last.then_inc(summed, 1)

            @block.scalar
            def _(act):
                by_runs = act.value_load(g.is_sorted[0:1, 0:1], min_val=0, max_val=1)

                def any_order(layer):
                    act.wait_ge(pooled, layer + 1)
                    nc.scalar.activation(pool_t[:, :], g.wide(2), ACT.Relu, bias=g.b_sage[:, 2 * layer:2 * layer + 1]).then_inc(pool_ready, 1)

                def sorted_runs(layer):
                    base = layer * GROUPS
                    act.wait_ge(pooled_n, layer + 1)
                    nc.scalar.activation(pool_n[:, :, :], psum[0:P, 0:T * 512].rearrange("p (t f) -> p t f", f=512)[:, :, 0:D],
                                         ACT.Relu).then_inc(pool_n_ready, 1)

                    def step(n, group, pair):
                        act.wait_ge(running_turned, base + group + 1)
                        wait_past(act, rows_stored[n % 2], (pair + stores(layer, n % 2)) * 16)
                        nc.scalar.copy(rows[:, n % 2, :, :].rearrange("p j f -> p (j f)"), turned_rows(n)).then_inc(rows_copied, 1)

                    over_groups(act, step)
                    act.wait_ge(agg_turned, layer + 1)
                    nc.scalar.copy(agg_t[:, :, :].rearrange("f t p -> f (t p)"), g.wide(0)).then_inc(agg_ready, 1)

                act.wait_ge(turned, 1)
                nc.scalar.copy(g.x_t[:, 0, :], g.wide(0)).then_inc(x_t_ready, 1)
                act.wait_ge(g.sage_loaded, 16 * 12)
                for layer in range(2):
                    with act.If(by_runs != 0):
                        sorted_runs(layer)
                    with act.Else():
                        any_order(layer)
                    if layer == 0:
                        act.wait_ge(summed, 1)
                        nc.scalar.activation(g.x_t[:, 0, :], g.wide(0), ACT.Relu, bias=g.b_sage[:, 1:2]).then_inc(x_t_ready, 1)
                act.wait_ge(count_floored, 1)
                nc.scalar.activation(g.log_count[:, :, :], g.log_count[:, :, :], ACT.Ln).then_inc(log_ready, 1)
                g.layernorm_scalar(1)

            @block.sync
            def _(sp):
                by_runs = sp.value_load(g.is_sorted[0:1, 0:1], min_val=0, max_val=1)
                max_rows = g.max_rows.rearrange("(o j p) f -> p o j f", p=P, j=T)

                def sorted_runs(layer):
                    base = layer * GROUPS
                    if layer:
                        sp.wait_ge(agg_fetched, 16 * T * layer)

                    def step(n, group, pair):
                        sp.wait_ge(rows_copied, base + group + 1)
                        sp.dma_start(max_rows[:, ds(group, 1), :, :].rearrange("p o j f -> p (o j) f"), rows[:, n % 2, :, :]).then_inc(rows_stored[n % 2], 16)

                    over_groups(sp, step)

                for layer in range(2):
                    with sp.If(by_runs != 0):
                        sorted_runs(layer)
                sp.wait_ge(g.x_loaded, 16)

            @block.gpsimd
            def _(pool):
                by_runs = pool.value_load(g.is_sorted[0:1, 0:1], min_val=0, max_val=1)

                def sorted_runs(layer):
                    for parity in range(2):
                        pool.wait_ge(rows_stored[parity], 16 * stores(layer + 1, parity))
                    if layer:
                        pool.wait_ge(agg_turned, layer)
                    for t in range(T):
                        pool.indirect_dma_start(out=agg_n[:, t, :], out_offset=None, in_=g.max_rows,
                                                in_offset=bass.IndirectOffsetOnAxis(ap=g.run_end[:, t:t + 1], axis=0)).then_inc(agg_fetched, 16)

                pool.tensor_scalar(far[:, :, :], g.log_count[:, :, :], 0.0, -BIG, ALU.is_le, ALU.mult).then_inc(far_ready, 1)
                pool.wait_ge(far_ready, 1)
                pool.tensor_scalar(g.log_count[:, :, :], g.log_count[:, :, :], 1.0, None, ALU.max).then_inc(count_floored, 1)
                for layer in range(2):
                    with pool.If(by_runs != 0):
                        sorted_runs(layer)
                pool.wait_ge(log_ready, 1)
                pool.tensor_tensor(g.log_count[:, :, :], g.log_count[:, :, :], far[:, :, :], ALU.add).then_inc(g.log_count_ready, 1)
                pool.wait_ge(g.x_loaded, 16)

            @block.vector
            def _(dve):
                by_runs = dve.value_load(g.is_sorted[0:1, 0:1], min_val=0, max_val=1)
                chain = Chain(dve, g.dve_chain)
                chain.done = g.dve_links
                local = Chain(dve, any_chain)
                split = Chain(dve, parts_chain)
                dve.wait_ge(g.edges_spread, 32)

                def any_order(layer):
                    base = layer * N
                    dve.wait_ge(pool_ready, layer + 1)

                    def top(k, ready, to):
                        if ready is not None:
                            dve.wait_ge(row_ready, ready)
                            dve.sem_inc(row_seen, 1)
                        nc.vector.tensor_tensor_reduce(out=masked[:, k % RING, :], in0=row(k), in1=pool_t[:, :], scale=1.0, scalar=0.0,
                                                       op0=ALU.mult, op1=ALU.max, accum_out=to).then_inc(row_used, 1)

                    for t in range(T):
                        top(base + t, base + t + 1, staged[:, t, 0:1])
                    dve.wait_ge(row_used, base + T)
                    local.link(nc.vector.tensor_copy(agg_t[:, :, 0:1], staged[:, :, 0:1]))
                    with dve.Fori(0, TURNS) as i:
                        local.enter(i, 1)
                        for j in range(BODY):
                            for t in range(T):
                                k = base + T * FIRST + j * T + t
                                top(k, i * (BODY * T) + (k + 2) if (j * T + t) % 2 == 0 else None, staged[:, t, j:j + 1])
                        dve.wait_ge(row_used, i * (BODY * T) + (base + T * FIRST + BODY * T))
                        local.link(nc.vector.tensor_copy(agg_t[:, :, ds(i * BODY + FIRST, BODY)], staged[:, :, :]))
                    local.leave(TURNS)
                    nc.vector.engine_nop().then_inc(agg_ready, 1)

                def sorted_runs(layer):
                    base = layer * GROUPS
                    dve.wait_ge(pool_n_ready, layer + 1)
                    split.link(nc.vector.tensor_copy(parts[:, 0, :, :], pool_n[:, :, :]))
                    split.link(nc.vector.tensor_tensor(pool_n[:, :, :], pool_n[:, :, :], parts[:, 0, :, :], ALU.subtract))
                    split.link(nc.vector.tensor_copy(parts[:, 1, :, :], pool_n[:, :, :]))
                    nc.vector.tensor_tensor(parts[:, 2, :, :], pool_n[:, :, :], parts[:, 1, :, :], ALU.subtract).then_inc(parts_ready, 1)

                    def one_hot(n, group):
                        wait_past(dve, messages_ready, base + group - 1)
                        for t in range(T):
                            last = nc.vector.tensor_scalar(src_hot[:, n % 2, t, :], g.src_all[:, ds(group * N, N)], g.node_col[:, t:t + 1],
                                                           None, ALU.is_equal)
                        last.then_inc(hot_ready, 1)

                    def scan(n, group):
                        dve.wait_ge(messages_ready, base + group + 1)
                        wait_past(dve, running_turned, base + group - 1)
                        wait_past(dve, running_ready, base + group)
                        first = isinstance(group, int) and group == 0
                        nc.vector.tensor_tensor_scan(running[:, n % 2, :], g.keep_all[:, ds(group * N, N)], messages(n),
                                                     0.0 if first else running[:, (n + 1) % 2, N - 1:N], ALU.mult, ALU.max).then_inc(running_ready, 1)

                    def step(n, group, pair):
                        one_hot(n, group)
                        if isinstance(group, int) and group == 0:
                            return
                        scan(n + 1, group - 1)

                    over_groups(dve, step)
                    scan(GROUPS - 1, GROUPS - 1)
                    dve.wait_ge(agg_fetched, 16 * T * (layer + 1))
                    nc.vector.tensor_tensor(agg_n[:, :, :], agg_n[:, :, :], g.some_edge[:, :].unsqueeze(2).broadcast_to([P, T, D]),
                                            ALU.mult).then_inc(agg_masked, 1)

                for layer in range(2):
                    with dve.If(by_runs != 0):
                        sorted_runs(layer)
                    with dve.Else():
                        any_order(layer)
                dve.wait_ge(summed, 2)
                sums = psum[0:P, 0:T * 512].rearrange("p (t f) -> p t f", f=512)[:, :, 0:D]
                chain.link(nc.vector.tensor_tensor(g.res[:, :, :], sums, g.xa[:, :, :], ALU.add))
                chain.link(g.layernorm_vector(chain, g.res, g.xa, 1))
                g.dve_links = chain.done


def propagate(nc, g):
    with ExitStack() as ctx:
        def sb(name, shape, dt=F32):
            return ctx.enter_context(nc.sbuf_tensor(name, shape, dt))

        def sem(name):
            return ctx.enter_context(nc.semaphore(name))

        diag = sb("deg_diag", [P, T, P])
        diag_ready = sem("deg_diag_ready")
        spread = sem("deg_spread")
        summed = sem("prop_summed")
        psum = g.psum
        with nc.Block() as block:
            @block.sync
            def _(sp):
                w1 = g.a["L3_gnn_strong_W1"][0].rearrange("e (k p) f -> p e k f", p=FULL)
                w2 = g.a["L3_gnn_strong_W2"][0].rearrange("e (k p) f -> p e k f", p=FULL)
                for k in range(2):
                    sp.dma_start(g.w_weak[:, k, :, :], g.a["L3_gnn_weak_W"][0, :, k * FULL:(k + 1) * FULL, :].rearrange("e p f -> p e f")).then_inc(g.weak_loaded, 16)
                for e in range(NS):
                    sp.dma_start(g.w_strong1[:, e, :, :], w1[:, e, :, :]).then_inc(g.strong_loaded[e], 16)
                    sp.dma_start(g.w_strong2[:, e, :, :], w2[:, e, :, :]).then_inc(g.strong_loaded[e], 16)
                sp.dma_start(g.b_weak[:, :, :], g.a["L3_gnn_weak_b"].rearrange("l e f -> l (e f)").partition_broadcast(P)).then_inc(g.b_weak_loaded, 16)

            @block.gpsimd
            def _(pool):
                pool.tensor_tensor(diag[:, :, :], g.ident[0:P, 0:P].unsqueeze(1).broadcast_to([P, T, P]),
                                   g.recip_deg[:, :].unsqueeze(2).broadcast_to([P, T, P]), ALU.mult).then_inc(diag_ready, 1)

            @block.tensor
            def _(pe):
                for s in range(T):
                    for d in range(T):
                        last = nc.tensor.matmul(g.bank(s)[0:P, 0:D], g.count_t[:, d, s * P:(s + 1) * P], g.xa[:, d, :],
                                                start=d == 0, stop=d == T - 1)
                last.then_inc(summed, 1)
                pe.wait_ge(diag_ready, 1)
                for t in range(T):
                    last = nc.tensor.matmul(g.wide(5)[0:P, t * P:(t + 1) * P], g.ones[0:P, 0:P], diag[:, t, :], start=True, stop=True)
                last.then_inc(spread, 1)

            @block.scalar
            def _(act):
                g.layernorm_scalar(2)

            @block.vector
            def _(dve):
                chain = Chain(dve, g.dve_chain)
                chain.done = g.dve_links
                dve.wait_ge(summed, 1)
                sums = psum[0:P, 0:T * 512].rearrange("p (t f) -> p t f", f=512)[:, :, 0:D]
                chain.link(nc.vector.tensor_tensor(g.res[:, :, :], sums, g.xa[:, :, :], ALU.add))
                chain.link(g.layernorm_vector(chain, g.res, g.xb, 2))
                dve.wait_ge(spread, 1)
                for t in range(T):
                    last = nc.vector.tensor_tensor(g.count[:, t, :], g.count[:, t, :], g.wide(5)[0:P, :], ALU.mult)
                chain.link(last)
                g.dve_links = chain.done


def gat(nc, g):
    SHAPES = GAT_SHAPES
    LOW_AHEAD = 2
    SMAX, ATT, OUT = 0, 2, 6
    with ExitStack() as ctx:
        def sb(name, shape, dt=F32):
            return ctx.enter_context(nc.sbuf_tensor(name, shape, dt))

        def sem(name):
            return ctx.enter_context(nc.semaphore(name))

        feats = [sb("feats4", [P, T, HEADS, HID // HEADS + 1]), sb("feats1", [P, T, 1, D + 1])]
        src_score = sb("src_score", [P, T, HEADS])
        src_low = sb("src_low", [P, T, HEADS])
        dst_score = sb("dst_score", [P, T, HEADS])
        top = sb("top", [P, T])
        high_row = sb("high_row", [P, T])
        low_row = sb("low_row", [P, T])
        masked = sb("gat_masked", [P, T, N], BF16)
        src_col = sb("src_col", [P, T])
        dst_rows = sb("dst_rows", [P, 2, N])
        score = sb("score", [P, T, N])
        prob = sb("prob", [P, T, N])
        recip = sb("recip", [P, T])
        heads_out = sb("heads_out", [P, T, HID])
        elu_e = sb("elu_e", [P, T, HID])
        ones_ready = sem("gat_ones_ready")
        turned = sem("gat_turned")
        x_t_ready_s = sem("gat_x_t_ready_s")
        x_t_ready_v = sem("gat_x_t_ready_v")
        feats_done = sem("feats_done")
        feats_ready = sem("feats_ready")
        src_score_ready = sem("src_score_ready")
        src_col_ready = sem("src_col_ready")
        src_spread = sem("src_spread")
        top_done = sem("top_done")
        spread_seen = sem("spread_seen")
        row_cols_ready = sem("row_cols_ready")
        rows_spread = sem("rows_spread")
        rows_ready = sem("gat_rows_ready")
        low_ready = sem("low_ready")
        score_ready = sem("score_ready")
        counted_ready = sem("counted_ready")
        prob_ready = sem("prob_ready")
        heads_summed = sem("heads_summed")
        heads_copied = sem("heads_copied")
        min_ready = sem("min_ready")
        elu_exp_ready = sem("elu_exp_ready")
        elu_ready = sem("elu_ready")
        psum = g.psum

        def spread(b, col):
            for t in range(T):
                last = nc.tensor.matmul(g.wide(b)[0:P, t * P:(t + 1) * P], col[:, t:t + 1].broadcast_to([P, P]),
                                        g.ident[0:P, 0:P], start=True, stop=True)
            return last

        with nc.Block() as block:
            @block.gpsimd
            def _(pool):
                pool.memset(feats[0][:, :, :, HID // HEADS:], 1.0).then_inc(ones_ready, 1)
                pool.memset(feats[1][:, :, :, D:], 1.0).then_inc(ones_ready, 1)
                base = 0
                for layer, (KT, H, C) in enumerate(SHAPES):
                    pool.wait_ge(src_score_ready, layer + 1)

                    def source_column(h, n):
                        pool.wait_ge(src_spread, n)
                        pool.tensor_copy(src_col[:, :], src_score[:, :, ds(h, 1)].rearrange("p t o -> p (t o)")).then_inc(src_col_ready, 1)

                    source_column(0, base)
                    if H > 1:
                        with pool.Fori(1, H) as h:
                            source_column(h, h + base)
                    base += H

            @block.tensor
            def _(pe):
                pe.wait_ge(g.gat_loaded, 16 * 12)
                for t in range(T):
                    last = nc.tensor.transpose(g.wide(0)[:, t * P:(t + 1) * P], g.xb[:, t, :], g.ident[0:P, 0:P])
                last.then_inc(turned, 1)
                base = 0
                for layer, (KT, H, C) in enumerate(SHAPES):
                    w = g.w_gat[layer]
                    x1 = feats[0 if H > 1 else 1]
                    pe.wait_ge(x_t_ready_s, layer + 1)
                    if layer:
                        pe.wait_ge(x_t_ready_v, layer)
                    for t in range(T):
                        for k in range(KT):
                            last = nc.tensor.matmul(g.bank(t)[0:P, 0:H * C + 2 * H], g.x_t[:, k, t * P:(t + 1) * P], w[:, k, :],
                                                    start=k == 0, stop=k == KT - 1)
                    last.then_inc(feats_done, 1)
                    pe.wait_ge(feats_ready, T * (layer + 1))
                    pe.wait_ge(src_score_ready, layer + 1)

                    def spread_source(n):
                        pe.wait_ge(src_col_ready, n + 1)
                        pe.wait_ge(top_done, n)
                        spread(SMAX, src_col).then_inc(src_spread, 1)

                    def spread_rows(n):
                        pe.wait_ge(row_cols_ready, n + 1)
                        pe.wait_ge(rows_ready, n)
                        spread(ATT, high_row)
                        spread(ATT + 2, low_row).then_inc(rows_spread, 1)

                    def aggregate(h, n):
                        pe.wait_ge(heads_copied, n)
                        if H == 1:
                            pe.wait_ge(ones_ready, 2)
                        for s in range(T):
                            pe.wait_ge(prob_ready, n * T + (s + 1))
                            for d in range(T):
                                b, at = (OUT, d) if d < 3 else (OUT + 1, d - 3)
                                last = nc.tensor.matmul(g.bank(b)[0:P, at * (C + 1):(at + 1) * (C + 1)],
                                                        prob[:, s, d * P:(d + 1) * P],
                                                        x1[:, s, ds(h, 1), :].rearrange("p h c -> p (h c)"),
                                                        start=s == 0 and at == 0, stop=s == T - 1, skip_group_check=True)
                        last.then_inc(heads_summed, 1)

                    if layer == 0:
                        pe.wait_ge(ones_ready, 2)
                    spread_source(base)
                    spread_rows(base)
                    if H > 1:
                        spread_source(base + 1)
                        with pe.Fori(0, H - 2) as h:
                            spread_rows(h + (base + 1))
                            spread_source(h + (base + 2))
                            aggregate(h, h + base)
                        spread_rows(base + H - 1)
                        aggregate(H - 2, base + H - 2)
                    aggregate(H - 1, base + H - 1)
                    base += H
                    if layer < 2:
                        pe.wait_ge(elu_ready, layer + 1)
                        for k in range(2):
                            for t in range(T):
                                last = nc.tensor.transpose(g.wide(2 * k)[:, t * P:(t + 1) * P],
                                                           heads_out[:, t, k * FULL:(k + 1) * FULL], g.ident[0:P, 0:P])
                        last.then_inc(turned, 1)

            @block.scalar
            def _(act):
                act.wait_ge(turned, 1)
                nc.scalar.copy(g.x_t[:, 0, :], g.wide(0)).then_inc(x_t_ready_s, 1)
                base = 0
                for layer, (KT, H, C) in enumerate(SHAPES):
                    x1 = feats[0 if H > 1 else 1]
                    act.wait_ge(src_score_ready, layer + 1)
                    for t in range(T):
                        nc.scalar.copy(x1[:, t, :, 0:C], g.bank(t)[0:P, 0:H * C].rearrange("p (h c) -> p h c", h=H)).then_inc(feats_ready, 1)

                    def fetch_rows(n):
                        act.wait_ge(rows_spread, n + 1)
                        act.wait_ge(score_ready, n * T)
                        both = psum[0:P, ATT * 512:(ATT + 4) * 512].rearrange("p (r f) -> p r f", r=2)[:, :, EDGE:EDGE + N]
                        nc.scalar.copy(dst_rows[:, :, :], both).then_inc(rows_ready, 1)

                    def head(h, n):
                        act.wait_ge(rows_ready, n + 1)
                        for s in range(T + LOW_AHEAD):
                            if s < T:
                                nc.scalar.activation(score[:, s, :], dst_rows[:, 1, :], ACT.Identity,
                                                     bias=src_low[:, s, ds(h, 1)]).then_inc(low_ready, 1)
                            if s >= LOW_AHEAD:
                                e = s - LOW_AHEAD
                                act.wait_ge(counted_ready, n * T + e + 1)
                                if e == 0:
                                    act.wait_ge(heads_summed, n)
                                nc.scalar.activation(prob[:, e, :], score[:, e, :], ACT.Exp).then_inc(prob_ready, 1)

                    fetch_rows(base)
                    if H > 1:
                        with act.Fori(0, H - 1) as h:
                            head(h, h + base)
                            fetch_rows(h + (base + 1))
                    head(H - 1, base + H - 1)
                    base += H
                    if layer < 2:
                        act.wait_ge(min_ready, layer + 1)
                        nc.scalar.activation(elu_e[:, :, :], elu_e[:, :, :], ACT.Exp).then_inc(elu_exp_ready, 1)
                        act.wait_ge(turned, layer + 2)
                        nc.scalar.copy(g.x_t[:, 0, :], g.wide(0)).then_inc(x_t_ready_s, 1)
                g.layernorm_scalar(3)

            @block.vector
            def _(dve):
                chain = Chain(dve, g.dve_chain)
                chain.done = g.dve_links
                dve.wait_ge(g.gat_loaded, 16 * 12)
                base = 0
                for layer, (KT, H, C) in enumerate(SHAPES):
                    dve.wait_ge(feats_done, layer + 1)
                    scores = psum[0:P, 0:T * 512].rearrange("p (t f) -> p t f", f=512)[:, :, H * C:H * C + 2 * H]
                    nc.vector.tensor_copy(src_score[:, :, 0:H], scores[:, :, 0:H])
                    nc.vector.tensor_copy(dst_score[:, :, 0:H], scores[:, :, H:2 * H])
                    nc.vector.tensor_scalar(src_low[:, :, 0:H], scores[:, :, 0:H], NEG_SLOPE, None, ALU.mult).then_inc(src_score_ready, 1)
                    dve.wait_ge(src_score_ready, layer + 1)

                    def maximum(h, n):
                        dve.wait_ge(src_spread, n + 1)
                        dve.sem_inc(spread_seen, 1)
                        for t in range(T):
                            last = nc.vector.tensor_tensor_reduce(out=masked[:, t, :], in0=g.wide(SMAX)[0:P, :], in1=g.no_edge_t[:, t, :],
                                                                  scale=1.0, scalar=-3.0e38, op0=ALU.add, op1=ALU.max,
                                                                  accum_out=top[:, t:t + 1])
                        last.then_inc(top_done, 1)
                        dve.wait_ge(top_done, n + 1)
                        dve.wait_ge(rows_spread, n)
                        d_col = dst_score[:, :, ds(h, 1)].rearrange("p t o -> p (t o)")
                        chain.link(nc.vector.tensor_tensor(top[:, :], top[:, :], d_col, ALU.add))
                        chain.link(nc.vector.scalar_tensor_tensor(top[:, :], top[:, :], NEG_SLOPE, top[:, :], ALU.mult, ALU.max))
                        nc.vector.tensor_tensor(high_row[:, :], d_col, top[:, :], ALU.subtract)
                        nc.vector.scalar_tensor_tensor(low_row[:, :], d_col, NEG_SLOPE, top[:, :], ALU.mult, ALU.subtract).then_inc(row_cols_ready, 1)

                    def weigh(h, n):
                        dve.wait_ge(rows_ready, n + 1)
                        for s in range(T + 1):
                            if s < T:
                                dve.wait_ge(low_ready, n * T + (s + 1))
                                nc.vector.scalar_tensor_tensor(score[:, s, :], dst_rows[:, 0, :], src_score[:, s, ds(h, 1)],
                                                               score[:, s, :], ALU.add, ALU.max).then_inc(score_ready, 1)
                            if s > 0:
                                dve.wait_ge(score_ready, n * T + s)
                                nc.vector.tensor_tensor(score[:, s - 1, :], score[:, s - 1, :], g.log_count[:, s - 1, :],
                                                        ALU.add).then_inc(counted_ready, 1)

                    def normalise(h, n):
                        dve.wait_ge(heads_summed, n + 1)
                        sums = [g.bank(OUT)[0:P, 0:3 * (C + 1)].rearrange("p (t c) -> p t c", c=C + 1),
                                g.bank(OUT + 1)[0:P, 0:2 * (C + 1)].rearrange("p (t c) -> p t c", c=C + 1)]
                        for (lo, hi), s in zip(((0, 3), (3, 5)), sums):
                            last = nc.vector.tensor_scalar(recip[:, lo:hi], s[:, :, C], 1e-16, None, ALU.add)
                        chain.link(last)
                        chain.link(nc.vector.reciprocal(recip[:, :], recip[:, :]))
                        for (lo, hi), s in zip(((0, 3), (3, 5)), sums):
                            to = heads_out[:, lo:hi, ds(h * C, C)]
                            last = nc.vector.tensor_tensor(to, s[:, :, 0:C], recip[:, lo:hi].unsqueeze(2).broadcast_to([P, hi - lo, C]), ALU.mult)
                        last.then_inc(heads_copied, 1)

                    if layer == 0:
                        dve.wait_ge(g.log_count_ready, 1)
                    maximum(0, base)
                    if H > 1:
                        maximum(1, base + 1)
                        weigh(0, base)
                        with dve.Fori(0, H - 2) as h:
                            chain.enter(h, 4)
                            maximum(h + 2, h + (base + 2))
                            normalise(h, h + base)
                            weigh(h + 1, h + (base + 1))
                        chain.leave(H - 2)
                        normalise(H - 2, base + H - 2)
                    weigh(H - 1, base + H - 1)
                    normalise(H - 1, base + H - 1)
                    base += H
                    dve.wait_ge(heads_copied, base)
                    HC = H * C
                    chain.link(nc.vector.tensor_tensor(heads_out[:, :, 0:HC], heads_out[:, :, 0:HC],
                                                       g.b_gat[layer][:, :].unsqueeze(1).broadcast_to([P, T, HC]), ALU.add))
                    if layer < 2:
                        nc.vector.tensor_scalar(elu_e[:, :, :], heads_out[:, :, :], 0.0, None, ALU.min).then_inc(min_ready, 1)
                        dve.wait_ge(elu_exp_ready, layer + 1)
                        nc.vector.scalar_tensor_tensor(heads_out[:, :, :], elu_e[:, :, :], -1.0, heads_out[:, :, :], ALU.add, ALU.max).then_inc(elu_ready, 1)
                        dve.wait_ge(turned, layer + 2)
                        nc.vector.tensor_copy(g.x_t[:, 1, :], g.wide(2)).then_inc(x_t_ready_v, 1)
                chain.link(nc.vector.tensor_tensor(g.res[:, :, :], heads_out[:, :, 0:D], g.xb[:, :, :], ALU.add))
                chain.link(g.layernorm_vector(chain, g.res, g.xa, 3))
                g.dve_links = chain.done


def moe(nc, g):
    a = g.a
    MOE_LOADS = 16 * (3 * LAYERS + 7)
    WEAK_BANK, STRONG_BANK = 4, 6
    with ExitStack() as ctx:
        def sb(name, shape, dt=F32):
            return ctx.enter_context(nc.sbuf_tensor(name, shape, dt))

        def sem(name):
            return ctx.enter_context(nc.semaphore(name))

        h = sb("h", [P, T, HID])
        agg_t = sb("moe_agg_t", [FULL, 2, N])
        hidden_t = sb("hidden_t", [FULL, 4, N])
        tri = sb("tri", [P, NEXP, NEXP])
        logits = sb("logits", [P, T, NEXP + 1])
        beats = sb("beats", [P, T, NEXP, NEXP])
        ties = sb("ties", [P, T, NEXP, NEXP])
        rank = sb("rank", [P, T, NEXP])
        best = sb("best", [P, T])
        gate = sb("gate", [P, T, NEXP])
        shifted = sb("shifted", [P, T, NEXP])
        conf = sb("conf", [P, T])
        total = sb("total", [P, T])
        gate_t = sb("gate_t", [NEXP, N])
        weak_sum = sb("weak_sum", [P, 2, 2 * HID])
        moe_sum = sb("moe_sum", [P, T, HID])
        y = sb("y", [P, T, D])
        tri_ready = sem("tri_ready")
        x3_turned = sem("x3_turned")
        x3_t_ready = sem("x3_t_ready")
        h_done = sem("h_done")
        h_ready = sem("h_ready")
        turned = sem("moe_turned")
        h_t_ready_s = sem("h_t_ready_s")
        h_t_ready_v = sem("h_t_ready_v")
        agg_done = sem("agg_done")
        agg_ready_s = sem("agg_ready_s")
        agg_ready_v = sem("agg_ready_v")
        logits_done = sem("logits_done")
        shifted_ready = sem("shifted_ready")
        exps_ready = sem("exps_ready")
        gate_ready = sem("gate_ready")
        gate_turned = sem("gate_turned")
        gate_t_ready = sem("gate_t_ready")
        weak_done = sem("weak_done")
        weak_read = sem("weak_read")
        hidden_done = sem("hidden_done")
        hidden_ready = sem("hidden_ready")
        strong_done = sem("strong_done")
        strong_read = sem("strong_read")
        weak_pair = sem("weak_pair")
        bias_done = sem("bias_done")
        bias_bank_seen = sem("bias_bank_seen")
        bias_read = sem("bias_read")
        y_done = sem("y_done")
        y_ready = sem("y_ready")
        stored = sem("stored")
        psum = g.psum
        WPAIR = NW // 2

        with nc.Block() as block:
            @block.sync
            def _(sp):
                w1 = a["L3_gnn_strong_W1"].rearrange("l e (k p) f -> l e p k f", p=FULL)
                w2 = a["L3_gnn_strong_W2"].rearrange("l e (k p) f -> l e p k f", p=FULL)
                ww = a["L3_gnn_weak_W"].rearrange("l e (k p) f -> l k p e f", p=FULL)
                with sp.Fori(1, LAYERS) as l:
                    sp.wait_ge(weak_done, l * (T * WPAIR))
                    for k in range(2):
                        sp.dma_start(g.w_weak[:, k, :, :], ww[ds(l, 1), k].rearrange("l p e f -> p (l e) f")).then_inc(g.weak_loaded, 16)
                    for e in range(NS):
                        sp.wait_ge(strong_done, l * (NS * T) + (e + 1 - NS) * T)
                        sp.dma_start(g.w_strong1[:, e, :, :], w1[ds(l, 1), e].rearrange("l p k f -> p (l k) f")).then_inc(g.strong_loaded[e], 16)
                        sp.dma_start(g.w_strong2[:, e, :, :], w2[ds(l, 1), e].rearrange("l p k f -> p (l k) f")).then_inc(g.strong_loaded[e], 16)
                sp.wait_ge(y_ready, 1)
                sp.dma_start(g.out.rearrange("(t p) f -> p t f", p=P), y[:, :, :]).then_inc(stored, 16)
                sp.wait_ge(stored, 16)

            @block.gpsimd
            def _(pool):
                pool.memset(tri[:, :, :], 1.0).then_inc(tri_ready, 1)
                pool.wait_ge(tri_ready, 1)
                pool.affine_select(out=tri[:, :, :], in_=tri[:, :, :], compare_op=ALU.is_gt, fill=0.0, base=0,
                                   pattern=[[1, NEXP], [-1, NEXP]], channel_multiplier=0).then_inc(tri_ready, 1)

            @block.tensor
            def _(pe):
                pe.wait_ge(g.moe_loaded, MOE_LOADS)
                for t in range(T):
                    last = nc.tensor.transpose(g.wide(0)[:, t * P:(t + 1) * P], g.xa[:, t, :], g.ident[0:P, 0:P])
                last.then_inc(x3_turned, 1)
                pe.wait_ge(x3_t_ready, 1)
                for t in range(T):
                    to = g.bank(2 + t)[0:P, 0:HID]
                    nc.tensor.matmul(to, g.x_t[:, 0, t * P:(t + 1) * P], g.w_in[:, :], start=True, stop=False)
                    last = nc.tensor.matmul(to, g.ones[0:1, 0:P], g.b_in[:, :], start=False, stop=True)
                last.then_inc(h_done, 1)

                def turn_h(n):
                    pe.wait_ge(h_ready, n + 1)
                    for k in range(2):
                        for t in range(T):
                            last = nc.tensor.transpose(g.wide(2 * k)[:, t * P:(t + 1) * P],
                                                       h[:, t, k * FULL:(k + 1) * FULL], g.ident[0:P, 0:P])
                    last.then_inc(turned, 1)

                with pe.Fori(0, LAYERS) as l:
                    turn_h(l)
                    for f in range(2):
                        for lo, hi in ROWS:
                            for s in range(T):
                                last = nc.tensor.matmul(g.wide(4 + 2 * f)[:, lo:hi], h[:, s, f * FULL:(f + 1) * FULL],
                                                        g.count[:, s, lo:hi], start=s == 0, stop=s == T - 1)
                    last.then_inc(agg_done, 1)
                    pe.wait_ge(h_t_ready_s, l + 1)
                    pe.wait_ge(h_t_ready_v, l + 1)
                    pe.wait_ge(agg_ready_s, l + 1)
                    pe.wait_ge(agg_ready_v, l + 1)
                    for t in range(T):
                        to = g.bank(STRONG_BANK)[0:P, t * 16:t * 16 + NEXP + 1]
                        for k in range(4):
                            lhs = (g.x_t if k < 2 else agg_t)[:, k % 2, t * P:(t + 1) * P]
                            nc.tensor.matmul(to, lhs, g.w_router[:, ds(l, 1), k, :].rearrange("p l e -> p (l e)"),
                                             start=k == 0, stop=False)
                        last = nc.tensor.matmul(to, g.ones[0:1, 0:P], g.b_router[:, ds(l, 1), :].rearrange("p l e -> p (l e)"),
                                                start=False, stop=True)
                    last.then_inc(logits_done, 1)
                    pe.wait_ge(g.weak_loaded, l * 32 + 32)
                    for t in range(T):
                        for q in range(WPAIR):
                            n = t * WPAIR + q
                            if n >= 2:
                                pe.wait_ge(weak_read, l * (T * WPAIR) + (n - 1))
                            for k in range(2):
                                last = nc.tensor.matmul(g.bank(WEAK_BANK + n % 2)[0:P, :], agg_t[:, k, t * P:(t + 1) * P],
                                                        g.w_weak[:, k, 2 * q:2 * q + 2, :].rearrange("p e f -> p (e f)"),
                                                        start=k == 0, stop=k == 1)
                            last.then_inc(weak_done, 1)
                    pe.wait_ge(gate_ready, l + 1)
                    for t in range(T):
                        last = nc.tensor.transpose(g.wide(STRONG_BANK)[0:NEXP, t * P:(t + 1) * P], gate[:, t, :], g.ident[0:P, 0:P])
                    last.then_inc(gate_turned, 1)
                    for e in range(NS):
                        pe.wait_ge(g.strong_loaded[e], l * 32 + 32)
                        for m in range(4):
                            n = e * 4 + m
                            if n >= 2:
                                pe.wait_ge(hidden_ready, l * (NS * 4) + (n - 1))
                            for lo, hi in ROWS:
                                for k in range(2):
                                    last = nc.tensor.matmul(g.wide(2 * (n % 2))[:, lo:hi], g.w_strong1[:, e, k, m * FULL:(m + 1) * FULL],
                                                            agg_t[:, k, lo:hi], start=k == 0, stop=k == 1)
                            last.then_inc(hidden_done, 1)
                        if e == 0:
                            pe.wait_ge(gate_t_ready, l + 1)
                        pe.wait_ge(hidden_ready, l * (NS * 4) + (e * 4 + 4))
                        for t in range(T):
                            n = e * T + t
                            if n >= 2:
                                pe.wait_ge(strong_read, l * (NS * T) + (n - 1))
                            for k in range(4):
                                last = nc.tensor.matmul(g.bank(STRONG_BANK + n % 2)[0:P, 0:HID], hidden_t[:, k, t * P:(t + 1) * P],
                                                        g.w_strong2[:, e, k, :], start=k == 0, stop=k == 3)
                            last.then_inc(strong_done, 1)
                    pe.wait_ge(weak_read, l * (T * WPAIR) + T * WPAIR)
                    pe.sem_inc(bias_bank_seen, 1)
                    for t in range(T):
                        if t >= 2:
                            pe.wait_ge(bias_read, l * T + (t - 1))
                            pe.sem_inc(bias_bank_seen, 1)
                        nc.tensor.matmul(g.bank(WEAK_BANK + t % 2)[0:P, 0:HID], gate_t[:, t * P:(t + 1) * P],
                                         g.b_strong2[:, ds(l, 1), :].rearrange("p l f -> p (l f)"), start=True, stop=True).then_inc(bias_done, 1)

                turn_h(LAYERS)
                pe.wait_ge(h_t_ready_s, LAYERS + 1)
                pe.wait_ge(h_t_ready_v, LAYERS + 1)
                for t in range(T):
                    to = g.bank(t)[0:P, 0:D]
                    for k in range(2):
                        nc.tensor.matmul(to, g.x_t[:, k, t * P:(t + 1) * P], g.w_out[:, k, :], start=k == 0, stop=False)
                    last = nc.tensor.matmul(to, g.ones[0:1, 0:P], g.b_out[:, :], start=False, stop=True)
                last.then_inc(y_done, 1)

            @block.scalar
            def _(act):
                act.wait_ge(g.moe_loaded, MOE_LOADS)
                act.wait_ge(x3_turned, 1)
                nc.scalar.copy(g.x_t[:, 0, :], g.wide(0)).then_inc(x3_t_ready, 1)
                with act.Fori(0, LAYERS) as l:
                    act.wait_ge(turned, l + 1)
                    nc.scalar.copy(g.x_t[:, 0, :], g.wide(0)).then_inc(h_t_ready_s, 1)
                    act.wait_ge(agg_done, l + 1)
                    nc.scalar.copy(agg_t[:, 0, :], g.wide(4)).then_inc(agg_ready_s, 1)
                    act.wait_ge(shifted_ready, l + 1)
                    nc.scalar.activation(shifted[:, :, :], shifted[:, :, :], ACT.Exp)
                    nc.scalar.activation(conf[:, :], conf[:, :], ACT.Exp, scale=-1.0).then_inc(exps_ready, 1)
                    for e in range(NS):
                        for m in range(4):
                            n = e * 4 + m
                            act.wait_ge(hidden_done, l * (NS * 4) + (n + 1))
                            if m == 0:
                                act.wait_ge(strong_done, l * (NS * T) + e * T)
                            nc.scalar.activation(hidden_t[:, m, :], g.wide(2 * (n % 2)), ACT.Relu,
                                                 bias=g.b_strong1[:, ds(l, 1), e, m]).then_inc(hidden_ready, 1)
                act.wait_ge(turned, LAYERS + 1)
                nc.scalar.copy(g.x_t[:, 0, :], g.wide(0)).then_inc(h_t_ready_s, 1)
                g.layernorm_scalar(4)

            @block.vector
            def _(dve):
                chain = Chain(dve, g.dve_chain)
                chain.done = g.dve_links
                dve.wait_ge(g.moe_loaded, MOE_LOADS)
                dve.wait_ge(h_done, 1)
                nc.vector.tensor_copy(h[:, :, :], psum[0:P, 2 * 512:7 * 512].rearrange("p (t f) -> p t f", f=512)[:, :, 0:HID]).then_inc(h_ready, 1)
                dve.wait_ge(tri_ready, 2)
                dve.wait_ge(g.b_weak_loaded, 16)
                with dve.Fori(0, LAYERS) as l:
                    chain.enter(l, 31)
                    dve.wait_ge(turned, l + 1)
                    nc.vector.tensor_copy(g.x_t[:, 1, :], g.wide(2)).then_inc(h_t_ready_v, 1)
                    dve.wait_ge(agg_done, l + 1)
                    nc.vector.tensor_copy(agg_t[:, 1, :], g.wide(6)).then_inc(agg_ready_v, 1)
                    dve.wait_ge(logits_done, l + 1)
                    chain.link(nc.vector.tensor_copy(logits[:, :, :], g.bank(STRONG_BANK)[0:P, 0:T * 16].rearrange("p (t e) -> p t e", e=16)[:, :, 0:NEXP + 1]))
                    lg = logits[:, :, 0:NEXP]
                    nc.vector.tensor_copy(conf[:, :], logits[:, :, NEXP])
                    chain.link(nc.vector.tensor_reduce(best[:, :], lg, AX.X, ALU.max))
                    nc.vector.tensor_tensor(shifted[:, :, :], lg, best[:, :].unsqueeze(2).broadcast_to([P, T, NEXP]), ALU.subtract).then_inc(shifted_ready, 1)
                    for t in range(T):
                        other = logits[:, t, 0:NEXP].unsqueeze(1).broadcast_to([P, NEXP, NEXP])
                        mine = logits[:, t, 0:NEXP].unsqueeze(2).broadcast_to([P, NEXP, NEXP])
                        nc.vector.tensor_tensor(beats[:, t, :, :], other, mine, ALU.is_gt)
                        last = nc.vector.tensor_tensor(ties[:, t, :, :], other, mine, ALU.is_equal)
                    chain.link(last)
                    for t in range(T):
                        last = nc.vector.tensor_tensor(ties[:, t, :, :], ties[:, t, :, :], tri[:, :, :], ALU.mult)
                    chain.link(last)
                    chain.link(nc.vector.tensor_tensor(beats[:, :, :, :], beats[:, :, :, :], ties[:, :, :, :], ALU.add))
                    chain.link(nc.vector.tensor_reduce(rank[:, :, :], beats[:, :, :, :], AX.X, ALU.add))
                    dve.wait_ge(exps_ready, l + 1)
                    chain.link(nc.vector.scalar_tensor_tensor(gate[:, :, :], rank[:, :, :], 2.0, shifted[:, :, :], ALU.is_lt, ALU.mult))
                    chain.link(nc.vector.tensor_reduce(total[:, :], gate[:, :, :], AX.X, ALU.add))
                    chain.link(nc.vector.reciprocal(total[:, :], total[:, :]))
                    nc.vector.tensor_tensor(gate[:, :, :], gate[:, :, :], total[:, :].unsqueeze(2).broadcast_to([P, T, NEXP]), ALU.mult).then_inc(gate_ready, 1)
                    chain.link(nc.vector.tensor_scalar(conf[:, :], conf[:, :], 1.0, None, ALU.add))
                    chain.link(nc.vector.reciprocal(conf[:, :], conf[:, :]))
                    for t in range(T):
                        for q in range(WPAIR):
                            n = t * WPAIR + q
                            dve.wait_ge(weak_done, l * (T * WPAIR) + (n + 1))
                            nc.vector.tensor_tensor(weak_sum[:, q, :], g.bank(WEAK_BANK + n % 2)[0:P, :],
                                                    g.b_weak[:, ds(l, 1), 2 * q * HID:(2 * q + 2) * HID].rearrange("p l f -> p (l f)"),
                                                    ALU.add).then_inc(weak_read, 1)
                            dve.wait_ge(weak_read, l * (T * WPAIR) + (n + 1))
                            for j in range(2):
                                e = 2 * q + j
                                part = weak_sum[:, q, j * HID:(j + 1) * HID]
                                to = moe_sum[:, t, :] if e == 0 else part
                                last = nc.vector.tensor_scalar(to, part, 0.0, gate[:, t, e:e + 1], ALU.max, ALU.mult)
                            chain.link(last)
                            for j in range(2):
                                if 2 * q + j:
                                    add = nc.vector.tensor_tensor(moe_sum[:, t, :], moe_sum[:, t, :], weak_sum[:, q, j * HID:(j + 1) * HID], ALU.add)
                                    if j == 1:
                                        chain.link(add)
                                    else:
                                        add.then_inc(weak_pair, 1)
                                        dve.wait_ge(weak_pair, l * T + (t + 1))
                    dve.wait_ge(gate_turned, l + 1)
                    nc.vector.tensor_copy(gate_t[:, :], g.wide(STRONG_BANK)[0:NEXP, :]).then_inc(gate_t_ready, 1)
                    for e in range(NS):
                        for t in range(T):
                            n = e * T + t
                            dve.wait_ge(strong_done, l * (NS * T) + (n + 1))
                            if e:
                                dve.wait_ge(strong_read, l * (NS * T) + (n - T + 1))
                            nc.vector.scalar_tensor_tensor(moe_sum[:, t, :], g.bank(STRONG_BANK + n % 2)[0:P, 0:HID], gate[:, t, NW + e:NW + e + 1],
                                                           moe_sum[:, t, :], ALU.mult, ALU.add).then_inc(strong_read, 1)
                    for t in range(T):
                        dve.wait_ge(bias_done, l * T + (t + 1))
                        dve.wait_ge(strong_read, l * (NS * T) + NS * T)
                        nc.vector.tensor_tensor(moe_sum[:, t, :], g.bank(WEAK_BANK + t % 2)[0:P, 0:HID], moe_sum[:, t, :], ALU.add).then_inc(bias_read, 1)
                    dve.wait_ge(bias_read, l * T + T)
                    for t in range(T):
                        last = nc.vector.scalar_tensor_tensor(h[:, t, :], moe_sum[:, t, :], conf[:, t:t + 1], h[:, t, :], ALU.mult, ALU.add)
                    last.then_inc(h_ready, 1)
                chain.leave(LAYERS)
                dve.wait_ge(turned, LAYERS + 1)
                nc.vector.tensor_copy(g.x_t[:, 1, :], g.wide(2)).then_inc(h_t_ready_v, 1)
                dve.wait_ge(y_done, 1)
                sums = psum[0:P, 0:T * 512].rearrange("p (t f) -> p t f", f=512)[:, :, 0:D]
                chain.link(nc.vector.tensor_tensor(g.res[:, :, :], sums, g.xa[:, :, :], ALU.add))
                g.layernorm_vector(chain, g.res, y, 4).then_inc(y_ready, 1)


_WEIGHTS_TURNED = ("L0_gnn_Wp1", "L0_gnn_Ws1", "L0_gnn_Wn1", "L0_gnn_Wp2", "L0_gnn_Ws2", "L0_gnn_Wn2")


def kernel(**inputs):
    import numpy as _np
    import concourse.bacc as _bacc
    from concourse import mybir as _mybir
    from concourse.bass_utils import run_bass_kernel_spmd as _run

    nc = _bacc.Bacc("TRN2", target_bir_lowering=False, num_devices=1)
    arrays, aps = {}, {}
    for name, value in inputs.items():
        v = _np.asarray(value)
        v = _np.ascontiguousarray(v.T if name in _WEIGHTS_TURNED else v)
        arrays[f"in_{name}"] = v
        aps[name] = nc.dram_tensor(f"in_{name}", v.shape, _mybir.dt.from_np(v.dtype), kind="ExternalInput").ap()
    out = nc.dram_tensor("out_x", (N, D), F32, kind="ExternalOutput").ap()
    build(nc, aps, out)
    r = _run(nc, [arrays], core_ids=[0])
    return r.results[0]["out_x"]
```

```python
from contextlib import ExitStack

import concourse.bass as bass
from concourse import mybir

N = 625
P = 125
T = N // P
E = 20625
CHUNKS = E // P
D = 128
FULL = 128
WIDE = 4 * P
EDGE = 512 - WIDE
HEADS = 4
HID = 256
GAT_SHAPES = ((1, HEADS, HID // HEADS), (2, HEADS, HID // HEADS), (2, 1, D))
LAYERS = 3
NEXP = 8
NW = 4
NS = 4
FF = 512
EXPERT = 2 * HID * FF // FULL
NEG_SLOPE = 0.2
BIG = 1.0e30
EPS = 1e-5

ALU = mybir.AluOpType
ACT = mybir.ActivationFunctionType
AX = mybir.AxisListType
F32 = mybir.dt.float32
BF16 = mybir.dt.bfloat16
F16 = mybir.dt.float16
F32R = mybir.dt.float32r
I32 = mybir.dt.int32
ds = bass.ds

ROWS = ((0, WIDE), (WIDE, N))
HALF = 312
HALVES = ((0, HALF), (HALF, N + 1))


class Chain:

    def __init__(self, eng, sem):
        self.eng, self.sem, self.done, self.loop = eng, sem, 0, 0

    def link(self, ins):
        self.done += 1
        ins.then_inc(self.sem, 1)
        self.eng.wait_ge(self.sem, self.loop + self.done)

    def enter(self, i, per_turn):
        self.start, self.per_turn = self.done, per_turn
        self.loop = i * per_turn

    def leave(self, turns):
        assert self.done - self.start == self.per_turn, self.done - self.start
        self.loop = 0
        self.done = self.start + turns * self.per_turn


class Program:
    pass


def build(nc, a, out):
    g = Program()
    g.a, g.out = a, out
    with ExitStack() as ctx:
        def sb(name, shape, dt=F32):
            return ctx.enter_context(nc.sbuf_tensor(name, shape, dt))

        def sem(name):
            return ctx.enter_context(nc.semaphore(name))

        g.psum = ctx.enter_context(nc.psum_tensor("psum", [FULL, 8 * 512], F32))

        def wide(b):
            return g.psum[:, b * 512 + EDGE:b * 512 + EDGE + N]

        def bank(b):
            return g.psum[:, b * 512:(b + 1) * 512]

        g.ident = sb("ident", [FULL, FULL])
        g.ident_bf = sb("ident_bf", [FULL, FULL], BF16)
        g.ones = sb("ones", [FULL, FULL])
        g.count = sb("count", [P, T, N])
        g.count_t = sb("count_t", [P, T, N])
        g.log_count = sb("log_count", [P, T, N])
        g.degree = sb("degree", [P, T])
        g.recip_deg = sb("recip_deg", [P, T])
        g.some_edge = sb("some_edge", [P, T])
        g.run_end = sb("run_end", [P, T], I32)
        g.is_sorted = sb("is_sorted", [1, 1], I32)
        g.node_col = sb("node_col", [P, T])
        g.xa = sb("xa", [P, T, D])
        g.xb = sb("xb", [P, T, D])
        g.res = sb("res", [P, T, D])
        g.x_t = sb("x_t", [FULL, 2, N])
        g.ln_stats = sb("ln_stats", [P, T, 6])
        g.ln_mv = sb("ln_mv", [P, T, 2])
        g.ln_var = sb("ln_var", [P, T])
        g.ln_std = sb("ln_std", [P, T])
        g.ln_rstd = sb("ln_rstd", [P, T])

        g.b_sage = sb("b_sage", [FULL, 3])
        g.b_sage2 = sb("b_sage2", [1, D])
        g.b_pool = sb("b_pool", [P, 2, D])
        g.w_gat = [sb(f"w_gat{i}", [FULL, kt, h * c + 2 * h]) for i, (kt, h, c) in enumerate(GAT_SHAPES)]
        g.att = [sb(f"att{i}", [FULL, 2, h * c]) for i, (kt, h, c) in enumerate(GAT_SHAPES)]
        g.b_gat = [sb(f"b_gat{i}", [P, HID if i < 2 else D]) for i in range(3)]
        g.w_in = sb("w_in", [FULL, HID])
        g.b_in = sb("b_in", [P, HID])
        g.w_router = sb("w_router", [FULL, LAYERS, 4, NEXP + 1])
        g.b_router = sb("b_router", [P, LAYERS, NEXP + 1])
        g.b_strong1 = sb("b_strong1", [FULL, LAYERS, NS, 4])
        g.b_strong2 = sb("b_strong2", [NEXP, LAYERS, HID])
        g.w_out = sb("w_out", [FULL, 2, D])
        g.b_out = sb("b_out", [1, D])

        g.edges_loaded = sem("edges_loaded")
        g.x_loaded = sem("x_loaded")
        g.sage_loaded = sem("sage_loaded")
        g.edges_spread = sem("edges_spread")
        g.gat_loaded = sem("gat_loaded")
        g.moe_loaded = sem("moe_loaded")
        g.b_weak_loaded = sem("b_weak_loaded")
        g.raw_loaded = [sem(f"raw{k}_loaded") for k in range(3)]
        g.consts_ready = sem("consts_ready")
        g.log_count_ready = sem("log_count_ready")
        g.dve_chain = sem("dve_chain")
        g.ln_var_ready = sem("ln_var_ready")
        g.ln_std_ready = sem("ln_std_ready")

        def layernorm_vector(chain, r, y, k):
            for t in range(T):
                last = nc.vector.bn_stats(g.ln_stats[:, t, :], r[:, t, :])
            chain.link(last)
            for t in range(T):
                last = nc.vector.bn_aggr(g.ln_mv[:, t, :], g.ln_stats[:, t, :])
            chain.link(last)
            nc.vector.tensor_scalar(g.ln_var[:, :], g.ln_mv[:, :, 1], EPS, None, ALU.add).then_inc(g.ln_var_ready, 1)
            nc.vector.wait_ge(g.ln_std_ready, k)
            chain.link(nc.vector.reciprocal(g.ln_rstd[:, :], g.ln_std[:, :]))
            for t in range(T):
                last = nc.vector.tensor_scalar(y[:, t, :], r[:, t, :], g.ln_mv[:, t, 0:1], g.ln_rstd[:, t:t + 1],
                                               ALU.subtract, ALU.mult)
            return last

        def layernorm_scalar(k):
            nc.scalar.wait_ge(g.ln_var_ready, k)
            nc.scalar.activation(g.ln_std[:, :], g.ln_var[:, :], ACT.Sqrt).then_inc(g.ln_std_ready, 1)

        def load_weak(sp, l):
            w = g.a["L3_gnn_weak_W"].rearrange("l e (k p) f -> l k p e f", p=FULL)
            to = g.w_raw[:, 0, :].rearrange("p (k e f) -> p k e f", k=2, e=NW)
            for k in range(2):
                sp.dma_start(to[:, k, :, :], w[ds(l, 1), k].rearrange("l p e f -> p (l e) f")).then_inc(g.raw_loaded[0], 16)

        def load_strong(sp, l, e):
            part = 1 + e % 2
            w1 = g.a["L3_gnn_strong_W1"].rearrange("l e (k p) f -> l e p k f", p=FULL)
            w2 = g.a["L3_gnn_strong_W2"].rearrange("l e (k p) f -> l e p k f", p=FULL)
            to1 = g.w_raw[:, part, 0:2 * FF].rearrange("p (k f) -> p k f", f=FF)
            to2 = g.w_raw[:, part, 2 * FF:].rearrange("p (k f) -> p k f", f=HID)
            sp.dma_start(to1, w1[ds(l, 1), e].rearrange("l p k f -> p (l k) f")).then_inc(g.raw_loaded[part], 16)
            sp.dma_start(to2, w2[ds(l, 1), e].rearrange("l p k f -> p (l k) f")).then_inc(g.raw_loaded[part], 16)

        g.load_weak, g.load_strong = load_weak, load_strong
        g.wide, g.bank = wide, bank
        g.layernorm_vector, g.layernorm_scalar = layernorm_vector, layernorm_scalar
        g.src_row = nc.dram_tensor("src_row", (E,), F16, kind="Internal").ap()
        g.keep_row = nc.dram_tensor("keep_row", (E + 1,), BF16, kind="Internal").ap()
        g.max_rows = nc.dram_tensor("max_rows", (E, D), F32, kind="Internal").ap()
        with ExitStack() as edges:
            g.w_sage = edges.enter_context(nc.sbuf_tensor("w_sage", [FULL, 6, D], F32))
            g.src_all = edges.enter_context(nc.sbuf_tensor("src_all", [P, E + 1], F16))
            g.keep_all = edges.enter_context(nc.sbuf_tensor("keep_all", [FULL, E], BF16))
            adjacency(nc, g)
            sage(nc, g)
        with ExitStack() as experts:
            def ex(name, shape):
                return experts.enter_context(nc.sbuf_tensor(name, shape, F32))

            g.no_edge_t = experts.enter_context(nc.sbuf_tensor("no_edge_t", [P, T, N], BF16))
            g.b_weak = ex("b_weak", [P, LAYERS, NW * HID])
            g.w_raw = ex("w_raw", [FULL, 3, EXPERT])
            propagate(nc, g)
            gat(nc, g)
            moe(nc, g)


def adjacency(nc, g):
    a = g.a
    ROW_PARTS, ROWS_EACH = 3, CHUNKS // 3
    RING = 5
    GROUPS = CHUNKS // RING
    VISITS = GROUPS + T - 1
    STEPS = VISITS * RING
    PAD = (T - 1) * RING
    ODD_EACH = 3
    REST = 5 * 512
    assert ROW_PARTS * ROWS_EACH == CHUNKS and GROUPS * RING == CHUNKS and VISITS % (2 * ODD_EACH) == 1
    with ExitStack() as ctx:
        def sb(name, shape, dt=F32):
            return ctx.enter_context(nc.sbuf_tensor(name, shape, dt))

        def sem(name):
            return ctx.enter_context(nc.semaphore(name))

        ends_i = sb("ends_i", [ROWS_EACH, 2, ROW_PARTS, P], I32)
        ends_f = sb("ends_f", [ROWS_EACH, 2, ROW_PARTS, P])
        next_i = sb("next_i", [ROWS_EACH, ROW_PARTS, P], I32)
        next_f = sb("next_f", [ROWS_EACH, ROW_PARTS, P])
        src16 = sb("src16", [ROWS_EACH, ROW_PARTS, P], F16)
        keep = sb("keep", [ROWS_EACH, ROW_PARTS, P], BF16)
        zero16 = sb("zero16", [1, N], BF16)
        falls = sb("falls", [ROWS_EACH, ROW_PARTS, P])
        any_fall = sb("any_fall", [ROWS_EACH, 1])
        ends = sb("ends", [P, 2, PAD + CHUNKS + PAD])
        last_visit = sb("last_visit", [P, T - 1])
        steps_i = sb("steps_i", [P, T - 1], I32)
        steps = sb("steps", [P, T - 1])
        visit_i = sb("visit_i", [P, VISITS, RING], I32)
        visit = sb("visit", [P, STEPS])
        tile_of = sb("tile_of", [P, STEPS])
        tile_reg = sb("tile_reg", [1, VISITS], I32)
        room = g.log_count[:, :, :].rearrange("p t n -> p (t n)")
        below = room[:, 0:(T - 1) * GROUPS].rearrange("p (t c) -> p t c", c=GROUPS)
        left = room[:, (T - 1) * GROUPS:(T - 1) * (GROUPS + STEPS)].rearrange("p (v t) -> p v t", t=T - 1)
        picked = room[:, N * T - 2 * STEPS * T:N * T].rearrange("p (s v t) -> p s v t", s=2, t=T)
        assert (T - 1) * (GROUPS + STEPS) + 2 * STEPS * T <= N * T
        visit_ends = sb("visit_ends", [P, 2, STEPS])
        tri = sb("adj_tri", [P, P])
        node_col_i = sb("node_col_i", [P, T], I32)
        before = sb("before", [P, T + 1])
        last_place = sb("last_place", [P, T])
        node_i = sb("node_i", [P, N], I32)
        node = sb("node", [P, N], F16)
        onehot = sb("onehot", [P, RING, 2, N], BF16)
        visit_dst = sb("visit_dst", [P, STEPS], F16)
        dst_hot = sb("dst_hot", [P, 2, RING, P], BF16)
        minus_dst = sb("minus_dst", [P, STEPS])
        distance = sb("distance", [P, RING, P], F16)
        nodes_ready = sem("nodes_ready")
        ends_f_ready = sem("ends_f_ready")
        ends_turned = sem("ends_turned")
        ends_ready = sem("ends_ready")
        fall_ready = sem("fall_ready")
        lasts_spread = sem("lasts_spread")
        flag_ready = sem("flag_ready")
        tiles_ready = sem("tiles_ready")
        zero_ready = sem("zero_ready")
        onehot_ready = sem("onehot_ready")
        dst_hot_ready_v = sem("dst_hot_ready_v")
        dst_hot_ready_s = sem("dst_hot_ready_s")
        minus_dst_ready = sem("minus_dst_ready")
        distance_ready = sem("distance_ready")
        onehot_used = sem("onehot_used")
        counts_ready = sem("counts_ready")
        counts_copied_v = sem("counts_copied_v")
        counts_copied_s = sem("counts_copied_s")
        turned = sem("turned")
        turned_copied_v = sem("turned_copied_v")
        turned_copied_s = sem("turned_copied_s")
        ident_zero = sem("ident_zero")
        next_zero = sem("next_zero")
        next_loaded = sem("next_loaded")
        edge_rows_ready = sem("edge_rows_ready")
        rows_written = sem("rows_written")
        tri_ready = sem("adj_tri_ready")
        degree_ready = sem("degree_ready")
        ends_done = sem("ends_done")
        psum = g.psum
        FLAG, LASTS = 504, 336

        def row_main(t):
            return psum[0:P, t * 512:t * 512 + WIDE]

        def row_rest(t):
            return psum[0:P, REST + t * FULL:REST + t * FULL + P]

        def edge_rows(vector):
            return vector.rearrange("(k r p) -> r k p", r=ROWS_EACH, p=P)

        with nc.Block() as block:
            @block.sync
            def _(sp):
                for i, name in enumerate(("src", "dst")):
                    sp.dma_start(ends_i[:, i, :, :], edge_rows(a[name])).then_inc(g.edges_loaded, 16)
                sp.wait_ge(next_zero, 1)
                for k in range(ROW_PARTS):
                    lo = k * ROWS_EACH * P
                    whole = ROWS_EACH if k < ROW_PARTS - 1 else ROWS_EACH - 1
                    sp.dma_start(next_i[0:whole, k, :], a["dst"][lo + 1:lo + whole * P + 1].rearrange("(r p) -> r p", p=P)).then_inc(next_loaded, 16)
                sp.dma_start(next_i[ROWS_EACH - 1:ROWS_EACH, ROW_PARTS - 1, 0:P - 1], a["dst"][E - P + 1:E].rearrange("(o p) -> o p", o=1)).then_inc(next_loaded, 16)
                sp.dma_start(g.xa[:, :, :], a["x"].rearrange("(t p) f -> p t f", p=P)).then_inc(g.x_loaded, 16)
                for i, name in enumerate(("Wp1", "Ws1", "Wn1", "Wp2", "Ws2", "Wn2")):
                    sp.dma_start(g.w_sage[:, i, :], a["L0_gnn_" + name]).then_inc(g.sage_loaded, 16)
                for i, name in enumerate(("bp1", "b1", "bp2")):
                    sp.dma_start(g.b_sage[:, i:i + 1], a["L0_gnn_" + name].rearrange("(p o) -> p o", o=1)).then_inc(g.sage_loaded, 16)
                for i, name in enumerate(("bp1", "bp2")):
                    sp.dma_start(g.b_pool[:, i, :], a["L0_gnn_" + name].partition_broadcast(P)).then_inc(g.sage_loaded, 16)
                sp.dma_start(g.b_sage2[:, :], a["L0_gnn_b2"].rearrange("(o f) -> o f", o=1)).then_inc(g.sage_loaded, 16)
                for i, (kt, h, c) in enumerate(GAT_SHAPES):
                    sp.dma_start(g.w_gat[i][:, :, 0:h * c], a[f"L2_gnn_W{i}"].rearrange("(k p) f -> p k f", p=FULL)).then_inc(g.gat_loaded, 16)
                    for j, side in enumerate(("src", "dst")):
                        vec = a[f"L2_gnn_a_{side}{i}"].rearrange("h c -> (h c)")
                        sp.dma_start(g.att[i][:, j, :], vec.partition_broadcast(FULL)).then_inc(g.gat_loaded, 16)
                    sp.dma_start(g.b_gat[i][:, :], a[f"L2_gnn_b{i}"].partition_broadcast(P)).then_inc(g.gat_loaded, 16)

            @block.gpsimd
            def _(pool):
                pool.iota(node_i[:, :], pattern=[[1, N]], base=0, channel_multiplier=0).then_inc(nodes_ready, 1)
                pool.iota(node_col_i[:, :], pattern=[[P, T]], base=0, channel_multiplier=1).then_inc(nodes_ready, 1)
                pool.iota(steps_i[:, :], pattern=[[1, T - 1]], base=0, channel_multiplier=0).then_inc(nodes_ready, 1)
                pool.iota(visit_i[:, :, :], pattern=[[1, VISITS], [0, RING]], base=0, channel_multiplier=0).then_inc(nodes_ready, 1)
                pool.memset(tri[:, :], 1.0).then_inc(tri_ready, 1)
                pool.wait_ge(tri_ready, 1)
                pool.affine_select(out=tri[:, :], in_=tri[:, :], compare_op=ALU.is_ge, fill=0.0, base=0,
                                   pattern=[[1, P]], channel_multiplier=-1).then_inc(tri_ready, 1)
                pool.memset(g.ident[:, :], 0.0).then_inc(ident_zero, 1)
                pool.memset(g.ones[:, :], 1.0).then_inc(g.consts_ready, 1)
                pool.wait_ge(ident_zero, 1)
                pool.affine_select(out=g.ident[:, :], in_=g.ident[:, :], compare_op=ALU.not_equal, fill=1.0,
                                   base=0, pattern=[[-1, FULL]], channel_multiplier=1).then_inc(g.consts_ready, 1)
                pool.wait_ge(g.consts_ready, 2)
                pool.tensor_copy(g.ident_bf[:, :], g.ident[:, :]).then_inc(g.consts_ready, 1)
                pool.memset(g.w_router[:, :, :, :], 0.0).then_inc(g.consts_ready, 1)
                pool.memset(g.b_strong2[:, :, :], 0.0).then_inc(g.consts_ready, 1)
                pool.wait_ge(g.consts_ready, 5)
                with nc.allow_non_contiguous_dma(reason="small weights, once"):
                    for l in range(LAYERS):
                        pool.dma_start(g.w_router[:, l, :, 0:NEXP], a["L3_gnn_router_W"][l].rearrange("(k p) e -> p k e", p=FULL)).then_inc(g.moe_loaded, 16)
                        pool.dma_start(g.w_router[:, l, 0:2, NEXP:NEXP + 1], a["L3_gnn_conf_W"][l].rearrange("(k p) e -> p k e", p=FULL)).then_inc(g.moe_loaded, 16)
                        pool.dma_start(g.b_strong1[:, l, :, :], a["L3_gnn_strong_b1"][l].rearrange("e (k p) -> p e k", p=FULL)).then_inc(g.moe_loaded, 16)
                    pool.dma_start(g.b_router[:, :, 0:NEXP], a["L3_gnn_router_b"].partition_broadcast(P)).then_inc(g.moe_loaded, 16)
                    pool.dma_start(g.b_router[:, :, NEXP:NEXP + 1], a["L3_gnn_conf_b"].partition_broadcast(P)).then_inc(g.moe_loaded, 16)
                    pool.dma_start(g.b_strong2[NW:NEXP, :, :], a["L3_gnn_strong_b2"].rearrange("l e f -> e l f")).then_inc(g.moe_loaded, 16)
                    pool.dma_start(g.w_in[:, :], a["L3_gnn_W_in"]).then_inc(g.moe_loaded, 16)
                    pool.dma_start(g.b_in[:, :], a["L3_gnn_b_in"].partition_broadcast(P)).then_inc(g.moe_loaded, 16)
                    pool.dma_start(g.w_out[:, :, :], a["L3_gnn_W_out"].rearrange("(k p) f -> p k f", p=FULL)).then_inc(g.moe_loaded, 16)
                    pool.dma_start(g.b_out[:, :], a["L3_gnn_b_out"].rearrange("(o f) -> o f", o=1)).then_inc(g.moe_loaded, 16)

            @block.scalar
            def _(act):
                act.wait_ge(edge_rows_ready, 2)
                act.dma_start(edge_rows(g.src_row), src16[:, :, :]).then_inc(rows_written, 16)
                act.dma_start(edge_rows(g.keep_row[1:E + 1]), keep[:, :, :]).then_inc(rows_written, 16)
                act.dma_start(g.keep_row[0:1].rearrange("(o c) -> o c", o=1), zero16[:, 0:1]).then_inc(rows_written, 16)
                act.wait_ge(rows_written, 48)
                act.dma_start(g.src_all[:, 0:E], g.src_row.partition_broadcast(P)).then_inc(g.edges_spread, 16)
                act.dma_start(g.keep_all[:, :], g.keep_row[0:E].partition_broadcast(FULL)).then_inc(g.edges_spread, 16)
                act.wait_ge(flag_ready, 1)
                by_runs = act.value_load(g.is_sorted[0:1, 0:1], min_val=0, max_val=1)
                with act.If(by_runs != 0):
                    act.wait_ge(minus_dst_ready, 1)
                    with act.Fori(0, VISITS // 2 // ODD_EACH) as i:
                        for n in range(ODD_EACH):
                            act.wait_ge(dst_hot_ready_s, i * ODD_EACH + n)
                            for k in range(RING):
                                column = i * (2 * RING * ODD_EACH) + ((2 * n + 1) * RING + k)
                                last = nc.scalar.activation(distance[:, k, :], node[:, 0:P], ACT.Abs, bias=minus_dst[:, ds(column, 1)])
                            last.then_inc(distance_ready, 1)
                            act.wait_ge(distance_ready, i * ODD_EACH + (n + 1))
                            act.wait_ge(onehot_used, i * (2 * RING * ODD_EACH) + 2 * RING * n)
                            nc.scalar.activation(dst_hot[:, 1, :, :], distance[:, :, :], ACT.Relu, bias=g.ones[0:P, 0:1],
                                                 scale=-1.0).then_inc(dst_hot_ready_s, 1)
                act.wait_ge(counts_ready, 1)
                for t in range(3):
                    nc.scalar.copy(g.count_t[:, t, 0:WIDE], row_main(t)).then_inc(counts_copied_s, 1)
                act.wait_ge(turned, 1)
                for t in range(3):
                    nc.scalar.copy(g.count[:, t, 0:WIDE], row_main(t)).then_inc(turned_copied_s, 1)

            @block.tensor
            def _(pe):
                pe.wait_ge(ends_f_ready, 1)
                pe.wait_ge(g.consts_ready, 2)
                for side in range(2):
                    for k in range(ROW_PARTS):
                        at = side * CHUNKS + k * ROWS_EACH
                        last = nc.tensor.transpose(g.bank(7)[0:P, at:at + ROWS_EACH], ends_f[:, side, k, :],
                                                   g.ident[0:ROWS_EACH, 0:ROWS_EACH])
                last.then_inc(ends_turned, 1)
                pe.wait_ge(zero_ready, 1)
                for t in range(T):
                    nc.tensor.matmul(row_main(t), zero16[:, 0:P], zero16[:, 0:WIDE], start=True, stop=False, skip_group_check=True)
                    nc.tensor.matmul(row_rest(t), zero16[:, 0:P], zero16[:, 0:P], start=t in (0, 4), stop=False, skip_group_check=True)
                pe.wait_ge(ends_ready, 1)
                pe.wait_ge(fall_ready, 1)
                nc.tensor.matmul(g.bank(7)[0:P, LASTS:LASTS + GROUPS], g.ident[0:P, P - 1:P].broadcast_to([P, P]),
                                 ends[:, 1, PAD:PAD + CHUNKS].rearrange("p (v k) -> p v k", k=RING)[:, :, RING - 1],
                                 start=True, stop=True)
                nc.tensor.matmul(g.bank(7)[0:P, FLAG:FLAG + 1], g.ones[0:ROWS_EACH, 0:P], any_fall[:, :],
                                 start=True, stop=True).then_inc(lasts_spread, 1)
                pe.wait_ge(flag_ready, 1)
                by_runs = pe.value_load(g.is_sorted[0:1, 0:1], min_val=0, max_val=1)

                def count_visit(v, parity, pair):
                    pe.wait_ge(dst_hot_ready_s if parity else dst_hot_ready_v, pair + 1)
                    tile = pe.value_load(tile_reg[0:1, ds(v, 1)], min_val=0, max_val=T - 1)
                    for k in range(RING):
                        pe.wait_ge(onehot_ready, v * RING + (k + 1))
                        lhs = dst_hot[:, parity, k, :]
                        nc.tensor.matmul(psum[0:P, ds(tile * 512, WIDE)], lhs, onehot[:, k, 0, 0:WIDE], start=False, stop=False,
                                         skip_group_check=True)
                        nc.tensor.matmul(psum[0:P, ds(tile * FULL + REST, P)], lhs, onehot[:, k, 0, WIDE:N], start=False, stop=False,
                                         skip_group_check=True).then_inc(onehot_used, 1)

                def count_chunk(k, c):
                    pe.wait_ge(onehot_ready, c + 1)
                    for t in range(T):
                        lhs = onehot[:, k, 1, t * P:(t + 1) * P]
                        nc.tensor.matmul(row_main(t), lhs, onehot[:, k, 0, 0:WIDE], start=False, stop=False, skip_group_check=True)
                        last = nc.tensor.matmul(row_rest(t), lhs, onehot[:, k, 0, WIDE:N], start=False, stop=False, skip_group_check=True)
                    last.then_inc(onehot_used, 1)

                with pe.If(by_runs != 0):
                    pe.wait_ge(tiles_ready, 1)
                    count_visit(0, 0, 0)
                    with pe.Fori(0, VISITS // 2) as i:
                        count_visit(i * 2 + 1, 1, i)
                        count_visit(i * 2 + 2, 0, i + 1)
                    pe.wait_ge(onehot_used, STEPS)
                with pe.Else():
                    with pe.Fori(0, GROUPS) as i:
                        for k in range(RING):
                            count_chunk(k, i * RING + k)
                    pe.wait_ge(onehot_used, CHUNKS)
                nc.tensor.matmul(g.bank(7)[0:P, 0:1], zero16[:, 0:P], zero16[:, 0:1], start=True, stop=True).then_inc(counts_ready, 1)
                pe.wait_ge(counts_copied_v, 3)
                pe.wait_ge(counts_copied_s, 3)
                for s in range(T):
                    for d in range(T):
                        to = row_main(s)[:, d * P:(d + 1) * P] if d < 4 else row_rest(s)
                        last = nc.tensor.transpose(to, g.count_t[:, d, s * P:(s + 1) * P], g.ident[0:P, 0:P])
                last.then_inc(turned, 1)
                pe.wait_ge(degree_ready, 1)
                pe.wait_ge(tri_ready, 2)
                nc.tensor.matmul(g.bank(7)[0:P, 0:T], tri[:, :], g.degree[:, :], start=True, stop=False)
                nc.tensor.matmul(g.bank(7)[0:P, 0:T], g.ones[0:P, 0:P], before[:, 0:T], start=False, stop=True).then_inc(ends_done, 1)

            @block.vector
            def _(dve):
                chain = Chain(dve, g.dve_chain)
                nc.vector.memset(next_i[:, :, :], 1 << 20).then_inc(next_zero, 1)
                nc.vector.memset(zero16[:, :], 0.0).then_inc(zero_ready, 1)
                chain.link(nc.vector.memset(ends[:, :, :], 0.0))
                dve.wait_ge(g.edges_loaded, 32)
                nc.vector.tensor_copy(ends_f[:, :, :, :], ends_i[:, :, :, :]).then_inc(ends_f_ready, 1)
                dve.wait_ge(ends_f_ready, 1)
                nc.vector.tensor_copy(src16[:, :, :], ends_f[:, 0, :, :]).then_inc(edge_rows_ready, 1)
                dve.wait_ge(next_loaded, 16 * (ROW_PARTS + 1))
                chain.link(nc.vector.tensor_copy(next_f[:, :, :], next_i[:, :, :]))
                nc.vector.tensor_tensor(keep[:, :, :], next_f[:, :, :], ends_f[:, 1, :, :], ALU.is_equal).then_inc(edge_rows_ready, 1)
                chain.link(nc.vector.tensor_tensor(falls[:, :, :], next_f[:, :, :], ends_f[:, 1, :, :], ALU.is_lt))
                nc.vector.tensor_reduce(any_fall[:, :], falls[:, :, :], AX.XY, ALU.max).then_inc(fall_ready, 1)
                dve.wait_ge(ends_turned, 1)
                nc.vector.tensor_copy(ends[:, :, PAD:PAD + CHUNKS],
                                      g.bank(7)[0:P, 0:2 * CHUNKS].rearrange("p (s c) -> p s c", s=2)).then_inc(ends_ready, 1)
                dve.wait_ge(nodes_ready, 4)
                nc.vector.tensor_copy(node[:, :], node_i[:, :])
                nc.vector.tensor_copy(g.node_col[:, :], node_col_i[:, :])
                nc.vector.tensor_copy(steps[:, :], steps_i[:, :])
                chain.link(nc.vector.tensor_copy(visit[:, :], visit_i[:, :, :].rearrange("p v k -> p (v k)")))
                dve.wait_ge(ends_ready, 1)
                dve.wait_ge(lasts_spread, 1)
                nc.vector.tensor_scalar(g.is_sorted[:, :], g.bank(7)[0:1, FLAG:FLAG + 1], 0.0, None, ALU.is_le).then_inc(flag_ready, 1)
                for t in range(T - 1):
                    last = nc.vector.tensor_scalar(below[:, t, :], g.bank(7)[0:P, LASTS:LASTS + GROUPS], float(P * (t + 1)), None, ALU.is_lt)
                chain.link(last)
                chain.link(nc.vector.tensor_reduce(last_visit[:, :], below[:, :, :], AX.X, ALU.add))
                chain.link(nc.vector.scalar_tensor_tensor(last_visit[:, :], last_visit[:, :], float(GROUPS - 1), steps[:, :], ALU.min, ALU.add))
                chain.link(nc.vector.tensor_tensor(left[:, :, :], visit[:, :].unsqueeze(2).broadcast_to([P, STEPS, T - 1]),
                                                   last_visit[:, :].unsqueeze(1).broadcast_to([P, STEPS, T - 1]), ALU.is_gt))
                chain.link(nc.vector.tensor_reduce(tile_of[:, :], left[:, :, :], AX.X, ALU.add))
                nc.vector.tensor_copy(tile_reg[:, :], tile_of[0:1, :].rearrange("p (v k) -> p v k", k=RING)[:, :, 0]).then_inc(tiles_ready, 1)
                for t in range(T):
                    at = PAD - t * RING
                    last = nc.vector.scalar_tensor_tensor(picked[:, :, :, t], tile_of[:, :].unsqueeze(1).broadcast_to([P, 2, STEPS]), float(t),
                                                          ends[:, :, at:at + STEPS], ALU.is_equal, ALU.mult)
                chain.link(last)
                chain.link(nc.vector.tensor_reduce(visit_ends[:, :, :], picked[:, :, :, :], AX.X, ALU.add))
                chain.link(nc.vector.scalar_tensor_tensor(visit_dst[:, :], tile_of[:, :], -float(P), visit_ends[:, 1, :], ALU.mult, ALU.add))
                nc.vector.scalar_tensor_tensor(minus_dst[:, :], tile_of[:, :], float(P), visit_ends[:, 1, :], ALU.mult, ALU.subtract).then_inc(minus_dst_ready, 1)
                dve.wait_ge(flag_ready, 1)
                by_runs = dve.value_load(g.is_sorted[0:1, 0:1], min_val=0, max_val=1)

                def one_hot(k, side, column):
                    return nc.vector.tensor_scalar(onehot[:, k, side, :], node[:, :], column, None, ALU.is_equal)

                def visit_dsts(v):
                    nc.vector.tensor_tensor(dst_hot[:, 0, :, :], node[:, 0:P].unsqueeze(1).broadcast_to([P, RING, P]),
                                            visit_dst[:, ds(v * RING, RING)].unsqueeze(2).broadcast_to([P, RING, P]),
                                            ALU.is_equal).then_inc(dst_hot_ready_v, 1)

                with dve.If(by_runs != 0):
                    visit_dsts(0)
                    for k in range(RING):
                        one_hot(k, 0, visit_ends[:, 0, k:k + 1]).then_inc(onehot_ready, 1)
                    with dve.Fori(0, VISITS // 2) as i:
                        for n in (1, 2):
                            if n == 2:
                                visit_dsts(i * 2 + n)
                            for k in range(RING):
                                dve.wait_ge(onehot_used, i * (2 * RING) + ((n - 1) * RING + k + 1))
                                one_hot(k, 0, visit_ends[:, 0, ds(i * (2 * RING) + (n * RING + k), 1)]).then_inc(onehot_ready, 1)
                with dve.Else():
                    for k in range(RING):
                        one_hot(k, 0, ends[:, 0, PAD + k:PAD + k + 1])
                        one_hot(k, 1, ends[:, 1, PAD + k:PAD + k + 1]).then_inc(onehot_ready, 1)
                    with dve.Fori(1, GROUPS) as i:
                        for k in range(RING):
                            dve.wait_ge(onehot_used, (i - 1) * RING + (k + 1))
                            one_hot(k, 0, ends[:, 0, ds(i * RING + (PAD + k), 1)])
                            one_hot(k, 1, ends[:, 1, ds(i * RING + (PAD + k), 1)]).then_inc(onehot_ready, 1)
                dve.wait_ge(counts_ready, 1)
                rests = psum[0:P, REST:REST + T * FULL].rearrange("p (t n) -> p t n", n=FULL)[:, :, 0:P]

                def copy_rows(to, copied):
                    for t in (3, 4):
                        nc.vector.tensor_copy(to[:, t, 0:WIDE], row_main(t)).then_inc(copied, 1)
                    nc.vector.tensor_copy(to[:, :, WIDE:N], rests).then_inc(copied, 1)

                copy_rows(g.count_t, counts_copied_v)
                dve.wait_ge(counts_copied_v, 3)
                dve.wait_ge(counts_copied_s, 3)
                chain.link(nc.vector.tensor_reduce(g.degree[:, :], g.count_t[:, :, :], AX.X, ALU.add))
                dve.wait_ge(turned, 1)
                copy_rows(g.count, turned_copied_v)
                chain.link(nc.vector.memset(before[:, 0:1], 0.0))
                for t in range(T):
                    chain.link(nc.vector.tensor_tensor(before[:, t + 1:t + 2], before[:, t:t + 1], g.degree[:, t:t + 1], ALU.add))
                nc.vector.tensor_scalar(g.some_edge[:, :], g.degree[:, :], 1.0, None, ALU.min).then_inc(degree_ready, 1)
                chain.link(nc.vector.tensor_scalar(g.recip_deg[:, :], g.degree[:, :], 1.0, None, ALU.max))
                nc.vector.reciprocal(g.recip_deg[:, :], g.recip_deg[:, :])
                dve.wait_ge(ends_done, 1)
                chain.link(nc.vector.tensor_scalar(last_place[:, :], g.bank(7)[0:P, 0:T], -1.0, 0.0, ALU.add, ALU.max))
                chain.link(nc.vector.tensor_copy(g.run_end[:, :], last_place[:, :]))
                g.dve_links = chain.done


def sage(nc, g):
    FIRST = 1
    BODY = 4
    TURNS = (P - FIRST) // BODY
    RING = 4
    GROUPS = E // N
    AHEAD = 3
    assert GROUPS * N == E and (GROUPS - AHEAD) % 2 == 0
    with ExitStack() as ctx:
        def sb(name, shape, dt=F32):
            return ctx.enter_context(nc.sbuf_tensor(name, shape, dt))

        def sem(name):
            return ctx.enter_context(nc.semaphore(name))

        far = sb("far", [P, T, N], BF16)
        agg_t = sb("agg_t", [FULL, T, P])
        staged = sb("staged", [FULL, T, BODY])
        pool_n = sb("pool_n", [P, T, D])
        parts = sb("parts", [P, 2, T, D], F32R)
        src_hot = sb("src_hot", [P, 2, T, N + 1], F32R)
        running = sb("running", [FULL, 2, N])
        pool_t = running[:, 0, :]
        rows = sb("rows", [P, 2, T, D])
        agg_n = g.xb
        has_edge_t = g.keep_all[0:P, 0:T * N].rearrange("p (t n) -> p t n", t=T)
        masked = g.keep_all[:, T * N:(T + RING) * N].rearrange("p (k n) -> p k n", k=RING)
        att_prod = g.x_t[:, 1, 0:2 * HID].rearrange("p (k f) -> p k f", k=2)
        far_ready = sem("far_ready")
        count_floored = sem("count_floored")
        log_ready = sem("log_ready")
        turned = sem("sage_turned")
        x_t_ready = sem("sage_x_t_ready")
        agg_ready = sem("agg_ready")
        summed = sem("sage_summed")
        self_added = sem("self_added")
        has_edge_ready = sem("has_edge_ready")
        pooled = sem("pooled")
        pool_ready = sem("pool_ready")
        row_ready = sem("row_ready")
        row_used = sem("row_used")
        row_seen = sem("row_seen")
        any_chain = sem("any_chain")
        pooled_n = sem("pooled_n")
        parts_chain = sem("parts_chain")
        parts_ready = sem("parts_ready")
        hot_ready = sem("hot_ready")
        messages_ready = sem("messages_ready")
        running_ready = sem("running_ready")
        running_turned = sem("running_turned")
        rows_copied = sem("rows_copied")
        rows_stored = [sem(f"rows{k}_stored") for k in range(2)]
        agg_fetched = sem("agg_fetched")
        agg_masked = sem("agg_masked")
        agg_turned = sem("agg_turned")
        psum = g.psum

        def row(k):
            return g.wide(2 * (k % RING))

        def messages(n, width=N):
            at = (2 * (n % 2) + 1) * 512 - HALF
            return psum[:, at:at + width]

        def turned_rows(n):
            b = 4 + 2 * (n % 2)
            return psum[0:P, b * 512:b * 512 + T * D]

        def wait_past(eng, semaphore, value):
            if not isinstance(value, int) or value > 0:
                eng.wait_ge(semaphore, value)

        def over_groups(eng, step):
            for n in range(AHEAD):
                step(n, n, n // 2)
            with eng.Fori(0, (GROUPS - AHEAD) // 2) as i:
                for n in range(AHEAD, AHEAD + 2):
                    step(n, i * 2 + n, i + n // 2)

        def stores(layer, parity):
            return layer * ((GROUPS + 1 - parity) // 2)

        with nc.Block() as block:
            @block.tensor
            def _(pe):
                by_runs = pe.value_load(g.is_sorted[0:1, 0:1], min_val=0, max_val=1)

                def any_order(layer, wp):
                    base = layer * N
                    for lo, hi in ROWS:
                        last = nc.tensor.matmul(g.wide(2)[:, lo:hi], wp, g.x_t[:, 0, lo:hi], start=True, stop=True)
                    last.then_inc(pooled, 1)
                    pe.wait_ge(pool_ready, layer + 1)
                    pe.wait_ge(has_edge_ready, 1)

                    def spread(k, p, t):
                        lhs = g.ident_bf[0:P, ds(p, 1)].broadcast_to([P, FULL])
                        for lo, hi in ROWS:
                            last = nc.tensor.matmul(row(k)[:, lo:hi], lhs, has_edge_t[:, t, lo:hi], start=True, stop=True)
                        last.then_inc(row_ready, 1)

                    for t in range(T):
                        wait_past(pe, row_used, base + t - RING + 1)
                        spread(base + t, 0, t)
                    with pe.Fori(0, TURNS) as i:
                        for j in range(BODY):
                            for t in range(T):
                                k = base + T * FIRST + j * T + t
                                pe.wait_ge(row_used, i * (BODY * T) + (k - RING + 1))
                                spread(k, i * BODY + (FIRST + j), t)

                def sorted_runs(layer, wp):
                    base = layer * GROUPS
                    for t in range(T):
                        last = nc.tensor.matmul(g.bank(t)[0:P, 0:D], g.x_t[:, 0, t * P:(t + 1) * P], wp, start=True, stop=True)
                    last.then_inc(pooled_n, 1)
                    pe.wait_ge(parts_ready, layer + 1)

                    def fetch(n, group):
                        pe.wait_ge(hot_ready, base + group + 1)
                        wait_past(pe, running_ready, base + group - 1)
                        for lo, hi in HALVES:
                            for k in range(2 * T):
                                part, s = k % 2, k // 2
                                last = nc.tensor.matmul(messages(n, hi)[:, lo:hi], parts[:, part, s, :], src_hot[:, n % 2, s, lo:hi],
                                                        start=k == 0, stop=k == 2 * T - 1)
                        last.then_inc(messages_ready, 1)

                    def turn(n, group):
                        pe.wait_ge(running_ready, base + group + 1)
                        wait_past(pe, rows_copied, base + group - 1)
                        for j in range(T):
                            last = nc.tensor.transpose(turned_rows(n)[:, j * D:(j + 1) * D], running[:, n % 2, j * P:(j + 1) * P],
                                                       g.ident[:, :])
                        last.then_inc(running_turned, 1)

                    def step(n, group, pair):
                        fetch(n, group)
                        if isinstance(group, int) and group == 0:
                            return
                        turn(n + 1, group - 1)

                    over_groups(pe, step)
                    turn(GROUPS - 1, GROUPS - 1)
                    pe.wait_ge(agg_masked, layer + 1)
                    for t in range(T):
                        last = nc.tensor.transpose(g.wide(0)[:, t * P:(t + 1) * P], agg_n[:, t, :], g.ident[0:P, 0:P])
                    last.then_inc(agg_turned, 1)

                pe.wait_ge(g.x_loaded, 16)
                for t in range(T):
                    last = nc.tensor.transpose(g.wide(0)[:, t * P:(t + 1) * P], g.xa[:, t, :], g.ident[0:P, 0:P])
                last.then_inc(turned, 1)
                pe.wait_ge(g.sage_loaded, 16 * 12)
                for layer in range(2):
                    wp, ws, wn = (g.w_sage[:, 3 * layer + i, :] for i in range(3))
                    pe.wait_ge(x_t_ready, layer + 1)
                    with pe.If(by_runs != 0):
                        sorted_runs(layer, wp)
                    with pe.Else():
                        any_order(layer, wp)
                    pe.wait_ge(agg_ready, layer + 1)
                    if layer == 0:
                        for lo, hi in ROWS:
                            nc.tensor.matmul(g.wide(0)[:, lo:hi], ws, g.x_t[:, 0, lo:hi], start=True, stop=False)
                            last = nc.tensor.matmul(g.wide(0)[:, lo:hi], wn, agg_t[:, :, :].rearrange("f t p -> f (t p)")[:, lo:hi],
                                                    start=False, stop=True)
                        last.then_inc(summed, 1)
                    else:
                        for t in range(T):
                            to = g.bank(t)[0:P, 0:D]
                            nc.tensor.matmul(to, g.x_t[:, 0, t * P:(t + 1) * P], ws, start=True, stop=False)
                            nc.tensor.matmul(to, agg_t[:, t, :], wn, start=False, stop=False)
                            last = nc.tensor.matmul(to, g.ones[0:1, 0:P], g.b_sage2[:, :], start=False, stop=True)
                        last.then_inc(summed, 1)

            @block.scalar
            def _(act):
                by_runs = act.value_load(g.is_sorted[0:1, 0:1], min_val=0, max_val=1)

                def any_order(layer):
                    act.wait_ge(pooled, layer + 1)
                    nc.scalar.activation(pool_t[:, :], g.wide(2), ACT.Relu, bias=g.b_sage[:, 2 * layer:2 * layer + 1]).then_inc(pool_ready, 1)

                def sorted_runs(layer):
                    base = layer * GROUPS
                    def step(n, group, pair):
                        act.wait_ge(running_turned, base + group + 1)
                        wait_past(act, rows_stored[n % 2], (pair + stores(layer, n % 2)) * 16)
                        nc.scalar.copy(rows[:, n % 2, :, :].rearrange("p j f -> p (j f)"), turned_rows(n)).then_inc(rows_copied, 1)

                    over_groups(act, step)
                    act.wait_ge(agg_turned, layer + 1)
                    nc.scalar.copy(agg_t[:, :, :].rearrange("f t p -> f (t p)"), g.wide(0)).then_inc(agg_ready, 1)

                act.wait_ge(turned, 1)
                nc.scalar.copy(g.x_t[:, 0, :], g.wide(0)).then_inc(x_t_ready, 1)
                act.wait_ge(g.sage_loaded, 16 * 12)
                for layer in range(2):
                    with act.If(by_runs != 0):
                        sorted_runs(layer)
                    with act.Else():
                        any_order(layer)
                    if layer == 0:
                        act.wait_ge(summed, 1)
                        nc.scalar.activation(g.x_t[:, 0, :], g.wide(0), ACT.Relu, bias=g.b_sage[:, 1:2]).then_inc(x_t_ready, 1)
                act.wait_ge(count_floored, 1)
                nc.scalar.activation(g.log_count[:, :, :], g.log_count[:, :, :], ACT.Ln).then_inc(log_ready, 1)
                g.layernorm_scalar(1)

            @block.sync
            def _(sp):
                by_runs = sp.value_load(g.is_sorted[0:1, 0:1], min_val=0, max_val=1)
                max_rows = g.max_rows.rearrange("(o j p) f -> p o j f", p=P, j=T)

                def sorted_runs(layer):
                    base = layer * GROUPS
                    if layer:
                        sp.wait_ge(agg_fetched, 16 * T * layer)

                    def step(n, group, pair):
                        sp.wait_ge(rows_copied, base + group + 1)
                        sp.dma_start(max_rows[:, ds(group, 1), :, :].rearrange("p o j f -> p (o j) f"), rows[:, n % 2, :, :]).then_inc(rows_stored[n % 2], 16)

                    over_groups(sp, step)

                for layer in range(2):
                    with sp.If(by_runs != 0):
                        sorted_runs(layer)
                sp.wait_ge(g.x_loaded, 16)

            @block.gpsimd
            def _(pool):
                by_runs = pool.value_load(g.is_sorted[0:1, 0:1], min_val=0, max_val=1)

                def sorted_runs(layer):
                    for parity in range(2):
                        pool.wait_ge(rows_stored[parity], 16 * stores(layer + 1, parity))
                    if layer:
                        pool.wait_ge(agg_turned, layer)
                    for t in range(T):
                        pool.indirect_dma_start(out=agg_n[:, t, :], out_offset=None, in_=g.max_rows,
                                                in_offset=bass.IndirectOffsetOnAxis(ap=g.run_end[:, t:t + 1], axis=0)).then_inc(agg_fetched, 16)

                pool.tensor_copy(g.log_count[:, :, :], g.count[:, :, :]).then_inc(self_added, 1)
                pool.wait_ge(self_added, 1)
                for t in range(T):
                    block_t = g.log_count[:, t, t * P:(t + 1) * P]
                    last = pool.tensor_tensor(block_t, block_t, g.ident[0:P, 0:P], ALU.add)
                last.then_inc(self_added, 1)
                pool.wait_ge(self_added, 2)
                pool.tensor_scalar(far[:, :, :], g.log_count[:, :, :], 0.0, -BIG, ALU.is_le, ALU.mult).then_inc(far_ready, 1)
                pool.wait_ge(far_ready, 1)
                pool.tensor_scalar(g.log_count[:, :, :], g.log_count[:, :, :], 1.0, None, ALU.max).then_inc(count_floored, 1)
                for layer in range(2):
                    with pool.If(by_runs != 0):
                        sorted_runs(layer)
                pool.wait_ge(log_ready, 1)
                pool.tensor_tensor(g.log_count[:, :, :], g.log_count[:, :, :], far[:, :, :], ALU.add).then_inc(g.log_count_ready, 1)
                pool.wait_ge(g.x_loaded, 16)

            @block.vector
            def _(dve):
                by_runs = dve.value_load(g.is_sorted[0:1, 0:1], min_val=0, max_val=1)
                chain = Chain(dve, g.dve_chain)
                chain.done = g.dve_links
                local = Chain(dve, any_chain)
                split = Chain(dve, parts_chain)
                dve.wait_ge(g.edges_spread, 32)
                split.link(nc.vector.memset(g.src_all[:, E:E + 1], 0.0))

                def any_order(layer):
                    base = layer * N
                    if layer == 0:
                        nc.vector.tensor_scalar(has_edge_t, g.count_t[:, :, :], 1.0, None, ALU.min).then_inc(has_edge_ready, 1)
                    dve.wait_ge(pool_ready, layer + 1)

                    def top(k, ready, to):
                        if ready is not None:
                            dve.wait_ge(row_ready, ready)
                            dve.sem_inc(row_seen, 1)
                        nc.vector.tensor_tensor_reduce(out=masked[:, k % RING, :], in0=row(k), in1=pool_t[:, :], scale=1.0, scalar=0.0,
                                                       op0=ALU.mult, op1=ALU.max, accum_out=to).then_inc(row_used, 1)

                    for t in range(T):
                        top(base + t, base + t + 1, staged[:, t, 0:1])
                    dve.wait_ge(row_used, base + T)
                    local.link(nc.vector.tensor_copy(agg_t[:, :, 0:1], staged[:, :, 0:1]))
                    with dve.Fori(0, TURNS) as i:
                        local.enter(i, 1)
                        for j in range(BODY):
                            for t in range(T):
                                k = base + T * FIRST + j * T + t
                                top(k, i * (BODY * T) + (k + 2) if (j * T + t) % 2 == 0 else None, staged[:, t, j:j + 1])
                        dve.wait_ge(row_used, i * (BODY * T) + (base + T * FIRST + BODY * T))
                        local.link(nc.vector.tensor_copy(agg_t[:, :, ds(i * BODY + FIRST, BODY)], staged[:, :, :]))
                    local.leave(TURNS)
                    nc.vector.engine_nop().then_inc(agg_ready, 1)

                def sorted_runs(layer):
                    base = layer * GROUPS
                    dve.wait_ge(pooled_n, layer + 1)
                    products = psum[0:P, 0:T * 512].rearrange("p (t f) -> p t f", f=512)[:, :, 0:D]
                    split.link(nc.vector.tensor_tensor(pool_n[:, :, :], products, g.b_pool[:, layer, :].unsqueeze(1).broadcast_to([P, T, D]), ALU.add))
                    split.link(nc.vector.tensor_scalar(parts[:, 0, :, :], pool_n[:, :, :], 0.0, None, ALU.max))
                    nc.vector.scalar_tensor_tensor(parts[:, 1, :, :], pool_n[:, :, :], 0.0, parts[:, 0, :, :].bitcast(F32),
                                                   ALU.max, ALU.subtract).then_inc(parts_ready, 1)

                    def one_hot(n, group):
                        wait_past(dve, messages_ready, base + group - 1)
                        for t in range(T):
                            last = nc.vector.tensor_scalar(src_hot[:, n % 2, t, :], g.src_all[:, ds(group * N, N + 1)], g.node_col[:, t:t + 1],
                                                           None, ALU.is_equal)
                        last.then_inc(hot_ready, 1)

                    def scan(n, group):
                        dve.wait_ge(messages_ready, base + group + 1)
                        wait_past(dve, running_turned, base + group - 1)
                        wait_past(dve, running_ready, base + group)
                        first = isinstance(group, int) and group == 0
                        nc.vector.tensor_tensor_scan(running[:, n % 2, :], g.keep_all[:, ds(group * N, N)], messages(n),
                                                     0.0 if first else running[:, (n + 1) % 2, N - 1:N], ALU.mult, ALU.max).then_inc(running_ready, 1)

                    def step(n, group, pair):
                        one_hot(n, group)
                        if isinstance(group, int) and group == 0:
                            return
                        scan(n + 1, group - 1)

                    over_groups(dve, step)
                    scan(GROUPS - 1, GROUPS - 1)
                    dve.wait_ge(agg_fetched, 16 * T * (layer + 1))
                    nc.vector.tensor_tensor(agg_n[:, :, :], agg_n[:, :, :], g.some_edge[:, :].unsqueeze(2).broadcast_to([P, T, D]),
                                            ALU.mult).then_inc(agg_masked, 1)

                for layer in range(2):
                    with dve.If(by_runs != 0):
                        sorted_runs(layer)
                    with dve.Else():
                        any_order(layer)
                dve.wait_ge(g.gat_loaded, 16 * 12)
                for i, (kt, h, c) in enumerate(GAT_SHAPES):
                    for side in range(2):
                        to = att_prod[:, 0:kt, 0:h * c]
                        chain.link(nc.vector.tensor_tensor(to, g.w_gat[i][:, :, 0:h * c],
                                                           g.att[i][:, side, :].unsqueeze(1).broadcast_to([FULL, kt, h * c]), ALU.mult))
                        at = h * c + side * h
                        chain.link(nc.vector.tensor_reduce(g.w_gat[i][:, :, at:at + h], to.rearrange("p k (h c) -> p k h c", h=h), AX.X, ALU.add))
                dve.wait_ge(summed, 2)
                sums = psum[0:P, 0:T * 512].rearrange("p (t f) -> p t f", f=512)[:, :, 0:D]
                chain.link(nc.vector.tensor_tensor(g.res[:, :, :], sums, g.xa[:, :, :], ALU.add))
                chain.link(g.layernorm_vector(chain, g.res, g.xa, 1))
                g.dve_links = chain.done


def propagate(nc, g):
    with ExitStack() as ctx:
        def sb(name, shape, dt=F32):
            return ctx.enter_context(nc.sbuf_tensor(name, shape, dt))

        def sem(name):
            return ctx.enter_context(nc.semaphore(name))

        spread = sem("deg_spread")
        summed = sem("prop_summed")
        psum = g.psum
        with nc.Block() as block:
            @block.sync
            def _(sp):
                g.load_weak(sp, 0)
                g.load_strong(sp, 0, 0)
                g.load_strong(sp, 0, 1)
                sp.dma_start(g.b_weak[:, :, :], g.a["L3_gnn_weak_b"].rearrange("l e f -> l (e f)").partition_broadcast(P)).then_inc(g.b_weak_loaded, 16)

            @block.tensor
            def _(pe):
                for t in range(T):
                    last = nc.tensor.matmul(g.wide(5)[0:P, t * P:(t + 1) * P], g.recip_deg[:, t:t + 1].broadcast_to([P, P]),
                                            g.ident[0:P, 0:P], start=True, stop=True)
                last.then_inc(spread, 1)
                for s in range(T):
                    for d in range(T):
                        last = nc.tensor.matmul(g.bank(s)[0:P, 0:D], g.count_t[:, d, s * P:(s + 1) * P], g.xa[:, d, :],
                                                start=d == 0, stop=d == T - 1)
                last.then_inc(summed, 1)

            @block.scalar
            def _(act):
                g.layernorm_scalar(2)

            @block.vector
            def _(dve):
                chain = Chain(dve, g.dve_chain)
                chain.done = g.dve_links
                chain.link(nc.vector.tensor_scalar(g.no_edge_t[:, :, :], g.count_t[:, :, :], 0.0, -BIG, ALU.is_le, ALU.mult))
                for t in range(T):
                    block_t = g.no_edge_t[:, t, t * P:(t + 1) * P]
                    last = nc.vector.scalar_tensor_tensor(block_t, g.ident[0:P, 0:P], 0.0, block_t, ALU.is_equal, ALU.mult)
                chain.link(last)
                dve.wait_ge(spread, 1)
                for t in range(T):
                    last = nc.vector.tensor_tensor(g.count[:, t, :], g.count[:, t, :], g.wide(5)[0:P, :], ALU.mult)
                chain.link(last)
                dve.wait_ge(summed, 1)
                sums = psum[0:P, 0:T * 512].rearrange("p (t f) -> p t f", f=512)[:, :, 0:D]
                chain.link(nc.vector.tensor_tensor(g.res[:, :, :], sums, g.xa[:, :, :], ALU.add))
                chain.link(g.layernorm_vector(chain, g.res, g.xb, 2))
                g.dve_links = chain.done


def gat(nc, g):
    SHAPES = GAT_SHAPES
    LOW_AHEAD = 2
    SMAX, ATT, OUT = 0, 2, 6
    with ExitStack() as ctx:
        def sb(name, shape, dt=F32):
            return ctx.enter_context(nc.sbuf_tensor(name, shape, dt))

        def sem(name):
            return ctx.enter_context(nc.semaphore(name))

        feats = [sb("feats4", [P, T, HEADS, HID // HEADS + 1]), sb("feats1", [P, T, 1, D + 1])]
        src_score = sb("src_score", [P, T, HEADS])
        src_low = sb("src_low", [P, T, HEADS])
        dst_score = sb("dst_score", [P, T, HEADS])
        top = sb("top", [P, T])
        high_row = sb("high_row", [P, T])
        low_row = sb("low_row", [P, T])
        masked = sb("gat_masked", [P, T, N], BF16)
        src_col = sb("src_col", [P, T])
        dst_rows = sb("dst_rows", [P, 2, N])
        score = sb("score", [P, T, N])
        prob = sb("prob", [P, T, N])
        recip = sb("recip", [P, T])
        heads_out = sb("heads_out", [P, T, HID])
        elu_e = sb("elu_e", [P, T, HID])
        ones_ready = sem("gat_ones_ready")
        turned = sem("gat_turned")
        x_t_ready_s = sem("gat_x_t_ready_s")
        x_t_ready_v = sem("gat_x_t_ready_v")
        feats_done = sem("feats_done")
        feats_ready = sem("feats_ready")
        src_score_ready = sem("src_score_ready")
        src_col_ready = sem("src_col_ready")
        src_spread = sem("src_spread")
        top_done = sem("top_done")
        spread_seen = sem("spread_seen")
        row_cols_ready = sem("row_cols_ready")
        rows_spread = sem("rows_spread")
        rows_ready = sem("gat_rows_ready")
        low_ready = sem("low_ready")
        score_ready = sem("score_ready")
        counted_ready = sem("counted_ready")
        prob_ready = sem("prob_ready")
        heads_summed = sem("heads_summed")
        heads_copied = sem("heads_copied")
        min_ready = sem("min_ready")
        elu_exp_ready = sem("elu_exp_ready")
        elu_ready = sem("elu_ready")
        psum = g.psum

        def spread(b, col):
            for t in range(T):
                last = nc.tensor.matmul(g.wide(b)[0:P, t * P:(t + 1) * P], col[:, t:t + 1].broadcast_to([P, P]),
                                        g.ident[0:P, 0:P], start=True, stop=True)
            return last

        with nc.Block() as block:
            @block.gpsimd
            def _(pool):
                pool.memset(feats[0][:, :, :, HID // HEADS:], 1.0).then_inc(ones_ready, 1)
                pool.memset(feats[1][:, :, :, D:], 1.0).then_inc(ones_ready, 1)
                base = 0
                for layer, (KT, H, C) in enumerate(SHAPES):
                    pool.wait_ge(src_score_ready, layer + 1)

                    def source_column(h, n):
                        pool.wait_ge(src_spread, n)
                        pool.tensor_copy(src_col[:, :], src_score[:, :, ds(h, 1)].rearrange("p t o -> p (t o)")).then_inc(src_col_ready, 1)

                    source_column(0, base)
                    if H > 1:
                        with pool.Fori(1, H) as h:
                            source_column(h, h + base)
                    base += H

            @block.tensor
            def _(pe):
                pe.wait_ge(g.gat_loaded, 16 * 12)
                for t in range(T):
                    last = nc.tensor.transpose(g.wide(0)[:, t * P:(t + 1) * P], g.xb[:, t, :], g.ident[0:P, 0:P])
                last.then_inc(turned, 1)
                base = 0
                for layer, (KT, H, C) in enumerate(SHAPES):
                    w = g.w_gat[layer]
                    x1 = feats[0 if H > 1 else 1]
                    pe.wait_ge(x_t_ready_s, layer + 1)
                    if layer:
                        pe.wait_ge(x_t_ready_v, layer)
                    for t in range(T):
                        for k in range(KT):
                            last = nc.tensor.matmul(g.bank(t)[0:P, 0:H * C + 2 * H], g.x_t[:, k, t * P:(t + 1) * P], w[:, k, :],
                                                    start=k == 0, stop=k == KT - 1)
                    last.then_inc(feats_done, 1)
                    pe.wait_ge(feats_ready, T * (layer + 1))
                    pe.wait_ge(src_score_ready, layer + 1)

                    def spread_source(n):
                        pe.wait_ge(src_col_ready, n + 1)
                        pe.wait_ge(top_done, n)
                        spread(SMAX, src_col).then_inc(src_spread, 1)

                    def spread_rows(n):
                        pe.wait_ge(row_cols_ready, n + 1)
                        pe.wait_ge(rows_ready, n)
                        spread(ATT, high_row)
                        spread(ATT + 2, low_row).then_inc(rows_spread, 1)

                    def aggregate(h, n):
                        pe.wait_ge(heads_copied, n)
                        if H == 1:
                            pe.wait_ge(ones_ready, 2)
                        for s in range(T):
                            pe.wait_ge(prob_ready, n * T + (s + 1))
                            for d in range(T):
                                b, at = (OUT, d) if d < 3 else (OUT + 1, d - 3)
                                last = nc.tensor.matmul(g.bank(b)[0:P, at * (C + 1):(at + 1) * (C + 1)],
                                                        prob[:, s, d * P:(d + 1) * P],
                                                        x1[:, s, ds(h, 1), :].rearrange("p h c -> p (h c)"),
                                                        start=s == 0 and at == 0, stop=s == T - 1, skip_group_check=True)
                        last.then_inc(heads_summed, 1)

                    if layer == 0:
                        pe.wait_ge(ones_ready, 2)
                    spread_source(base)
                    spread_rows(base)
                    if H > 1:
                        spread_source(base + 1)
                        with pe.Fori(0, H - 2) as h:
                            spread_rows(h + (base + 1))
                            spread_source(h + (base + 2))
                            aggregate(h, h + base)
                        spread_rows(base + H - 1)
                        aggregate(H - 2, base + H - 2)
                    aggregate(H - 1, base + H - 1)
                    base += H
                    if layer < 2:
                        for k in range(2):
                            pe.wait_ge(elu_ready, 2 * layer + k + 1)
                            for t in range(T):
                                last = nc.tensor.transpose(g.wide(2 * k)[:, t * P:(t + 1) * P],
                                                           heads_out[:, t, k * FULL:(k + 1) * FULL], g.ident[0:P, 0:P])
                            last.then_inc(turned, 1)

            @block.scalar
            def _(act):
                act.wait_ge(turned, 1)
                nc.scalar.copy(g.x_t[:, 0, :], g.wide(0)).then_inc(x_t_ready_s, 1)
                base = 0
                for layer, (KT, H, C) in enumerate(SHAPES):
                    x1 = feats[0 if H > 1 else 1]
                    act.wait_ge(src_score_ready, layer + 1)
                    for t in range(T):
                        nc.scalar.copy(x1[:, t, :, 0:C], g.bank(t)[0:P, 0:H * C].rearrange("p (h c) -> p h c", h=H)).then_inc(feats_ready, 1)

                    def fetch_rows(n):
                        act.wait_ge(rows_spread, n + 1)
                        act.wait_ge(score_ready, n * T)
                        both = psum[0:P, ATT * 512:(ATT + 4) * 512].rearrange("p (r f) -> p r f", r=2)[:, :, EDGE:EDGE + N]
                        nc.scalar.copy(dst_rows[:, :, :], both).then_inc(rows_ready, 1)

                    def head(h, n):
                        act.wait_ge(rows_ready, n + 1)
                        for s in range(T + LOW_AHEAD):
                            if s < T:
                                nc.scalar.activation(score[:, s, :], dst_rows[:, 1, :], ACT.Identity,
                                                     bias=src_low[:, s, ds(h, 1)]).then_inc(low_ready, 1)
                            if s >= LOW_AHEAD:
                                e = s - LOW_AHEAD
                                act.wait_ge(counted_ready, n * T + e + 1)
                                if e == 0:
                                    act.wait_ge(heads_summed, n)
                                nc.scalar.activation(prob[:, e, :], score[:, e, :], ACT.Exp).then_inc(prob_ready, 1)

                    fetch_rows(base)
                    if H > 1:
                        with act.Fori(0, H - 1) as h:
                            head(h, h + base)
                            fetch_rows(h + (base + 1))
                    head(H - 1, base + H - 1)
                    base += H
                    if layer < 2:
                        for k in range(2):
                            act.wait_ge(min_ready, 2 * layer + k + 1)
                            half = elu_e[:, :, k * FULL:(k + 1) * FULL]
                            nc.scalar.activation(half, half, ACT.Exp).then_inc(elu_exp_ready, 1)
                        act.wait_ge(turned, 2 * layer + 2)
                        nc.scalar.copy(g.x_t[:, 0, :], g.wide(0)).then_inc(x_t_ready_s, 1)
                g.layernorm_scalar(3)

            @block.vector
            def _(dve):
                chain = Chain(dve, g.dve_chain)
                chain.done = g.dve_links
                dve.wait_ge(g.gat_loaded, 16 * 12)
                base = 0
                for layer, (KT, H, C) in enumerate(SHAPES):
                    dve.wait_ge(feats_done, layer + 1)
                    scores = psum[0:P, 0:T * 512].rearrange("p (t f) -> p t f", f=512)[:, :, H * C:H * C + 2 * H]
                    nc.vector.tensor_copy(src_score[:, :, 0:H], scores[:, :, 0:H])
                    nc.vector.tensor_copy(dst_score[:, :, 0:H], scores[:, :, H:2 * H])
                    nc.vector.tensor_scalar(src_low[:, :, 0:H], scores[:, :, 0:H], NEG_SLOPE, None, ALU.mult).then_inc(src_score_ready, 1)
                    dve.wait_ge(src_score_ready, layer + 1)

                    def maximum(h, n):
                        dve.wait_ge(src_spread, n + 1)
                        dve.sem_inc(spread_seen, 1)
                        for t in range(T):
                            last = nc.vector.tensor_tensor_reduce(out=masked[:, t, :], in0=g.wide(SMAX)[0:P, :], in1=g.no_edge_t[:, t, :],
                                                                  scale=1.0, scalar=-3.0e38, op0=ALU.add, op1=ALU.max,
                                                                  accum_out=top[:, t:t + 1])
                        last.then_inc(top_done, 1)
                        dve.wait_ge(top_done, n + 1)
                        dve.wait_ge(rows_spread, n)
                        d_col = dst_score[:, :, ds(h, 1)].rearrange("p t o -> p (t o)")
                        chain.link(nc.vector.tensor_tensor(top[:, :], top[:, :], d_col, ALU.add))
                        chain.link(nc.vector.scalar_tensor_tensor(top[:, :], top[:, :], NEG_SLOPE, top[:, :], ALU.mult, ALU.max))
                        nc.vector.tensor_tensor(high_row[:, :], d_col, top[:, :], ALU.subtract)
                        nc.vector.scalar_tensor_tensor(low_row[:, :], d_col, NEG_SLOPE, top[:, :], ALU.mult, ALU.subtract).then_inc(row_cols_ready, 1)

                    def weigh(h, n):
                        dve.wait_ge(rows_ready, n + 1)
                        for s in range(T + 1):
                            if s < T:
                                dve.wait_ge(low_ready, n * T + (s + 1))
                                nc.vector.scalar_tensor_tensor(score[:, s, :], dst_rows[:, 0, :], src_score[:, s, ds(h, 1)],
                                                               score[:, s, :], ALU.add, ALU.max).then_inc(score_ready, 1)
                            if s > 0:
                                dve.wait_ge(score_ready, n * T + s)
                                nc.vector.tensor_tensor(score[:, s - 1, :], score[:, s - 1, :], g.log_count[:, s - 1, :],
                                                        ALU.add).then_inc(counted_ready, 1)

                    def normalise(h, n):
                        dve.wait_ge(heads_summed, n + 1)
                        sums = [g.bank(OUT)[0:P, 0:3 * (C + 1)].rearrange("p (t c) -> p t c", c=C + 1),
                                g.bank(OUT + 1)[0:P, 0:2 * (C + 1)].rearrange("p (t c) -> p t c", c=C + 1)]
                        for (lo, hi), s in zip(((0, 3), (3, 5)), sums):
                            last = nc.vector.tensor_scalar(recip[:, lo:hi], s[:, :, C], 1e-16, None, ALU.add)
                        chain.link(last)
                        chain.link(nc.vector.reciprocal(recip[:, :], recip[:, :]))
                        for (lo, hi), s in zip(((0, 3), (3, 5)), sums):
                            to = heads_out[:, lo:hi, ds(h * C, C)]
                            last = nc.vector.tensor_tensor(to, s[:, :, 0:C], recip[:, lo:hi].unsqueeze(2).broadcast_to([P, hi - lo, C]), ALU.mult)
                        last.then_inc(heads_copied, 1)

                    if layer == 0:
                        dve.wait_ge(g.log_count_ready, 1)
                    maximum(0, base)
                    if H > 1:
                        maximum(1, base + 1)
                        weigh(0, base)
                        with dve.Fori(0, H - 2) as h:
                            chain.enter(h, 4)
                            maximum(h + 2, h + (base + 2))
                            normalise(h, h + base)
                            weigh(h + 1, h + (base + 1))
                        chain.leave(H - 2)
                        normalise(H - 2, base + H - 2)
                    def elu(k):
                        dve.wait_ge(heads_copied, base + H * (k + 1) // 2)
                        x, e = (y[:, :, k * FULL:(k + 1) * FULL] for y in (heads_out, elu_e))
                        chain.link(nc.vector.tensor_tensor(x, x, g.b_gat[layer][:, k * FULL:(k + 1) * FULL].unsqueeze(1).broadcast_to([P, T, FULL]), ALU.add))
                        nc.vector.tensor_scalar(e, x, 0.0, None, ALU.min).then_inc(min_ready, 1)
                        dve.wait_ge(elu_exp_ready, 2 * layer + k + 1)
                        nc.vector.scalar_tensor_tensor(x, e, -1.0, x, ALU.add, ALU.max).then_inc(elu_ready, 1)

                    weigh(H - 1, base + H - 1)
                    if layer < 2:
                        elu(0)
                    normalise(H - 1, base + H - 1)
                    if layer < 2:
                        elu(1)
                        dve.wait_ge(turned, 2 * layer + 3)
                        nc.vector.tensor_copy(g.x_t[:, 1, :], g.wide(2)).then_inc(x_t_ready_v, 1)
                    base += H
                dve.wait_ge(heads_copied, base)
                chain.link(nc.vector.tensor_tensor(heads_out[:, :, 0:D], heads_out[:, :, 0:D],
                                                   g.b_gat[2][:, :].unsqueeze(1).broadcast_to([P, T, D]), ALU.add))
                chain.link(nc.vector.tensor_tensor(g.res[:, :, :], heads_out[:, :, 0:D], g.xb[:, :, :], ALU.add))
                chain.link(g.layernorm_vector(chain, g.res, g.xa, 3))
                g.dve_links = chain.done


def moe(nc, g):
    a = g.a
    MOE_LOADS = 16 * (3 * LAYERS + 7)
    WEAK_BANK, STRONG_BANK = 4, 6
    LOGIT_BANK = 0
    ITEMS = 1 + NS
    BIAS_AFTER_ROW = {1: (0, 1), 2: (2, 3), 3: (4,)}
    PAD = FULL
    WIDTH = T * PAD
    with ExitStack() as ctx:
        def sb(name, shape, dt=F32):
            return ctx.enter_context(nc.sbuf_tensor(name, shape, dt))

        def sem(name):
            return ctx.enter_context(nc.semaphore(name))

        h = sb("h", [P, T, HID])
        agg_t = sb("moe_agg_t", [FULL, 2, N])
        agg_hi = sb("agg_hi", [FULL, 2, WIDTH], F32R)
        agg_lo = sb("agg_lo", [FULL, 2, WIDTH], F32R)
        hidden_hi = sb("hidden_hi", [FULL, 4, WIDTH], F32R)
        hidden_lo = sb("hidden_lo", [FULL, 4, WIDTH], F32R)
        hidden_row = sb("hidden_row", [FULL, 2, WIDTH])
        w_hi = sb("w_hi", [FULL, 2, EXPERT], F32R)
        w_lo = sb("w_lo", [FULL, 2, EXPERT], F32R)
        tri = sb("tri", [P, NEXP, NEXP])
        logits = sb("logits", [P, T, NEXP + 1])
        beats = sb("beats", [P, T, NEXP, NEXP])
        ties = sb("ties", [P, T, NEXP, NEXP])
        rank = sb("rank", [P, T, NEXP])
        best = sb("best", [P, T])
        gate = sb("gate", [P, T, NEXP])
        shifted = sb("shifted", [P, T, NEXP])
        conf = sb("conf", [P, T])
        total = sb("total", [P, T])
        gate_t = sb("gate_t", [NEXP, N])
        weak_sum = sb("weak_sum", [P, 2, 2 * HID])
        moe_sum = sb("moe_sum", [P, T, HID])
        y = g.xb
        tri_ready = sem("tri_ready")
        x3_turned = sem("x3_turned")
        x3_t_ready = sem("x3_t_ready")
        h_done = sem("h_done")
        h_ready = sem("h_ready")
        turned = sem("moe_turned")
        h_t_ready_s = sem("h_t_ready_s")
        h_t_ready_v = sem("h_t_ready_v")
        agg_done = sem("agg_done")
        agg_ready_s = sem("agg_ready_s")
        agg_ready_v = sem("agg_ready_v")
        logits_done = sem("logits_done")
        shifted_ready = sem("shifted_ready")
        exps_ready = sem("exps_ready")
        gate_ready = sem("gate_ready")
        gate_turned = sem("gate_turned")
        gate_t_ready = sem("gate_t_ready")
        weak_done = sem("weak_done")
        weak_read = sem("weak_read")
        hidden_done = sem("hidden_done")
        hidden_hi_ready = sem("hidden_hi_ready")
        hidden_lo_ready = sem("hidden_lo_ready")
        pads_ready = sem("pads_ready")
        agg_hi_ready_s = sem("agg_hi_ready_s")
        agg_hi_ready_v = sem("agg_hi_ready_v")
        agg_lo_ready = sem("agg_lo_ready")
        w_hi_ready = sem("w_hi_ready")
        w_lo_ready = sem("w_lo_ready")
        strong_done = sem("strong_done")
        strong_read = sem("strong_read")
        weak_weighed = sem("weak_weighed")
        bias_done = sem("bias_done")
        bias_bank_seen = sem("bias_bank_seen")
        bias_read = sem("bias_read")
        y_done = sem("y_done")
        y_ready = sem("y_ready")
        stored = sem("stored")
        psum = g.psum
        WPAIR = NW // 2

        def slot(item):
            return (item + 1) % 2

        def raw_item(item):
            return (0, 1) if item == 0 else (1 + (item - 1) % 2, NS // 2)

        def split_high(eng, l, item):
            part, each = raw_item(item)
            eng.wait_ge(g.raw_loaded[part], l * (32 * each) + 32 * (max(item - 1, 0) // 2 + 1))
            nc.scalar.copy(w_hi[:, slot(item), :], g.w_raw[:, part, :]).then_inc(w_hi_ready, 1)

        def split_low(eng, l, item):
            eng.wait_ge(w_hi_ready, l * ITEMS + (item + 1))
            nc.vector.tensor_tensor(w_lo[:, slot(item), :], g.w_raw[:, raw_item(item)[0], :], w_hi[:, slot(item), :].bitcast(F32),
                                    ALU.subtract).then_inc(w_lo_ready, 1)

        def product(to, lefts, rights, start, stop):
            for n, (i, j) in enumerate(((0, 0), (0, 1), (1, 0))):
                last = nc.tensor.matmul(to, lefts[i], rights[j], start=start and n == 0, stop=stop and n == 2)
            return last

        def nodes(x, k):
            return x[:, k, :].rearrange("p (t n) -> p t n", n=PAD)[:, :, 0:P]

        def hidden_psum(n):
            at = (2 * (n % 2) + 1) * 512 - WIDTH // 2
            return psum[:, at:at + WIDTH]

        with nc.Block() as block:
            @block.sync
            def _(sp):
                def strong(l, e, used):
                    sp.wait_ge(w_lo_ready, used)
                    g.load_strong(sp, l, e)

                with sp.Fori(0, LAYERS - 1) as l:
                    sp.wait_ge(w_lo_ready, l * ITEMS + 1)
                    g.load_weak(sp, l + 1)
                    strong(l, 2, l * ITEMS + 2)
                    strong(l, 3, l * ITEMS + 3)
                    strong(l + 1, 0, l * ITEMS + 4)
                    strong(l + 1, 1, l * ITEMS + 5)
                strong(LAYERS - 1, 2, (LAYERS - 1) * ITEMS + 2)
                strong(LAYERS - 1, 3, (LAYERS - 1) * ITEMS + 3)
                sp.wait_ge(y_ready, 1)
                sp.dma_start(g.out.rearrange("(t p) f -> p t f", p=P), y[:, :, :]).then_inc(stored, 16)
                sp.wait_ge(stored, 16)

            @block.gpsimd
            def _(pool):
                for x in (agg_hi, agg_lo):
                    tiles = x[:, :, :].rearrange("p k (t n) -> p (k t) n", n=PAD)
                    some = g.ones[:, 0:2 * T * (PAD - P)].rearrange("p (k n) -> p k n", n=PAD - P)
                    pool.tensor_scalar(tiles[:, :, P:PAD], some, 0.0, None, ALU.mult).then_inc(pads_ready, 1)
                pool.memset(tri[:, :, :], 1.0).then_inc(tri_ready, 1)
                pool.wait_ge(tri_ready, 1)
                pool.affine_select(out=tri[:, :, :], in_=tri[:, :, :], compare_op=ALU.is_gt, fill=0.0, base=0,
                                   pattern=[[1, NEXP], [-1, NEXP]], channel_multiplier=0).then_inc(tri_ready, 1)

            @block.tensor
            def _(pe):
                pe.wait_ge(g.moe_loaded, MOE_LOADS)
                for t in range(T):
                    last = nc.tensor.transpose(g.wide(0)[:, t * P:(t + 1) * P], g.xa[:, t, :], g.ident[0:P, 0:P])
                last.then_inc(x3_turned, 1)
                pe.wait_ge(x3_t_ready, 1)
                for t in range(T):
                    last = nc.tensor.matmul(g.bank(2 + t)[0:P, 0:HID], g.x_t[:, 0, t * P:(t + 1) * P], g.w_in[:, :], start=True, stop=True)
                last.then_inc(h_done, 1)

                def turn_h(n):
                    pe.wait_ge(h_ready, n + 1)
                    for k in range(2):
                        for t in range(T):
                            last = nc.tensor.transpose(g.wide(2 * k)[:, t * P:(t + 1) * P],
                                                       h[:, t, k * FULL:(k + 1) * FULL], g.ident[0:P, 0:P])
                    last.then_inc(turned, 1)

                with pe.Fori(0, LAYERS) as l:
                    turn_h(l)
                    for f in range(2):
                        for lo, hi in ROWS:
                            for s in range(T):
                                last = nc.tensor.matmul(g.wide(4 + 2 * f)[:, lo:hi], h[:, s, f * FULL:(f + 1) * FULL],
                                                        g.count[:, s, lo:hi], start=s == 0, stop=s == T - 1)
                    last.then_inc(agg_done, 1)
                    pe.wait_ge(h_t_ready_s, l + 1)
                    pe.wait_ge(h_t_ready_v, l + 1)

                    def logit_part(k, start, stop):
                        for t in range(T):
                            to = g.bank(LOGIT_BANK)[0:P, t * 16:t * 16 + NEXP + 1]
                            lhs = (g.x_t if k < 2 else agg_t)[:, k % 2, t * P:(t + 1) * P]
                            last = nc.tensor.matmul(to, lhs, g.w_router[:, ds(l, 1), k, :].rearrange("p l e -> p (l e)"),
                                                    start=start and t == 0, stop=stop, skip_group_check=True)
                        return last

                    logit_part(0, True, False)
                    logit_part(1, False, False)
                    pe.wait_ge(agg_ready_s, l + 1)
                    pe.wait_ge(agg_ready_v, l + 1)
                    logit_part(2, False, False)
                    logit_part(3, False, True).then_inc(logits_done, 1)
                    pe.wait_ge(pads_ready, 2)
                    pe.wait_ge(agg_lo_ready, 2 * l + 2)
                    pe.wait_ge(w_lo_ready, l * ITEMS + 1)
                    for t in range(T):
                        for q in range(WPAIR):
                            n = t * WPAIR + q
                            if n >= 2:
                                pe.wait_ge(weak_read, l * (T * WPAIR) + (n - 1))
                            for k in range(2):
                                at = (k * NW + 2 * q) * HID
                                last = product(g.bank(WEAK_BANK + n % 2)[:, :], [x[:, k, t * PAD:(t + 1) * PAD] for x in (agg_hi, agg_lo)],
                                               [w[:, slot(0), at:at + 2 * HID] for w in (w_hi, w_lo)], k == 0, k == 1)
                            last.then_inc(weak_done, 1)
                    pe.wait_ge(gate_ready, l + 1)
                    for t in range(T):
                        last = nc.tensor.transpose(g.wide(STRONG_BANK)[0:NEXP, t * P:(t + 1) * P], gate[:, t, :], g.ident[0:P, 0:P])
                    last.then_inc(gate_turned, 1)
                    for e in range(NS):
                        pe.wait_ge(w_lo_ready, l * ITEMS + (e + 2))
                        for m in range(4):
                            n = e * 4 + m
                            if n >= 2:
                                pe.wait_ge(hidden_hi_ready, l * (NS * 4) + (n - 1))
                            for lo in (0, WIDTH // 2):
                                hi = lo + WIDTH // 2
                                for k in range(2):
                                    at = k * FF + m * FULL
                                    last = product(hidden_psum(n)[:, lo:hi], [w[:, slot(e + 1), at:at + FULL] for w in (w_hi, w_lo)],
                                                   [x[:, k, lo:hi] for x in (agg_hi, agg_lo)], k == 0, k == 1)
                            last.then_inc(hidden_done, 1)
                            if n == 1:
                                pe.wait_ge(gate_t_ready, l + 1)
                                pe.wait_ge(weak_read, l * (T * WPAIR) + T * WPAIR)
                                pe.sem_inc(bias_bank_seen, 1)
                            for t in BIAS_AFTER_ROW.get(n, ()):
                                if t >= 2:
                                    pe.wait_ge(bias_read, l * T + (t - 1))
                                    pe.sem_inc(bias_bank_seen, 1)
                                nc.tensor.matmul(g.bank(WEAK_BANK + t % 2)[0:P, 0:HID], gate_t[:, t * P:(t + 1) * P],
                                                 g.b_strong2[:, ds(l, 1), :].rearrange("p l f -> p (l f)"), start=True, stop=True).then_inc(bias_done, 1)
                        def strong_part(t, ks):
                            for k in ks:
                                at = 2 * FF + k * HID
                                last = product(g.bank(STRONG_BANK + (e * T + t) % 2)[:, 0:HID], [x[:, k, t * PAD:(t + 1) * PAD] for x in (hidden_hi, hidden_lo)],
                                               [w[:, slot(e + 1), at:at + HID] for w in (w_hi, w_lo)], k == 0, k == 3)
                            return last

                        pe.wait_ge(hidden_lo_ready, l * (NS * 4) + (e * 4 + 3))
                        for t, ks in ((0, (0, 1, 2)), (1, (0, 1))):
                            if e * T + t >= 2:
                                pe.wait_ge(strong_read, l * (NS * T) + (e * T + t - 1))
                            strong_part(t, ks)
                        pe.wait_ge(hidden_lo_ready, l * (NS * 4) + (e * 4 + 4))
                        for t, ks in ((0, (3,)), (1, (2, 3)), (2, range(4)), (3, range(4)), (4, range(4))):
                            if t >= 2:
                                pe.wait_ge(strong_read, l * (NS * T) + (e * T + t - 1))
                            strong_part(t, ks).then_inc(strong_done, 1)

                turn_h(LAYERS)
                pe.wait_ge(h_t_ready_s, LAYERS + 1)
                pe.wait_ge(h_t_ready_v, LAYERS + 1)
                for t in range(T):
                    to = g.bank(t)[0:P, 0:D]
                    for k in range(2):
                        nc.tensor.matmul(to, g.x_t[:, k, t * P:(t + 1) * P], g.w_out[:, k, :], start=k == 0, stop=False)
                    last = nc.tensor.matmul(to, g.ones[0:1, 0:P], g.b_out[:, :], start=False, stop=True)
                last.then_inc(y_done, 1)

            @block.scalar
            def _(act):
                act.wait_ge(g.moe_loaded, MOE_LOADS)
                act.wait_ge(x3_turned, 1)
                nc.scalar.copy(g.x_t[:, 0, :], g.wide(0)).then_inc(x3_t_ready, 1)
                with act.Fori(0, LAYERS) as l:
                    act.wait_ge(turned, l + 1)
                    nc.scalar.copy(g.x_t[:, 0, :], g.wide(0)).then_inc(h_t_ready_s, 1)
                    act.wait_ge(strong_done, l * (NS * T))
                    split_high(act, l, 0)
                    split_high(act, l, 1)
                    act.wait_ge(agg_done, l + 1)
                    nc.scalar.copy(agg_t[:, 0, :], g.wide(4)).then_inc(agg_ready_s, 1)
                    nc.scalar.copy(nodes(agg_hi, 0), g.wide(4).rearrange("p (t n) -> p t n", n=P)).then_inc(agg_hi_ready_s, 1)
                    act.wait_ge(shifted_ready, l + 1)
                    nc.scalar.activation(shifted[:, :, :], shifted[:, :, :], ACT.Exp)
                    nc.scalar.activation(conf[:, :], conf[:, :], ACT.Exp, scale=-1.0).then_inc(exps_ready, 1)
                    act.wait_ge(gate_ready, l + 1)
                    for n in range(T * WPAIR):
                        t, q = divmod(n, WPAIR)
                        act.wait_ge(weak_read, l * (T * WPAIR) + (n + 1))
                        for j in range(2):
                            part = weak_sum[:, q, j * HID:(j + 1) * HID]
                            last = nc.scalar.activation(part, part, ACT.Relu, scale=gate[:, t, 2 * q + j:2 * q + j + 1])
                        last.then_inc(weak_weighed, 1)
                    for e in range(NS):
                        for m in range(4):
                            n = e * 4 + m
                            act.wait_ge(hidden_done, l * (NS * 4) + (n + 1))
                            if m == 0:
                                act.wait_ge(strong_done, l * (NS * T) + e * T)
                            if n >= 2:
                                act.wait_ge(hidden_lo_ready, l * (NS * 4) + (n - 1))
                            for to in (hidden_hi[:, m, :], hidden_row[:, n % 2, :]):
                                last = nc.scalar.activation(to, hidden_psum(n), ACT.Relu, bias=g.b_strong1[:, ds(l, 1), e, m])
                            last.then_inc(hidden_hi_ready, 1)
                        if e < NS - 1:
                            if e == 0:
                                act.wait_ge(weak_done, l * (T * WPAIR) + T * WPAIR)
                            split_high(act, l, e + 2)
                act.wait_ge(turned, LAYERS + 1)
                nc.scalar.copy(g.x_t[:, 0, :], g.wide(0)).then_inc(h_t_ready_s, 1)
                g.layernorm_scalar(4)

            @block.vector
            def _(dve):
                chain = Chain(dve, g.dve_chain)
                chain.done = g.dve_links
                dve.wait_ge(g.moe_loaded, MOE_LOADS)
                dve.wait_ge(h_done, 1)
                nc.vector.tensor_tensor(h[:, :, :], psum[0:P, 2 * 512:7 * 512].rearrange("p (t f) -> p t f", f=512)[:, :, 0:HID],
                                        g.b_in[:, :].unsqueeze(1).broadcast_to([P, T, HID]), ALU.add).then_inc(h_ready, 1)
                dve.wait_ge(tri_ready, 2)
                dve.wait_ge(g.b_weak_loaded, 16)
                with dve.Fori(0, LAYERS) as l:
                    chain.enter(l, 26)
                    dve.wait_ge(turned, l + 1)
                    nc.vector.tensor_copy(g.x_t[:, 1, :], g.wide(2)).then_inc(h_t_ready_v, 1)
                    split_low(dve, l, 0)
                    split_low(dve, l, 1)
                    dve.wait_ge(agg_done, l + 1)
                    nc.vector.tensor_copy(agg_t[:, 1, :], g.wide(6)).then_inc(agg_ready_v, 1)
                    nc.vector.tensor_copy(nodes(agg_hi, 1), g.wide(6).rearrange("p (t n) -> p t n", n=P)).then_inc(agg_hi_ready_v, 1)
                    dve.wait_ge(agg_ready_v, l + 1)
                    dve.wait_ge(agg_ready_s, l + 1)
                    dve.wait_ge(agg_hi_ready_v, l + 1)
                    dve.wait_ge(agg_hi_ready_s, l + 1)
                    for k in range(2):
                        nc.vector.tensor_tensor(nodes(agg_lo, k), agg_t[:, k, :].rearrange("p (t n) -> p t n", n=P),
                                                nodes(agg_hi, k).bitcast(F32), ALU.subtract).then_inc(agg_lo_ready, 1)
                    dve.wait_ge(logits_done, l + 1)
                    chain.link(nc.vector.tensor_tensor(logits[:, :, :], g.bank(LOGIT_BANK)[0:P, 0:T * 16].rearrange("p (t e) -> p t e", e=16)[:, :, 0:NEXP + 1],
                                                       g.b_router[:, ds(l, 1), :].broadcast_to([P, T, NEXP + 1]), ALU.add))
                    lg = logits[:, :, 0:NEXP]
                    nc.vector.tensor_copy(conf[:, :], logits[:, :, NEXP])
                    chain.link(nc.vector.tensor_reduce(best[:, :], lg, AX.X, ALU.max))
                    nc.vector.tensor_tensor(shifted[:, :, :], lg, best[:, :].unsqueeze(2).broadcast_to([P, T, NEXP]), ALU.subtract).then_inc(shifted_ready, 1)
                    for t in range(T):
                        other = logits[:, t, 0:NEXP].unsqueeze(1).broadcast_to([P, NEXP, NEXP])
                        mine = logits[:, t, 0:NEXP].unsqueeze(2).broadcast_to([P, NEXP, NEXP])
                        nc.vector.tensor_tensor(beats[:, t, :, :], other, mine, ALU.is_gt)
                        last = nc.vector.tensor_tensor(ties[:, t, :, :], other, mine, ALU.is_equal)
                    chain.link(last)
                    for t in range(T):
                        last = nc.vector.tensor_tensor(ties[:, t, :, :], ties[:, t, :, :], tri[:, :, :], ALU.mult)
                    chain.link(last)
                    chain.link(nc.vector.tensor_tensor(beats[:, :, :, :], beats[:, :, :, :], ties[:, :, :, :], ALU.add))
                    chain.link(nc.vector.tensor_reduce(rank[:, :, :], beats[:, :, :, :], AX.X, ALU.add))
                    dve.wait_ge(exps_ready, l + 1)
                    chain.link(nc.vector.scalar_tensor_tensor(gate[:, :, :], rank[:, :, :], 2.0, shifted[:, :, :], ALU.is_lt, ALU.mult))
                    chain.link(nc.vector.tensor_reduce(total[:, :], gate[:, :, :], AX.X, ALU.add))
                    chain.link(nc.vector.reciprocal(total[:, :], total[:, :]))
                    nc.vector.tensor_tensor(gate[:, :, :], gate[:, :, :], total[:, :].unsqueeze(2).broadcast_to([P, T, NEXP]), ALU.mult).then_inc(gate_ready, 1)
                    chain.link(nc.vector.tensor_scalar(conf[:, :], conf[:, :], 1.0, None, ALU.add))
                    chain.link(nc.vector.reciprocal(conf[:, :], conf[:, :]))
                    for n in range(T * WPAIR + 1):
                        if n < T * WPAIR:
                            q = n % WPAIR
                            dve.wait_ge(weak_done, l * (T * WPAIR) + (n + 1))
                            nc.vector.tensor_tensor(weak_sum[:, q, :], g.bank(WEAK_BANK + n % 2)[0:P, :],
                                                    g.b_weak[:, ds(l, 1), 2 * q * HID:(2 * q + 2) * HID].rearrange("p l f -> p (l f)"),
                                                    ALU.add).then_inc(weak_read, 1)
                        if n > 0:
                            t, q = divmod(n - 1, WPAIR)
                            dve.wait_ge(weak_weighed, l * (T * WPAIR) + n)
                            first, second = weak_sum[:, q, 0:HID], weak_sum[:, q, HID:2 * HID]
                            if q == 0:
                                chain.link(nc.vector.tensor_tensor(moe_sum[:, t, :], first, second, ALU.add))
                            else:
                                chain.link(nc.vector.tensor_tensor(first, first, second, ALU.add))
                                chain.link(nc.vector.tensor_tensor(moe_sum[:, t, :], moe_sum[:, t, :], first, ALU.add))
                    dve.wait_ge(gate_turned, l + 1)
                    nc.vector.tensor_copy(gate_t[:, :], g.wide(STRONG_BANK)[0:NEXP, :]).then_inc(gate_t_ready, 1)
                    for e in range(NS):
                        for m in range(4):
                            n = e * 4 + m
                            dve.wait_ge(hidden_hi_ready, l * (NS * 4) + (n + 1))
                            nc.vector.tensor_tensor(hidden_lo[:, m, :], hidden_row[:, n % 2, :], hidden_hi[:, m, :].bitcast(F32),
                                                    ALU.subtract).then_inc(hidden_lo_ready, 1)
                            for t in BIAS_AFTER_ROW.get(n, ()):
                                dve.wait_ge(bias_done, l * T + (t + 1))
                                nc.vector.tensor_tensor(moe_sum[:, t, :], g.bank(WEAK_BANK + t % 2)[0:P, 0:HID], moe_sum[:, t, :],
                                                        ALU.add).then_inc(bias_read, 1)
                        for t in range(T):
                            if t == 3 and e < NS - 1:
                                split_low(dve, l, e + 2)
                            n = e * T + t
                            dve.wait_ge(strong_done, l * (NS * T) + (n + 1))
                            if e:
                                dve.wait_ge(strong_read, l * (NS * T) + (n - T + 1))
                            else:
                                dve.wait_ge(bias_read, l * T + (t + 1))
                            nc.vector.scalar_tensor_tensor(moe_sum[:, t, :], g.bank(STRONG_BANK + n % 2)[0:P, 0:HID], gate[:, t, NW + e:NW + e + 1],
                                                           moe_sum[:, t, :], ALU.mult, ALU.add).then_inc(strong_read, 1)
                            if e == NS - 1:
                                dve.wait_ge(strong_read, l * (NS * T) + (n + 1))
                                last = nc.vector.scalar_tensor_tensor(h[:, t, :], moe_sum[:, t, :], conf[:, t:t + 1], h[:, t, :], ALU.mult, ALU.add)
                    last.then_inc(h_ready, 1)
                chain.leave(LAYERS)
                dve.wait_ge(turned, LAYERS + 1)
                nc.vector.tensor_copy(g.x_t[:, 1, :], g.wide(2)).then_inc(h_t_ready_v, 1)
                dve.wait_ge(y_done, 1)
                sums = psum[0:P, 0:T * 512].rearrange("p (t f) -> p t f", f=512)[:, :, 0:D]
                chain.link(nc.vector.tensor_tensor(g.res[:, :, :], sums, g.xa[:, :, :], ALU.add))
                g.layernorm_vector(chain, g.res, y, 4).then_inc(y_ready, 1)


_WEIGHTS_TURNED = ("L0_gnn_Wp1", "L0_gnn_Ws1", "L0_gnn_Wn1", "L0_gnn_Wp2", "L0_gnn_Ws2", "L0_gnn_Wn2")


def kernel(**inputs):
    import numpy as _np
    import concourse.bacc as _bacc
    from concourse import mybir as _mybir
    from concourse.bass_utils import run_bass_kernel_spmd as _run

    nc = _bacc.Bacc("TRN2", target_bir_lowering=False, num_devices=1)
    arrays, aps = {}, {}
    for name, value in inputs.items():
        v = _np.asarray(value)
        v = _np.ascontiguousarray(v.T if name in _WEIGHTS_TURNED else v)
        arrays[f"in_{name}"] = v
        aps[name] = nc.dram_tensor(f"in_{name}", v.shape, _mybir.dt.from_np(v.dtype), kind="ExternalInput").ap()
    out = nc.dram_tensor("out_x", (N, D), F32, kind="ExternalOutput").ap()
    build(nc, aps, out)
    r = _run(nc, [arrays], core_ids=[0])
    return r.results[0]["out_x"]
```
